# Optimizing a Trainium2 kernel written in Bass

```python
import numpy as np
import jax
import jax.numpy as jnp

def _softmax(x, axis=-1):
    return jax.nn.softmax(x, axis=axis)

def _gelu(x):
    return jax.nn.gelu(x, approximate=True)

def _silu(x):
    return jax.nn.silu(x)

def _sigmoid(x):
    return jax.nn.sigmoid(x)

def _layernorm(x, axis=-1, eps=1e-05):
    m = jnp.mean(x, axis=axis, keepdims=True)
    v = jnp.var(x, axis=axis, keepdims=True)
    return (x - m) / jnp.sqrt(v + eps)

def _scatter_add(tgt, idx, src, axis=0):
    return tgt.at[idx].add(src)

def _segment_sum(src, seg, n):
    return jax.ops.segment_sum(src, seg, n)
kernel_name = 'mk_gnn_preln_d2_gnn_r32_56fd28'

def setup_inputs(seed: int=0):
    np.random.seed(seed)
    _w = jnp.asarray

    def _rec_inputs():
        import jax
        import jax.numpy as jnp
        _gk = jax.random.key(seed)
        x = -0.0003713 + 1 * jax.random.normal(jax.random.fold_in(_gk, 1), (50000, 256), jnp.float32)
        _s = jax.random.randint(jax.random.fold_in(_gk, 2), (12500,), 0, 50000, jnp.int32)
        _d = jax.random.randint(jax.random.fold_in(_gk, 3), (12500,), 0, 50000, jnp.int32)
        _loop = jnp.arange(50000, dtype=jnp.int32)
        src = jnp.concatenate([_s, _d, _loop])
        dst = jnp.concatenate([_d, _s, _loop])
        _o = jnp.argsort(dst, stable=True)
        src = src[_o]
        dst = dst[_o]
        return (x, src, dst)
    x, src, dst = _rec_inputs()

    def _L0_gnn_setup():
        import jax, jax.numpy as jnp
        import numpy as np
        N_NODES = 50000
        N_EDGES = 25000
        D_IN = 256
        D_OUT = 256
        BN_EPS = 1e-05

        def _forward(x, edge_index, w1, b1, gamma, beta, w2, b2, w_gcn, b_gcn):
            n = x.shape[0]
            h = x @ w1.T + b1
            mean = jnp.mean(h, axis=0)
            var = jnp.var(h, axis=0)
            h = (h - mean) * jax.lax.rsqrt(var + BN_EPS) * gamma + beta
            h = jax.nn.relu(h)
            h = h @ w2.T + b2
            xw = h @ w_gcn.T
            src = jnp.concatenate([edge_index[0], jnp.arange(n, dtype=edge_index.dtype)])
            dst = jnp.concatenate([edge_index[1], jnp.arange(n, dtype=edge_index.dtype)])
            deg = jax.ops.segment_sum(jnp.ones_like(dst, dtype=xw.dtype), dst, num_segments=n)
            dinv = jnp.where(deg > 0, jax.lax.rsqrt(jnp.maximum(deg, 1.0)), 0.0)
            norm = dinv[src] * dinv[dst]
            msgs = xw[src] * norm[:, None]
            out = jax.ops.segment_sum(msgs, dst, num_segments=n) + b_gcn
            return out
        key = jax.random.key(seed)
        ks = jax.random.split(key, 8)
        x = jax.random.normal(ks[0], (N_NODES, D_IN), dtype=jnp.float32)
        edge_index = jax.random.randint(ks[1], (2, N_EDGES), 0, N_NODES, dtype=jnp.int64)
        s1 = 1.0 / np.sqrt(D_IN)
        s2 = 1.0 / np.sqrt(D_OUT)
        w1 = jax.random.uniform(ks[2], (D_OUT, D_IN), jnp.float32, -s1, s1)
        b1 = jax.random.uniform(ks[3], (D_OUT,), jnp.float32, -s1, s1)
        gamma = jnp.ones((D_OUT,), jnp.float32)
        beta = jnp.zeros((D_OUT,), jnp.float32)
        w2 = jax.random.uniform(ks[4], (D_OUT, D_OUT), jnp.float32, -s2, s2)
        b2 = jax.random.uniform(ks[5], (D_OUT,), jnp.float32, -s2, s2)
        w_gcn = jax.random.uniform(ks[6], (D_OUT, D_OUT), jnp.float32, -s2, s2)
        b_gcn = jnp.zeros((D_OUT,), jnp.float32)
        return {'x': x, 'edge_index': edge_index, 'w1': w1, 'b1': b1, 'gamma': gamma, 'beta': beta, 'w2': w2, 'b2': b2, 'w_gcn': w_gcn, 'b_gcn': b_gcn}
    _L0_gnn_all = _L0_gnn_setup()
    _L0_gnn_in = {k: v for k, v in _L0_gnn_all.items() if k in ('w1', 'b1', 'gamma', 'beta', 'w2', 'b2', 'w_gcn', 'b_gcn')}
    del _L0_gnn_all

    def _L1_gnn_setup():
        import jax, jax.numpy as jnp
        import numpy as np
        N = 50000
        E = 50000
        D = 256
        H = 8
        DH = D // H
        key = jax.random.key(seed)
        ks = jax.random.split(key, 12)
        s = 1.0 / np.sqrt(D)
        inp = {'x': jax.random.normal(ks[0], (N, D), dtype=jnp.float32), 'row': jax.random.randint(ks[1], (E,), 0, N), 'col': jax.random.randint(ks[2], (E,), 0, N), 'Wq': jax.random.normal(ks[3], (D, D), dtype=jnp.float32) * s, 'bq': jax.random.normal(ks[4], (D,), dtype=jnp.float32) * s, 'Wk': jax.random.normal(ks[5], (D, D), dtype=jnp.float32) * s, 'bk': jax.random.normal(ks[6], (D,), dtype=jnp.float32) * s, 'Wv': jax.random.normal(ks[7], (D, D), dtype=jnp.float32) * s, 'bv': jax.random.normal(ks[8], (D,), dtype=jnp.float32) * s, 'Wo': jax.random.normal(ks[9], (D, D), dtype=jnp.float32) * s, 'bo': jax.random.normal(ks[10], (D,), dtype=jnp.float32) * s}
        return inp
    _L1_gnn_all = _L1_gnn_setup()
    _L1_gnn_in = {k: v for k, v in _L1_gnn_all.items() if k in ('Wq', 'bq', 'Wk', 'bk', 'Wv', 'bv', 'Wo', 'bo')}
    del _L1_gnn_all
    return {'x': x, 'src': src, 'dst': dst, 'L0_gnn_w1': _L0_gnn_in['w1'], 'L0_gnn_b1': _L0_gnn_in['b1'], 'L0_gnn_gamma': _L0_gnn_in['gamma'], 'L0_gnn_beta': _L0_gnn_in['beta'], 'L0_gnn_w2': _L0_gnn_in['w2'], 'L0_gnn_b2': _L0_gnn_in['b2'], 'L0_gnn_w_gcn': _L0_gnn_in['w_gcn'], 'L0_gnn_b_gcn': _L0_gnn_in['b_gcn'], 'L1_gnn_Wq': _L1_gnn_in['Wq'], 'L1_gnn_bq': _L1_gnn_in['bq'], 'L1_gnn_Wk': _L1_gnn_in['Wk'], 'L1_gnn_bk': _L1_gnn_in['bk'], 'L1_gnn_Wv': _L1_gnn_in['Wv'], 'L1_gnn_bv': _L1_gnn_in['bv'], 'L1_gnn_Wo': _L1_gnn_in['Wo'], 'L1_gnn_bo': _L1_gnn_in['bo']}

def reference(x, src, dst, L0_gnn_w1, L0_gnn_b1, L0_gnn_gamma, L0_gnn_beta, L0_gnn_w2, L0_gnn_b2, L0_gnn_w_gcn, L0_gnn_b_gcn, L1_gnn_Wq, L1_gnn_bq, L1_gnn_Wk, L1_gnn_bk, L1_gnn_Wv, L1_gnn_bv, L1_gnn_Wo, L1_gnn_bo):
    import jax
    import jax.numpy as jnp

    def _L0_gnn_ref(x, edge_index, w1, b1, gamma, beta, w2, b2, w_gcn, b_gcn):
        import jax, jax.numpy as jnp
        import numpy as np
        N_NODES = 50000
        N_EDGES = 25000
        D_IN = 256
        D_OUT = 256
        BN_EPS = 1e-05

        def _forward(x, edge_index, w1, b1, gamma, beta, w2, b2, w_gcn, b_gcn):
            n = x.shape[0]
            h = x @ w1.T + b1
            mean = jnp.mean(h, axis=0)
            var = jnp.var(h, axis=0)
            h = (h - mean) * jax.lax.rsqrt(var + BN_EPS) * gamma + beta
            h = jax.nn.relu(h)
            h = h @ w2.T + b2
            xw = h @ w_gcn.T
            src = jnp.concatenate([edge_index[0], jnp.arange(n, dtype=edge_index.dtype)])
            dst = jnp.concatenate([edge_index[1], jnp.arange(n, dtype=edge_index.dtype)])
            deg = jax.ops.segment_sum(jnp.ones_like(dst, dtype=xw.dtype), dst, num_segments=n)
            dinv = jnp.where(deg > 0, jax.lax.rsqrt(jnp.maximum(deg, 1.0)), 0.0)
            norm = dinv[src] * dinv[dst]
            msgs = xw[src] * norm[:, None]
            out = jax.ops.segment_sum(msgs, dst, num_segments=n) + b_gcn
            return out
        return _forward(x, edge_index, w1, b1, gamma, beta, w2, b2, w_gcn, b_gcn)

    def _L1_gnn_ref(x, row, col, Wq, bq, Wk, bk, Wv, bv, Wo, bo):
        import jax, jax.numpy as jnp
        import numpy as np
        N = 50000
        E = 50000
        D = 256
        H = 8
        DH = D // H
        n = x.shape[0]
        scaling = DH ** (-0.5)
        q = (x @ Wq + bq).reshape(n, DH, H) * scaling
        k = (x @ Wk + bk).reshape(n, DH, H)
        v = (x @ Wv + bv).reshape(n, DH, H)
        s = jnp.einsum('edh,edh->eh', q[row], k[col])
        m = jax.ops.segment_max(s, row, num_segments=n)
        e = jnp.exp(s - m[row])
        z = jax.ops.segment_sum(e, row, num_segments=n)
        a = e / z[row]
        out = jax.ops.segment_sum(a[:, None, :] * v[col], row, num_segments=n)
        return out.reshape(n, -1) @ Wo + bo
    edge_index = jnp.stack([src, dst])
    h = jnp.maximum(_layernorm(x, axis=-1), 0.0)
    x = x + _L0_gnn_ref(h, edge_index, L0_gnn_w1, L0_gnn_b1, L0_gnn_gamma, L0_gnn_beta, L0_gnn_w2, L0_gnn_b2, L0_gnn_w_gcn, L0_gnn_b_gcn)
    h = jnp.maximum(_layernorm(x, axis=-1), 0.0)
    x = x + _L1_gnn_ref(h, src, dst, L1_gnn_Wq, L1_gnn_bq, L1_gnn_Wk, L1_gnn_bk, L1_gnn_Wv, L1_gnn_bv, L1_gnn_Wo, L1_gnn_bo)
    return x

_drawn_inputs = setup_inputs


def setup_inputs(seed=0):
    import zlib

    import numpy as np

    out = dict(_drawn_inputs(seed))
    spreads = {'L0_gnn_gamma': (1.0, 0.2), 'L0_gnn_beta': (0.0, 0.366), 'L0_gnn_b_gcn': (0.0, 0.1)}
    factors = {'L0_gnn_b1': 8.0, 'L0_gnn_b2': 2.724, 'L1_gnn_bq': 8.0, 'L1_gnn_bk': 8.0}
    for name, (base, spread) in spreads.items():
        noise = np.random.default_rng([zlib.crc32(name.encode()), seed]).standard_normal(out[name].shape)
        drawn = base * np.exp(spread * noise) if base else spread * noise
        out[name] = jnp.asarray(drawn.astype(out[name].dtype))
    for name, factor in factors.items():
        out[name] = (out[name] * factor).astype(out[name].dtype)
    return out
```

```python
from contextlib import ExitStack

import concourse.bass as bass
from concourse import mybir

F32 = mybir.dt.float32
BF16 = mybir.dt.bfloat16
F16 = mybir.dt.float16
I32 = mybir.dt.int32
ALU = mybir.AluOpType
ACT = mybir.ActivationFunctionType
AX = mybir.AxisListType

P = 128
D = 256
KC = D // P
H = 8
DH = D // H
ROWS = 4
TILE = P * ROWS
SLOTS = 8
GROUPS = 4
SCALE = float(DH) ** -0.5
LOW = -1.0e30
EPS = 1e-5
HIST = 6
W = ROWS * D


class Plan:

    def __init__(self, n, e):
        self.n, self.e = n, e
        self.tiles = -(-n // TILE)
        self.tiles += self.tiles % 2
        self.last = n - (self.tiles - 1) * TILE
        assert 0 < self.last < TILE and self.last % ROWS == 0 and self.last + P <= TILE
        self.last_p = self.last // ROWS
        self.table = self.tiles * TILE
        self.per_part = -(-e // P)
        self.cols = self.tiles * HIST
        assert self.per_part <= self.cols
        self.full_parts = e // self.per_part
        self.rest = e - self.full_parts * self.per_part
        self.packed = self.cols + 8


def row_block(table, tile):
    return table[bass.ds(tile * TILE, TILE), :].rearrange("(p r) d -> p (r d)", p=P)


def over_tiles(eng, plan, lag, step):
    pairs = plan.tiles // 2

    def pair(i, fixed):
        for u in range(2):
            def at(l):
                back, slot = divmod(u - l, 2)
                if fixed and not 0 <= 2 * (i + back) + slot < plan.tiles:
                    return None
                return i + back, slot

            step(at)

    head = (lag + 2) // 2
    for i in range(head):
        pair(i, True)
    with eng.Fori(head, pairs - 1) as i:
        pair(i, False)
    for i in range(pairs - 1, (plan.tiles - 1 + lag) // 2 + 1):
        pair(i, True)


def over_columns(eng, turns, lag, step):
    assert lag < SLOTS

    def turn(i, first, after):
        for k in range(SLOTS if not after else lag):
            def at(l):
                back, slot = divmod(k - l, SLOTS)
                if (first and back < 0) or (after and back == 0):
                    return None
                return i + back, slot

            step(at)

    turn(0, True, False)
    with eng.Fori(1, turns) as i:
        turn(i, False, False)
    turn(turns, False, True)


def row_moments(v, dve, hold, x, stats, moments, stats_ready, moments_ready, i):
    for j in range(ROWS):
        last = v.bn_stats(stats[:, j, :], x[:, j, :])
    last.then_inc(stats_ready, 1)
    hold(dve, stats_ready, i + 1)
    for j in range(ROWS):
        last = v.bn_aggr(moments[:, j, :], stats[:, j, :])
    last.then_inc(moments_ready, 1)


def row_scales(v, dve, moments, std, rstd, shift, std_ready, rstd_ready, shift_ready, i):
    dve.wait_ge(std_ready, i + 1)
    v.reciprocal(rstd[:, :], std[:, :]).then_inc(rstd_ready, 1)
    dve.wait_ge(rstd_ready, i + 1)
    v.scalar_tensor_tensor(shift[:, :], moments[:, :, 0], -1.0, rstd[:, :], ALU.mult, ALU.mult).then_inc(shift_ready, 1)


def build(nc, x, src, dst, w1, b1, gamma, beta, w2, b2, w_gcn, b_gcn,
          wq, bq, wk, bk, wv, bv, wo, bo, out):
    plan = Plan(x.shape[0], src.shape[0])
    NT, TAB, COLS, PACKED = plan.tiles, plan.table, plan.cols, plan.packed

    def dram(name, shape, dt=F32):
        return nc.dram_tensor(name, shape, dt, kind="Internal").ap()

    h1_table = dram("h1_table", [NT * P, KC * TILE])
    y_table = dram("y_table", [TAB, D])
    agg_table = dram("agg_table", [TAB + 2 * P, D])
    x1_table = dram("x1_table", [TAB, D])
    q_table = dram("q_table", [TAB, D])
    k_table = dram("k_table", [TAB, D])
    v_table = dram("v_table", [TAB, D])
    m_table = dram("m_table", [TAB + 2 * P, H])
    acc_table = dram("acc_table", [TAB + 2 * P, D + H])

    with ExitStack() as ctx:
        def sb(name, shape, dt=F32, where=ctx):
            return where.enter_context(nc.sbuf_tensor(name, shape, dt))

        in_use = []

        def sem(name):
            in_use.append(nc.alloc_semaphore(name))
            return in_use[-1]

        def pool_dma_sem(name):
            return nc.alloc_semaphore(name)

        def end_part():
            with nc.Block() as block:
                @block.sync
                def _(sp):
                    for s in in_use:
                        sp.sem_clear(s)
            for s in in_use:
                nc.release_semaphore(s)
            in_use.clear()

        ident = sb("ident", [P, P])
        ident_b = sb("ident_b", [P, P], BF16)
        earlier = sb("earlier", [P, P])
        spare = sb("spare", [P, 3])
        lane = sb("lane", [P, max(P, NT * ROWS)], F16)
        w1_t = sb("w1_t", [P, KC, D])
        w_mix = sb("w_mix", [P, KC, D])
        b_mix = sb("b_mix", [P, D])
        w_qkv = sb("w_qkv", [P, KC, 3 * D])
        b_qkv = sb("b_qkv", [P, 3 * D])
        w_out = sb("w_out", [P, KC, D])
        b_out = sb("b_out", [P, D])
        b_agg = sb("b_agg", [P, D])
        eps_col = sb("eps_col", [P, 1])
        bn_in = sb("bn_in", [P, 3, KC])
        dst_lo = sb("dst_lo", [P, COLS])
        dst_hi = sb("dst_hi", [P, COLS])
        is_self = sb("is_self", [P, COLS])
        packed_i = sb("packed_i", [P, 2, GROUPS, PACKED], I32)
        packed_f = sb("packed_f", [P, 2, GROUPS, PACKED])
        more_turns = sb("more_turns", [P, 1], I32)
        dinv = sb("dinv", [P, NT * ROWS])
        n_self = sb("n_self", [P, NT * ROWS])
        self_score = sb("self_score", [P, NT * ROWS * H])
        held = nc.alloc_semaphore("held")

        def hold(eng, s, value):
            eng.wait_ge(s, value)
            if not isinstance(value, int):
                eng.sem_inc(held, 1)

        with ExitStack() as part:
            w1_n = sb("w1_n", [P, KC, D], where=part)
            w2_n = sb("w2_n", [P, KC, D], where=part)
            wg_n = sb("wg_n", [P, KC, D], where=part)
            wg_t = sb("wg_t", [P, KC, D], where=part)
            b2_c = sb("b2_c", [P, KC], where=part)
            edges = sb("edges", [P, 2, COLS], I32, where=part)
            work_i = sb("work_i", [P, 2, COLS], I32, where=part)
            place = sb("place", [P, COLS], I32, where=part)
            edges_f = sb("edges_f", [P, 2, COLS], where=part)
            odd = sb("odd", [P, 2, 2, COLS], where=part)
            apart = sb("apart", [P, COLS], where=part)
            member = sb("member", [P, COLS], where=part)
            stock = sb("stock", [P, 2, COLS], where=part)
            best = sb("best", [P, 2, 8], where=part)
            counts = sb("counts", [P, GROUPS], where=part)
            most = sb("most", [P, GROUPS], where=part)
            most_i = sb("most_i", [P, GROUPS], I32, where=part)
            longest = sb("longest", [P, 1], where=part)
            empty = sb("empty", [P, 2 * GROUPS * PACKED], where=part)
            ps = [part.enter_context(nc.psum_tensor(f"prep_ps{i}", [P, 512], F32)) for i in range(4)]
            loaded = sem("prep_loaded")
            pads_ready = sem("pads_ready")
            edges_loaded = sem("edges_loaded")
            const_ready = sem("const_ready")
            turned = sem("weights_turned")
            copied = sem("weights_copied")
            mixed = sem("weights_mixed")
            chain = sem("prep_chain")
            counted = sem("edges_counted")
            most_ready = sem("most_ready")
            best_ready = [sem(f"best_ready{g}") for g in range(GROUPS)]
            replaced = [sem(f"best_replaced{g}") for g in range(GROUPS)]
            vchain = sem("prep_vector_chain")
            n_loads = 16

            with nc.Block() as block:
                @block.sync
                def _(sp):
                    def halves(w):
                        return w.rearrange("(c p) n -> p c n", p=P)

                    def column(v):
                        return v.rearrange("(c p) -> p c", p=P)

                    n = 0
                    pairs = [(w1_n[:, :, :], halves(w1)), (w2_n[:, :, :], halves(w2)), (wg_n[:, :, :], halves(w_gcn)),
                             (w_out[:, :, :], halves(wo)), (b_out[:, :], bo.partition_broadcast(P)),
                             (b_agg[:, :], b_gcn.partition_broadcast(P))]
                    for i, (w, b) in enumerate(((wq, bq), (wk, bk), (wv, bv))):
                        pairs.append((w_qkv[:, :, i * D:(i + 1) * D], halves(w)))
                        pairs.append((b_qkv[:, i * D:(i + 1) * D], b.partition_broadcast(P)))
                    with nc.allow_non_contiguous_dma(reason="a few hundred words, once"):
                        for i, v in enumerate((b1, gamma, beta)):
                            pairs.append((bn_in[:, i, :], column(v)))
                        pairs.append((b2_c[:, :], column(b2)))
                        assert len(pairs) == n_loads
                        sp.wait_ge(pads_ready, 1)
                        full, per, rest = plan.full_parts, plan.per_part, plan.rest
                        for i, e in enumerate((src, dst)):
                            lo = full // 16 * 16
                            for a, b in ((0, lo), (lo, full)):
                                if a < b:
                                    sp.dma_start(edges[a:b, i, 0:per], e[a * per:b * per].rearrange("(p c) -> p c", c=per)).then_inc(edges_loaded, 16)
                                    n += 1
                            if rest:
                                sp.dma_start(edges[full:full + 1, i, 0:rest], e[full * per:plan.e].rearrange("(p c) -> p c", p=1)).then_inc(edges_loaded, 16)
                                n += 1
                        plan.edge_loads = n
                        for o, i in pairs:
                            sp.dma_start(o, i).then_inc(loaded, 16)
                        sp.wait_ge(loaded, 16 * n_loads)
                        sp.wait_ge(edges_loaded, 16 * n)

                @block.gpsimd
                def _(pool):
                    pool.iota(edges[:, :, :], [[0, 2 * COLS]], base=plan.n, channel_multiplier=1).then_inc(pads_ready, 1)
                    pool.iota(place[:, :], [[1, COLS]], base=0, channel_multiplier=0).then_inc(const_ready, 1)
                    for i, base in enumerate((plan.n, TAB, TAB + P)):
                        pool.iota(spare[:, i:i + 1], [[0, 1]], base=base, channel_multiplier=1,
                                  allow_small_or_imprecise_dtypes=True).then_inc(const_ready, 1)
                    pool.iota(lane[:, :], [[1, max(P, NT * ROWS)]], base=0, channel_multiplier=0,
                              allow_small_or_imprecise_dtypes=True).then_inc(const_ready, 1)
                    pool.memset(eps_col[:, :], EPS).then_inc(const_ready, 1)
                    pool.memset(ident[:, :], 0.0).then_inc(chain, 1)
                    pool.memset(ident_b[:, :], 0.0).then_inc(chain, 1)
                    pool.memset(earlier[:, :], 0.0).then_inc(chain, 1)
                    pool.memset(packed_i[:, :, :, :], 0).then_inc(const_ready, 1)
                    pool.wait_ge(chain, 3)
                    for m in (ident, ident_b):
                        pool.affine_select(out=m[:, :], in_=m[:, :], compare_op=ALU.not_equal, fill=1.0, base=0,
                                           pattern=[[-1, P]], channel_multiplier=1).then_inc(const_ready, 1)
                    pool.affine_select(out=earlier[:, :], in_=earlier[:, :], compare_op=ALU.is_ge, fill=1.0, base=0,
                                       pattern=[[1, P]], channel_multiplier=-1).then_inc(const_ready, 1)
                    pool.wait_ge(counted, GROUPS)
                    pool.partition_all_reduce(most[:, :], counts[:, :], P, bass.bass_isa.ReduceOp.max).then_inc(most_ready, 1)

                @block.tensor
                def _(pe):
                    pe.wait_ge(loaded, 16 * n_loads)
                    pe.wait_ge(const_ready, 10)
                    for b, w in enumerate((w1_n, wg_n)):
                        for kc in range(KC):
                            for oc in range(KC):
                                last = nc.tensor.transpose(ps[b][:, kc * D + oc * P:kc * D + oc * P + P],
                                                           w[:, oc, kc * P:(kc + 1) * P], ident[:, :])
                        last.then_inc(turned, 1)
                    pe.wait_ge(copied, 2)
                    for kc in range(KC):
                        for jc in range(KC):
                            nc.tensor.matmul(ps[2][:, kc * D:(kc + 1) * D], w2_n[:, jc, kc * P:(kc + 1) * P],
                                             wg_t[:, jc, :], start=jc == 0, stop=jc == KC - 1)
                    for jc in range(KC):
                        last = nc.tensor.matmul(ps[3][:, 0:D], b2_c[:, jc:jc + 1].to_broadcast([P, P]), wg_t[:, jc, :],
                                                start=jc == 0, stop=jc == KC - 1)
                    last.then_inc(mixed, 1)

                @block.scalar
                def _(act):
                    for b, w in enumerate((w1_t, wg_t)):
                        act.wait_ge(turned, b + 1)
                        nc.scalar.activation(w[:, :, :].rearrange("p a b -> p (a b)"), ps[b][:, :], ACT.Copy).then_inc(copied, 1)
                    act.wait_ge(mixed, 1)
                    nc.scalar.activation(w_mix[:, :, :].rearrange("p a b -> p (a b)"), ps[2][:, :], ACT.Copy)
                    nc.scalar.activation(b_mix[:, :], ps[3][:, 0:D], ACT.Copy)

                @block.vector
                def _(dve):
                    done = [0]

                    def link(ins):
                        done[0] += 1
                        ins.then_inc(vchain, 1)
                        dve.wait_ge(vchain, done[0])

                    v = nc.vector
                    dve.wait_ge(edges_loaded, 16 * plan.edge_loads)
                    dve.wait_ge(const_ready, 10)
                    v.tensor_scalar(work_i[:, 0, :], edges[:, 1, :], 2, P - 1, ALU.logical_shift_right, ALU.bitwise_and)
                    link(v.tensor_scalar(work_i[:, 1, :], edges[:, 1, :], 9, 2, ALU.logical_shift_right, ALU.logical_shift_left))
                    link(v.tensor_copy(dst_lo[:, :], work_i[:, 0, :]))
                    v.tensor_copy(dst_hi[:, :], work_i[:, 1, :])
                    link(v.tensor_copy(edges_f[:, :, :], edges[:, :, :]))
                    link(v.tensor_scalar(work_i[:, 0, :], edges[:, 1, :], ROWS - 1, None, ALU.bitwise_and))
                    link(v.tensor_copy(member[:, :], work_i[:, 0, :]))
                    v.tensor_tensor(dst_hi[:, :], dst_hi[:, :], member[:, :], ALU.add)
                    v.tensor_tensor(is_self[:, :], edges_f[:, 0, :], edges_f[:, 1, :], ALU.is_equal)
                    link(v.tensor_tensor(apart[:, :], edges_f[:, 0, :], edges_f[:, 1, :], ALU.not_equal))
                    link(v.tensor_scalar(work_i[:, :, :], edges[:, :, :], 1, None, ALU.bitwise_and))
                    link(v.tensor_copy(odd[:, :, 1, :], work_i[:, :, :]))
                    link(v.tensor_scalar(odd[:, :, 0, :], odd[:, :, 1, :], -1.0, 1.0, ALU.mult, ALU.add))
                    link(v.tensor_scalar(place[:, :], place[:, :], 16, 0x40000000, ALU.logical_shift_left, ALU.bitwise_or))
                    for i in range(2):
                        link(v.tensor_tensor(edges[:, i, :], edges[:, i, :], place[:, :], ALU.bitwise_or))
                    for g in range(GROUPS):
                        link(v.tensor_tensor(member[:, :], apart[:, :], odd[:, 0, g & 1, :], ALU.mult))
                        link(v.tensor_tensor(member[:, :], member[:, :], odd[:, 1, g >> 1, :], ALU.mult))
                        v.reduce_sum(counts[:, g:g + 1], member[:, :], axis=AX.X).then_inc(counted, 1)
                        dve.wait_ge(counted, g + 1)
                    dve.wait_ge(most_ready, 1)
                    link(v.tensor_scalar(most[:, :], most[:, :], 1.0, None, ALU.max))
                    link(v.tensor_copy(most_i[:, :], most[:, :]))
                    link(v.reduce_max(longest[:, :], most[:, :], axis=AX.X))
                    link(v.tensor_scalar(longest[:, :], longest[:, :], 4.0, -3.0, ALU.max, ALU.add))
                    link(v.tensor_copy(more_turns[:, :], longest[:, :]))
                    link(v.tensor_scalar(more_turns[:, :], more_turns[:, :], 1, None, ALU.logical_shift_right))
                    for g in range(GROUPS):
                        link(v.tensor_tensor(member[:, :], apart[:, :], odd[:, 0, g & 1, :], ALU.mult))
                        link(v.tensor_tensor(member[:, :], member[:, :], odd[:, 1, g >> 1, :], ALU.mult))
                        for i in range(2):
                            link(v.tensor_tensor(stock[:, i, :], edges[:, i, :].bitcast(F32), member[:, :], ALU.mult))
                        length = dve.value_load(most_i[0:1, g:g + 1], min_val=1, max_val=COLS)
                        with dve.Fori(0, length, 8) as c:
                            for i in range(2):
                                v.max(out=best[:, i, :], in_=stock[:, i, :]).then_inc(best_ready[g], 1)
                            hold(dve, best_ready[g], c // 8 * 2 + 2)
                            for i in range(2):
                                v.tensor_copy(packed_i[:, i, g, bass.ds(c, 8)], best[:, i, :].bitcast(I32))
                                v.match_replace(out=stock[:, i, :], in_to_replace=best[:, i, :], in_values=stock[:, i, :],
                                                imm_value=0.0).then_inc(replaced[g], 1)
                            hold(dve, replaced[g], c // 8 * 2 + 2)
                    pi = packed_i[:, :, :, :].rearrange("p a g c -> p (a g c)")
                    pf = packed_f[:, :, :, :].rearrange("p a g c -> p (a g c)")
                    link(v.tensor_copy(pf, pi))
                    link(v.tensor_scalar(empty[:, :], pf, 0.0, None, ALU.is_equal))
                    link(v.tensor_scalar(pi, pi, 0xFFFF, None, ALU.bitwise_and))
                    link(v.tensor_copy(pf, pi))
                    link(v.scalar_tensor_tensor(pi, empty[:, :], spare[:, 0:1], pf, ALU.mult, ALU.add))
                    for i in range(2):
                        for g in range(GROUPS):
                            at = (i * GROUPS + g) * PACKED
                            parity = g >> i & 1
                            v.scalar_tensor_tensor(packed_f[:, i, g, :], empty[:, at:at + PACKED], spare[:, 1 + parity:2 + parity],
                                                   packed_f[:, i, g, :], ALU.mult, ALU.add)

        end_part()

        with ExitStack() as part:
            two = range(2)
            xb = [sb(f"a_x{u}", [P, ROWS, D], where=part) for u in two]
            stats = [sb(f"a_stats{u}", [P, ROWS, 6], where=part) for u in two]
            moments = [sb(f"a_moments{u}", [P, ROWS, 2], where=part) for u in two]
            std = [sb(f"a_std{u}", [P, ROWS], where=part) for u in two]
            rstd = [sb(f"a_rstd{u}", [P, ROWS], where=part) for u in two]
            shift = [sb(f"a_shift{u}", [P, ROWS], where=part) for u in two]
            hn = [sb(f"a_hn{u}", [P, ROWS, D], where=part) for u in two]
            ht = [sb(f"a_ht{u}", [P, KC, TILE], where=part) for u in two]
            h1 = [sb(f"h1_{u}", [P, KC, TILE], where=part) for u in two]
            zero = sb("zero", [P, ROWS * (D + H)], where=part)
            third = HIST // 2
            hot_hi = [sb(f"hot_hi{w}", [P, third, NT * ROWS], F16, where=part) for w in two]
            hot_lo = [sb(f"hot_lo{w}", [P, third, 2, P], F16, where=part) for w in two]
            bn_stats = sb("bn_stats", [P, KC, NT * 6], where=part)
            bn_moments = sb("bn_moments", [P, KC, 2], where=part)
            bn_scale = sb("bn_scale", [P, KC], where=part)
            bn_shift = sb("bn_shift", [P, KC], where=part)
            x_loaded = [sem(f"a_x_loaded{u}") for u in two]
            stats_ready = [sem(f"a_stats_ready{u}") for u in two]
            moments_ready = [sem(f"a_moments_ready{u}") for u in two]
            std_ready = [sem(f"a_std_ready{u}") for u in two]
            rstd_ready = [sem(f"a_rstd_ready{u}") for u in two]
            shift_ready = [sem(f"a_shift_ready{u}") for u in two]
            hn_ready = [sem(f"a_hn_ready{u}") for u in two]
            turned = [sem(f"a_turned{u}") for u in two]
            ht_by_dve = [sem(f"a_ht_by_dve{u}") for u in two]
            ht_by_act = [sem(f"a_ht_by_act{u}") for u in two]
            product_ready = [sem(f"a_product_ready{u}") for u in two]
            h1_ready = [sem(f"a_h1_ready{u}") for u in two]
            h1_counted = [sem(f"a_h1_counted{u}") for u in two]
            h1_stored = [pool_dma_sem(f"a_h1_stored{u}") for u in two]
            hot_ready = [sem(f"hot_ready{w}") for w in two]
            hot_used = [sem(f"hot_used{w}") for w in two]
            zeroed = pool_dma_sem("acc_zeroed")
            zero_ready = sem("zero_ready")
            hist_ps = [part.enter_context(nc.psum_tensor(f"hist_ps{i}", [P, NT * ROWS], F32)) for i in two]

            with ExitStack() as inner, nc.Block() as block:
                turn_ps = [inner.enter_context(nc.psum_tensor(f"a_turn_ps{u}", [P, KC * TILE], F32)) for u in two]
                h1_ps = inner.enter_context(nc.psum_tensor("a_h1_ps", [P, KC * TILE], F32))

                @block.sync
                def _(sp):
                    def step(at):
                        if (here := at(0)) is None:
                            return
                        i, u = here
                        tile = i * 2 + u
                        sp.wait_ge(hn_ready[u], i)
                        if isinstance(tile, int) and tile == NT - 1:
                            rows = x[tile * TILE:plan.n, :].rearrange("(p r) d -> p (r d)", r=ROWS)
                            sp.dma_start(xb[u][0:plan.last_p, :, :].rearrange("p r d -> p (r d)"), rows).then_inc(x_loaded[u], 16)
                        else:
                            sp.dma_start(xb[u][:, :, :].rearrange("p r d -> p (r d)"), row_block(x, tile)).then_inc(x_loaded[u], 16)

                    over_tiles(sp, plan, 0, step)

                @block.gpsimd
                def _(pool):
                    pool.memset(zero[:, :], 0.0).then_inc(zero_ready, 1)
                    pool.wait_ge(zero_ready, 1)

                    def step(at):
                        if at(1) is None:
                            return
                        i, u = at(1)
                        tile = i * 2 + u
                        hold(pool, h1_ready[u], i + 1)
                        pool.dma_start(h1_table[bass.ds(tile * P, P), :], h1[u][:, :, :].rearrange("p k c -> p (k c)")).then_inc(h1_stored[u], 16)
                        pool.dma_start(row_block(acc_table, tile), zero[:, :]).then_inc(zeroed, 16)

                    over_tiles(pool, plan, 1, step)
                    for u in two:
                        pool.wait_ge(h1_stored[u], 16 * (NT // 2))
                    for table, width in ((acc_table, D + H), (agg_table, D), (m_table, H)):
                        pool.dma_start(table[TAB:TAB + 2 * P, :].rearrange("(p r) d -> p (r d)", p=P), zero[:, 0:2 * width]).then_inc(zeroed, 16)
                    pool.wait_ge(zeroed, 16 * (NT + 3))

                @block.scalar
                def _(act):
                    def step(at):
                        if at(0) is not None:
                            i, u = at(0)
                            act.wait_ge(moments_ready[u], i + 1)
                            act.wait_ge(shift_ready[u], i)
                            nc.scalar.activation(std[u][:, :], moments[u][:, :, 1], ACT.Sqrt, bias=eps_col[:, 0:1]).then_inc(std_ready[u], 1)
                            act.wait_ge(shift_ready[u], i + 1)
                            act.wait_ge(turned[u], i)
                            for j in range(ROWS):
                                last = nc.scalar.activation(hn[u][:, j, :], xb[u][:, j, :], ACT.Relu,
                                                            bias=shift[u][:, j:j + 1], scale=rstd[u][:, j:j + 1])
                            last.then_inc(hn_ready[u], 1)
                        if at(2) is not None:
                            i, u = at(2)
                            act.wait_ge(product_ready[u], i + 1)
                            act.wait_ge(h1_stored[u], 16 * i)
                            act.wait_ge(h1_counted[u], i)
                            for oc in range(KC):
                                last = nc.scalar.activation(h1[u][:, oc, :], h1_ps[:, oc * TILE:(oc + 1) * TILE],
                                                            ACT.Identity, bias=bn_in[:, 0, oc:oc + 1])
                            last.then_inc(h1_ready[u], 1)
                        if at(1) is not None:
                            i, u = at(1)
                            act.wait_ge(turned[u], i + 1)
                            act.wait_ge(product_ready[u], i)
                            nc.scalar.activation(ht[u][:, 1, :], turn_ps[u][:, TILE:2 * TILE], ACT.Copy).then_inc(ht_by_act[u], 1)

                    over_tiles(act, plan, 2, step)

                @block.tensor
                def _(pe):
                    def step(at):
                        if at(0) is not None:
                            i, u = at(0)
                            tile = i * 2 + u
                            fixed = isinstance(tile, int)
                            pe.wait_ge(hn_ready[u], i + 1)
                            pe.wait_ge(ht_by_dve[u], i)
                            pe.wait_ge(ht_by_act[u], i)
                            for kc in range(KC):
                                for j in range(ROWS):
                                    last = nc.tensor.transpose(turn_ps[u][:, kc * TILE + j * P:kc * TILE + (j + 1) * P],
                                                               hn[u][:, j, kc * P:(kc + 1) * P], ident[:, :])
                            last.then_inc(turned[u], 1)
                            for w in two:
                                pe.wait_ge(hot_ready[w], tile + 1)
                                for c in range(third):
                                    first = fixed and tile == 0 and w == 0 and c == 0
                                    end = fixed and tile == NT - 1 and w == 1 and c == third - 1
                                    for b in two:
                                        last = nc.tensor.matmul(hist_ps[b][:, :], hot_lo[w][:, c, b, :], hot_hi[w][:, c, :],
                                                                start=first, stop=end)
                                last.then_inc(hot_used[w], 1)
                        if at(1) is not None:
                            i, u = at(1)
                            pe.wait_ge(ht_by_dve[u], i + 1)
                            pe.wait_ge(ht_by_act[u], i + 1)
                            pe.wait_ge(h1_ready[1 - u], i + u)
                            for oc in range(KC):
                                for kc in range(KC):
                                    last = nc.tensor.matmul(h1_ps[:, oc * TILE:(oc + 1) * TILE], w1_t[:, kc, oc * P:(oc + 1) * P],
                                                            ht[u][:, kc, :], start=kc == 0, stop=kc == KC - 1)
                            last.then_inc(product_ready[u], 1)

                    over_tiles(pe, plan, 1, step)

                @block.vector
                def _(dve):
                    v = nc.vector

                    def one_hots(tile, w):
                        hold(dve, hot_used[w], tile)
                        for c in range(third):
                            col = bass.ds(tile * HIST + (w * third + c), 1)
                            v.tensor_scalar(hot_hi[w][:, c, :], lane[:, 0:NT * ROWS], dst_hi[:, col], None, ALU.is_equal)
                            v.tensor_scalar(hot_lo[w][:, c, 0, :], lane[:, 0:P], dst_lo[:, col], None, ALU.is_equal)
                            last = v.tensor_scalar(hot_lo[w][:, c, 1, :], lane[:, 0:P], dst_lo[:, col], is_self[:, col],
                                                   ALU.is_equal, ALU.mult)
                        last.then_inc(hot_ready[w], 1)

                    def step(at):
                        if at(0) is not None:
                            i, u = at(0)
                            tile = i * 2 + u
                            dve.wait_ge(x_loaded[u], 16 * i + 16)
                            dve.wait_ge(hn_ready[u], i)
                            row_moments(v, dve, hold, xb[u], stats[u], moments[u], stats_ready[u], moments_ready[u], i)
                            one_hots(tile, 0)
                            row_scales(v, dve, moments[u], std[u], rstd[u], shift[u],
                                       std_ready[u], rstd_ready[u], shift_ready[u], i)
                        if at(1) is not None:
                            i, u = at(1)
                            dve.wait_ge(turned[u], i + 1)
                            dve.wait_ge(product_ready[u], i)
                            v.tensor_copy(ht[u][:, 0, :], turn_ps[u][:, 0:TILE]).then_inc(ht_by_dve[u], 1)
                        if at(0) is not None:
                            one_hots(tile, 1)
                        if at(2) is not None:
                            i, u = at(2)
                            t2 = i * 2 + u
                            hold(dve, h1_ready[u], i + 1)
                            for oc in range(KC):
                                seen = h1[u][:, oc, :]
                                if isinstance(t2, int) and t2 == NT - 1:
                                    seen = seen.rearrange("p (j q) -> p j q", j=ROWS)[:, :, 0:plan.last_p]
                                last = v.bn_stats(bn_stats[:, oc, bass.ds(t2 * 6, 6)], seen)
                            last.then_inc(h1_counted[u], 1)

                    over_tiles(dve, plan, 2, step)

            hb = [sb(f"hb{u}", [P, KC, TILE], where=part) for u in two]
            mix = [sb(f"mix{u}", [P, ROWS, D], where=part) for u in two]
            y_out = [sb(f"y_out{u}", [P, ROWS, D], where=part) for u in two]
            agg_out = [sb(f"agg_out{u}", [P, ROWS, D], where=part) for u in two]
            self_weight = sb("self_weight", [P, NT * ROWS], where=part)
            h1_loaded = [sem(f"b_h1_loaded{u}") for u in two]
            hb_ready = [sem(f"hb_ready{u}") for u in two]
            mix_product = [sem(f"mix_product{u}") for u in two]
            mix_ready = [sem(f"mix_ready{u}") for u in two]
            y_ready = [sem(f"y_ready{u}") for u in two]
            agg_ready = [sem(f"agg_ready{u}") for u in two]
            y_stored = [pool_dma_sem(f"y_stored{u}") for u in two]
            agg_stored = [pool_dma_sem(f"agg_stored{u}") for u in two]
            bn_ready = sem("bn_ready")
            b_chain = sem("b_chain")
            roots_ready = sem("roots_ready")

            with ExitStack() as inner, nc.Block() as block:
                mix_ps = [inner.enter_context(nc.psum_tensor(f"mix_ps{u}", [P, ROWS * D], F32)) for u in two]

                @block.sync
                def _(sp):
                    def step(at):
                        i, u = at(0)
                        sp.wait_ge(hb_ready[u], i)
                        sp.dma_start(h1[u][:, :, :].rearrange("p k c -> p (k c)"),
                                     h1_table[bass.ds((i * 2 + u) * P, P), :]).then_inc(h1_loaded[u], 16)

                    over_tiles(sp, plan, 0, step)

                @block.scalar
                def _(act):
                    act.wait_ge(b_chain, 4)
                    nc.scalar.activation(dinv[:, :], dinv[:, :], ACT.Sqrt).then_inc(roots_ready, 1)
                    nc.scalar.activation(bn_scale[:, :], bn_moments[:, :, 1], ACT.Sqrt, bias=eps_col[:, 0:1]).then_inc(roots_ready, 1)
                    act.wait_ge(bn_ready, 1)

                    def step(at):
                        if at(0) is not None:
                            i, u = at(0)
                            act.wait_ge(h1_loaded[u], 16 * i + 16)
                            act.wait_ge(mix_product[u], i)
                            for kc in range(KC):
                                last = nc.scalar.activation(hb[u][:, kc, :], h1[u][:, kc, :], ACT.Relu,
                                                            bias=bn_shift[:, kc:kc + 1], scale=bn_scale[:, kc:kc + 1])
                            last.then_inc(hb_ready[u], 1)
                        if at(2) is not None:
                            i, u = at(2)
                            tile = i * 2 + u
                            hold(act, mix_ready[u], i + 1)
                            hold(act, agg_stored[u], 16 * i)
                            for j in range(ROWS):
                                last = nc.scalar.activation(agg_out[u][:, j, :], mix[u][:, j, :], ACT.Copy,
                                                            scale=self_weight[:, bass.ds(tile * ROWS + j, 1)])
                            last.then_inc(agg_ready[u], 1)

                    over_tiles(act, plan, 2, step)

                @block.tensor
                def _(pe):
                    def step(at):
                        i, u = at(0)
                        pe.wait_ge(hb_ready[u], i + 1)
                        pe.wait_ge(mix_ready[u], i)
                        for j in range(ROWS):
                            for kc in range(KC):
                                last = nc.tensor.matmul(mix_ps[u][:, j * D:(j + 1) * D], hb[u][:, kc, j * P:(j + 1) * P],
                                                        w_mix[:, kc, :], start=kc == 0, stop=kc == KC - 1)
                        last.then_inc(mix_product[u], 1)

                    over_tiles(pe, plan, 0, step)

                @block.vector
                def _(dve):
                    v = nc.vector
                    v.tensor_scalar(dinv[:, :], hist_ps[0][:, :], 1.0, None, ALU.add).then_inc(b_chain, 1)
                    v.tensor_copy(n_self[:, :], hist_ps[1][:, :]).then_inc(b_chain, 1)
                    for oc in range(KC):
                        v.bn_aggr(bn_moments[:, oc, :], bn_stats[:, oc, :]).then_inc(b_chain, 1)
                    dve.wait_ge(roots_ready, 2)
                    v.reciprocal(dinv[:, :], dinv[:, :]).then_inc(b_chain, 1)
                    v.reciprocal(bn_scale[:, :], bn_scale[:, :]).then_inc(b_chain, 1)
                    dve.wait_ge(b_chain, 6)
                    v.scalar_tensor_tensor(self_weight[:, :], n_self[:, :], 1.0, dinv[:, :], ALU.add, ALU.mult)
                    v.tensor_tensor(bn_scale[:, :], bn_scale[:, :], bn_in[:, 1, :], ALU.mult).then_inc(b_chain, 1)
                    dve.wait_ge(b_chain, 7)
                    v.scalar_tensor_tensor(bn_shift[:, :], bn_moments[:, :, 0], -1.0, bn_scale[:, :], ALU.mult, ALU.mult).then_inc(b_chain, 1)
                    dve.wait_ge(b_chain, 8)
                    v.tensor_tensor(bn_shift[:, :], bn_shift[:, :], bn_in[:, 2, :], ALU.add).then_inc(bn_ready, 1)

                    def step(at):
                        i, u = at(0)
                        tile = i * 2 + u
                        dve.wait_ge(mix_product[u], i + 1)
                        dve.wait_ge(agg_ready[u], i)
                        v.tensor_tensor(mix[u][:, :, :], mix_ps[u][:, :].rearrange("p (j d) -> p j d", j=ROWS),
                                        b_mix[:, :].unsqueeze(1).to_broadcast([P, ROWS, D]), ALU.add).then_inc(mix_ready[u], 1)
                        dve.wait_ge(mix_ready[u], i + 1)
                        dve.wait_ge(y_stored[u], 16 * i)
                        for j in range(ROWS):
                            last = v.tensor_scalar(y_out[u][:, j, :], mix[u][:, j, :],
                                                   dinv[:, bass.ds(tile * ROWS + j, 1)], None, ALU.mult)
                        last.then_inc(y_ready[u], 1)

                    over_tiles(dve, plan, 0, step)

                @block.gpsimd
                def _(pool):
                    def step(at):
                        i, u = at(0)
                        tile = i * 2 + u
                        for ready, rows, table, stored in ((y_ready, y_out, y_table, y_stored),
                                                           (agg_ready, agg_out, agg_table, agg_stored)):
                            hold(pool, ready[u], i + 1)
                            pool.dma_start(row_block(table, tile), rows[u][:, :, :].rearrange("p r d -> p (r d)")).then_inc(stored[u], 16)

                    over_tiles(pool, plan, 0, step)
                    for u in two:
                        pool.wait_ge(y_stored[u], 16 * (NT // 2))
                        pool.wait_ge(agg_stored[u], 16 * (NT // 2))

        end_part()

        eight = range(SLOTS)

        def column_parts(name, key, where):
            return {
                "key": key,
                "group": (lambda k: k & 3) if key == 0 else (lambda k: (k & 1) << 1 | k >> 1 & 1),
                "ends": [sb(f"{name}_ends{k}", [P, 2], I32, where) for k in eight],
                "keys": [sb(f"{name}_keys{k}", [P, 2], F32, where) for k in eight],
                "same": [sb(f"{name}_same{k}", [P, P], F32, where) for k in range(4)],
                "rank_of": sb(f"{name}_rank_of", [P, P], F32, where),
                "rank": [sb(f"{name}_rank{k}", [P, 1], F32, where) for k in eight],
                "offset": [sb(f"{name}_offset{k}", [P, 1], F32, where) for k in eight],
                "goal": [sb(f"{name}_goal{k}", [P, 1], I32, where) for k in eight],
                "across": [where.enter_context(nc.psum_tensor(f"{name}_across{k}", [P, 512], F32)) for k in range(2)],
                "staged": sem(f"{name}_staged"),
                "across_ready": sem(f"{name}_across_ready"),
                "ranked": sem(f"{name}_ranked"),
                "offset_ready": sem(f"{name}_offset_ready"),
                "goal_ready": sem(f"{name}_goal_ready"),
                "scattered": [pool_dma_sem(f"{name}_scattered{k}") for k in eight],
            }

        def number(column):
            i, k = column
            return i * SLOTS + (k + 1)

        def wait_past(eng, s, value):
            if not isinstance(value, int) or value > 0:
                eng.wait_ge(s, value)

        def load_turns(eng):
            return eng.value_load(more_turns[0:1, 0:1], min_val=0, max_val=PACKED // 2 - 2) + 2

        def stage_column(dve, c, column):
            i, k = column
            g = c["group"](k % GROUPS)
            at = bass.ds(i * 2 + k // GROUPS, 1)
            hold(dve, c["scattered"][k], i * 16)
            nc.vector.tensor_copy(c["ends"][k][:, :], packed_i[:, :, g, at].rearrange("p a o -> p (a o)"))
            nc.vector.tensor_copy(c["keys"][k][:, 0:1], packed_f[:, c["key"], g, at])
            nc.vector.tensor_scalar(c["keys"][k][:, 1:2], packed_f[:, c["key"], g, at], spare[:, 1 + k % 2:2 + k % 2], None,
                                    ALU.subtract).then_inc(c["staged"], 1)

        def keys_across(pe, c, column):
            i, k = column
            pe.wait_ge(c["staged"], number(column))
            wait_past(pe, c["ranked"], number(column) - 2)
            nc.tensor.matmul(c["across"][k % 2][:, 0:P], c["keys"][k][:, 0:1].to_broadcast([P, P]), ident[:, :],
                             start=True, stop=True).then_inc(c["across_ready"], 1)

        def find_goals(dve, c, column, write_same):
            i, k = column
            v = nc.vector
            n = number(column)
            across, keys = c["across"][k % 2][:, 0:P], c["keys"][k]
            dve.wait_ge(c["across_ready"], n)
            write_same(across, keys[:, 0:1], k)
            v.scalar_tensor_tensor(c["rank_of"][:, :], across, keys[:, 0:1], earlier[:, :], ALU.is_equal, ALU.mult,
                                   accum_out=c["rank"][k][:, 0:1]).then_inc(c["ranked"], 1)
            dve.wait_ge(c["ranked"], n)
            v.tensor_scalar(c["offset"][k][:, :], c["rank"][k][:, :], 0.0, keys[:, 1:2], ALU.is_equal,
                            ALU.mult).then_inc(c["offset_ready"], 1)
            dve.wait_ge(c["offset_ready"], n)
            v.tensor_scalar(c["goal"][k][:, :], c["offset"][k][:, :], spare[:, 1 + k % 2:2 + k % 2], None, ALU.add).then_inc(c["goal_ready"], 1)

        def gather(rows, table, index):
            return nc.gpsimd.indirect_dma_start(out=rows, out_offset=None, in_=table,
                                                in_offset=bass.IndirectOffsetOnAxis(ap=index, axis=0))

        def scatter(table, index, rows, **how):
            return nc.gpsimd.indirect_dma_start(out=table, out_offset=bass.IndirectOffsetOnAxis(ap=index, axis=0),
                                                in_=rows, in_offset=None, **how)

        with ExitStack() as part, nc.Block() as block:
            c = column_parts("gcn", 1, part)
            got = [sb(f"gcn_got{k}", [P, D], where=part) for k in eight]
            summed = [sb(f"gcn_summed{k}", [P, D], where=part) for k in eight]
            sum_ps = [part.enter_context(nc.psum_tensor(f"gcn_sum_ps{k}", [P, 512], F32)) for k in range(2)]
            gathered = [pool_dma_sem(f"gcn_gathered{k}") for k in eight]
            sum_ready = sem("gcn_sum_ready")
            summed_ready = sem("gcn_summed_ready")

            @block.gpsimd
            def _(pool):
                turns = load_turns(pool)

                def step(at):
                    if (col := at(0)) is not None:
                        i, k = col
                        hold(pool, c["staged"], number(col))
                        gather(got[k][:, :], y_table, c["ends"][k][:, 0:1]).then_inc(gathered[k], 16)
                    if (col := at(3)) is not None:
                        i, k = col
                        hold(pool, summed_ready, number(col))
                        if (two_back := at(5)) is not None:
                            hold(pool, c["scattered"][two_back[1]], two_back[0] * 16 + 16)
                        hold(pool, c["goal_ready"], number(col))
                        scatter(agg_table, c["goal"][k][:, 0:1], summed[k][:, :], compute_op=ALU.add).then_inc(c["scattered"][k], 16)

                over_columns(pool, turns, 3, step)
                for k in eight:
                    hold(pool, c["scattered"][k], turns * 16)

            @block.vector
            def _(dve):
                turns = load_turns(dve)

                def write_same(across, key, k):
                    nc.vector.tensor_scalar(c["same"][k % 4][:, :], across, key, None, ALU.is_equal)

                def step(at):
                    if (col := at(0)) is not None:
                        stage_column(dve, c, col)
                    if (col := at(1)) is not None:
                        wait_past(dve, sum_ready, number(col) - 4)
                        find_goals(dve, c, col, write_same)

                over_columns(dve, turns, 1, step)

            @block.tensor
            def _(pe):
                turns = load_turns(pe)

                def step(at):
                    if (col := at(0)) is not None:
                        keys_across(pe, c, col)
                    if (col := at(2)) is not None:
                        i, k = col
                        pe.wait_ge(c["ranked"], number(col))
                        pe.wait_ge(gathered[k], i * 16 + 16)
                        wait_past(pe, summed_ready, number(col) - 2)
                        nc.tensor.matmul(sum_ps[k % 2][:, 0:D], c["same"][k % 4][:, :], got[k][:, :],
                                         start=True, stop=True).then_inc(sum_ready, 1)

                over_columns(pe, turns, 2, step)

            @block.scalar
            def _(act):
                turns = load_turns(act)

                def step(at):
                    i, k = col = at(0)
                    act.wait_ge(sum_ready, number(col))
                    nc.scalar.activation(summed[k][:, :], sum_ps[k % 2][:, 0:D], ACT.Copy).then_inc(summed_ready, 1)

                over_columns(act, turns, 0, step)

        end_part()

        with ExitStack() as part, nc.Block() as block:
            agg = [sb(f"c_agg{u}", [P, ROWS, D], where=part) for u in two]
            xb = [sb(f"c_x{u}", [P, ROWS, D], where=part) for u in two]
            x1 = [sb(f"c_x1_{u}", [P, ROWS, D], where=part) for u in two]
            stats = [sb(f"c_stats{u}", [P, ROWS, 6], where=part) for u in two]
            moments = [sb(f"c_moments{u}", [P, ROWS, 2], where=part) for u in two]
            std = [sb(f"c_std{u}", [P, ROWS], where=part) for u in two]
            rstd = [sb(f"c_rstd{u}", [P, ROWS], where=part) for u in two]
            shift = [sb(f"c_shift{u}", [P, ROWS], where=part) for u in two]
            hn = [sb(f"c_hn{u}", [P, ROWS, D], where=part) for u in two]
            ht = [sb(f"c_ht{u}", [P, KC, TILE], where=part) for u in two]
            qkv = [sb(f"c_qkv{u}", [P, 3, ROWS, D], where=part) for u in two]
            qk = [sb(f"c_qk{u}", [P, ROWS, D], where=part) for u in two]
            raw = [sb(f"c_raw{u}", [P, ROWS, H], where=part) for u in two]
            masked = [sb(f"c_masked{u}", [P, ROWS, H], where=part) for u in two]
            peak0 = [sb(f"c_peak{u}", [P, ROWS, H], where=part) for u in two]
            has_self = sb("has_self", [P, NT * ROWS], where=part)
            no_self = sb("no_self", [P, NT * ROWS], where=part)
            loaded = [sem(f"c_loaded{u}") for u in two]
            biased = [sem(f"c_biased{u}") for u in two]
            x1_ready = [sem(f"c_x1_ready{u}") for u in two]
            x1_stored = [sem(f"c_x1_stored{u}") for u in two]
            stats_ready = [sem(f"c_stats_ready{u}") for u in two]
            moments_ready = [sem(f"c_moments_ready{u}") for u in two]
            std_ready = [sem(f"c_std_ready{u}") for u in two]
            rstd_ready = [sem(f"c_rstd_ready{u}") for u in two]
            shift_ready = [sem(f"c_shift_ready{u}") for u in two]
            hn_ready = [sem(f"c_hn_ready{u}") for u in two]
            turned = sem("c_turned")
            ht_ready = sem("c_ht_ready")
            product_ready = sem("c_product_ready")
            qkv_ready = sem("c_qkv_ready")
            qkv_stored = [sem(f"c_qkv_stored{u}") for u in two]
            qk_ready = sem("c_qk_ready")
            raw_ready = sem("c_raw_ready")
            masked_ready = sem("c_masked_ready")
            peak_ready = sem("c_peak_ready")
            peak_stored = [sem(f"c_peak_stored{u}") for u in two]
            c_chain = sem("c_chain")
            turn_ps = part.enter_context(nc.psum_tensor("c_turn_ps", [P, KC * TILE], F32))
            qkv_ps = [part.enter_context(nc.psum_tensor(f"c_qkv_ps{i}", [P, ROWS * D], F32)) for i in range(3)]

            def tile_of(t):
                return t[0] * 2 + t[1]

            @block.sync
            def _(sp):
                def step(at):
                    if at(0) is not None:
                        i, u = at(0)
                        tile = tile_of(at(0))
                        sp.wait_ge(x1_ready[u], i)
                        sp.dma_start(agg[u][:, :, :].rearrange("p r d -> p (r d)"), row_block(agg_table, tile)).then_inc(loaded[u], 16)
                        if isinstance(tile, int) and tile == NT - 1:
                            rows = x[tile * TILE:plan.n, :].rearrange("(p r) d -> p (r d)", r=ROWS)
                            sp.dma_start(xb[u][0:plan.last_p, :, :].rearrange("p r d -> p (r d)"), rows).then_inc(loaded[u], 16)
                        else:
                            sp.dma_start(xb[u][:, :, :].rearrange("p r d -> p (r d)"), row_block(x, tile)).then_inc(loaded[u], 16)
                    if at(1) is not None:
                        i, u = at(1)
                        sp.wait_ge(x1_ready[u], i + 1)
                        sp.dma_start(row_block(x1_table, tile_of(at(1))), x1[u][:, :, :].rearrange("p r d -> p (r d)")).then_inc(x1_stored[u], 16)
                    if at(3) is not None:
                        i, u = at(3)
                        tile = tile_of(at(3))
                        sp.wait_ge(qkv_ready, tile * 3 + 3)
                        for n, table in enumerate((q_table, k_table, v_table)):
                            sp.dma_start(row_block(table, tile), qkv[u][:, n, :, :].rearrange("p r d -> p (r d)")).then_inc(qkv_stored[u], 16)
                    if at(4) is not None:
                        i, u = at(4)
                        tile = tile_of(at(4))
                        sp.wait_ge(peak_ready, tile + 1)
                        sp.dma_start(row_block(m_table, tile), peak0[u][:, :, :].rearrange("p r h -> p (r h)")).then_inc(peak_stored[u], 16)

                over_tiles(sp, plan, 4, step)
                for u in two:
                    sp.wait_ge(x1_stored[u], 16 * (NT // 2))
                    sp.wait_ge(qkv_stored[u], 48 * (NT // 2))
                    sp.wait_ge(peak_stored[u], 16 * (NT // 2))

            @block.gpsimd
            def _(pool):
                def step(at):
                    if at(0) is not None:
                        i, u = at(0)
                        hold(pool, loaded[u], i * 32 + 32)
                        nc.gpsimd.tensor_tensor(xb[u][:, :, :], xb[u][:, :, :], b_agg[:, :].unsqueeze(1).to_broadcast([P, ROWS, D]),
                                                ALU.add).then_inc(biased[u], 1)
                    if at(2) is not None:
                        i, u = at(2)
                        tile = tile_of(at(2))
                        hold(pool, qkv_ready, tile * 3 + 2)
                        wait_past(pool, raw_ready, tile - 1)
                        nc.gpsimd.tensor_tensor(qk[u][:, :, :], qkv[u][:, 0, :, :], qkv[u][:, 1, :, :], ALU.mult).then_inc(qk_ready, 1)

                over_tiles(pool, plan, 2, step)

            @block.scalar
            def _(act):
                def step(at):
                    if at(0) is not None:
                        i, u = at(0)
                        act.wait_ge(moments_ready[u], i + 1)
                        act.wait_ge(shift_ready[u], i)
                        nc.scalar.activation(std[u][:, :], moments[u][:, :, 1], ACT.Sqrt, bias=eps_col[:, 0:1]).then_inc(std_ready[u], 1)
                        act.wait_ge(shift_ready[u], i + 1)
                        wait_past(act, turned, tile_of(at(0)) - 1)
                        for j in range(ROWS):
                            last = nc.scalar.activation(hn[u][:, j, :], x1[u][:, j, :], ACT.Relu,
                                                        bias=shift[u][:, j:j + 1], scale=rstd[u][:, j:j + 1])
                        last.then_inc(hn_ready[u], 1)
                        tile = tile_of(at(0))
                        act.wait_ge(turned, tile + 1)
                        wait_past(act, product_ready, tile * 3 - 3)
                        for kc in range(KC):
                            last = nc.scalar.activation(ht[u][:, kc, :], turn_ps[:, kc * TILE:(kc + 1) * TILE], ACT.Copy)
                        last.then_inc(ht_ready, 1)

                over_tiles(act, plan, 0, step)

            @block.tensor
            def _(pe):
                def step(at):
                    if at(0) is not None:
                        i, u = at(0)
                        pe.wait_ge(hn_ready[u], i + 1)
                        wait_past(pe, ht_ready, tile_of(at(0)))
                        for kc in range(KC):
                            for j in range(ROWS):
                                last = nc.tensor.transpose(turn_ps[:, kc * TILE + j * P:kc * TILE + (j + 1) * P],
                                                           hn[u][:, j, kc * P:(kc + 1) * P], ident[:, :])
                        last.then_inc(turned, 1)
                    if at(1) is not None:
                        i, u = at(1)
                        tile = tile_of(at(1))
                        pe.wait_ge(ht_ready, tile + 1)
                        for n in range(3):
                            wait_past(pe, qkv_ready, tile * 3 - 2 + n)
                            for j in range(ROWS):
                                for kc in range(KC):
                                    last = nc.tensor.matmul(qkv_ps[n][:, j * D:(j + 1) * D], ht[u][:, kc, j * P:(j + 1) * P],
                                                            w_qkv[:, kc, n * D:(n + 1) * D], start=kc == 0, stop=kc == KC - 1)
                            last.then_inc(product_ready, 1)

                over_tiles(pe, plan, 1, step)

            @block.vector
            def _(dve):
                v = nc.vector
                v.tensor_scalar(has_self[:, :], n_self[:, :], 1.0, None, ALU.min).then_inc(c_chain, 1)
                dve.wait_ge(c_chain, 1)
                v.tensor_scalar(no_self[:, :], has_self[:, :], -1.0, -LOW, ALU.add, ALU.mult).then_inc(c_chain, 1)
                dve.wait_ge(c_chain, 2)
                v.tensor_scalar(has_self[:, :], has_self[:, :], SCALE, None, ALU.mult).then_inc(c_chain, 1)
                dve.wait_ge(c_chain, 3)

                def step(at):
                    if at(0) is not None:
                        i, u = at(0)
                        tile = tile_of(at(0))
                        hold(dve, biased[u], i + 1)
                        hold(dve, x1_stored[u], i * 16)
                        hold(dve, hn_ready[u], i)
                        for j in range(ROWS):
                            last = v.scalar_tensor_tensor(x1[u][:, j, :], agg[u][:, j, :], dinv[:, bass.ds(tile * ROWS + j, 1)],
                                                          xb[u][:, j, :], ALU.mult, ALU.add)
                        last.then_inc(x1_ready[u], 1)
                        dve.wait_ge(x1_ready[u], i + 1)
                        row_moments(v, dve, hold, x1[u], stats[u], moments[u], stats_ready[u], moments_ready[u], i)
                    if at(2) is not None:
                        i, u2 = at(2)
                        t2 = tile_of(at(2))
                        for n in range(3):
                            dve.wait_ge(product_ready, t2 * 3 + 1 + n)
                            if n == 0:
                                dve.wait_ge(qkv_stored[u2], i * 48)
                                wait_past(dve, qk_ready, t2 - 1)
                            v.tensor_tensor(qkv[u2][:, n, :, :], qkv_ps[n][:, :].rearrange("p (j d) -> p j d", j=ROWS),
                                            b_qkv[:, n * D:(n + 1) * D].unsqueeze(1).to_broadcast([P, ROWS, D]),
                                            ALU.add).then_inc(qkv_ready, 1)
                            if n == 0 and at(0) is not None:
                                i0, u = at(0)
                                row_scales(v, dve, moments[u], std[u], rstd[u], shift[u],
                                           std_ready[u], rstd_ready[u], shift_ready[u], i0)
                    elif at(0) is not None:
                        row_scales(v, dve, moments[u], std[u], rstd[u], shift[u],
                                   std_ready[u], rstd_ready[u], shift_ready[u], i)
                    if at(3) is not None:
                        i, u = at(3)
                        tile = tile_of(at(3))
                        dve.wait_ge(qk_ready, tile + 1)
                        v.reduce_sum(raw[u][:, :, :], qk[u][:, :, :].rearrange("p j (d h) -> p j h d", h=H),
                                     axis=AX.X).then_inc(raw_ready, 1)
                        hold(dve, raw_ready, tile + 1)
                        here = bass.ds(tile * ROWS, ROWS)
                        v.tensor_scalar(self_score[:, bass.ds(tile * (ROWS * H), ROWS * H)],
                                        raw[u][:, :, :].rearrange("p j h -> p (j h)"), SCALE, None, ALU.mult)
                        v.tensor_tensor(masked[u][:, :, :], raw[u][:, :, :], has_self[:, here].unsqueeze(2).to_broadcast([P, ROWS, H]),
                                        ALU.mult).then_inc(masked_ready, 1)
                        hold(dve, masked_ready, tile + 1)
                        hold(dve, peak_stored[u], i * 16)
                        v.tensor_tensor(peak0[u][:, :, :], masked[u][:, :, :], no_self[:, here].unsqueeze(2).to_broadcast([P, ROWS, H]),
                                        ALU.add).then_inc(peak_ready, 1)

                over_tiles(dve, plan, 3, step)

        end_part()
        scores = sb("scores", [P, PACKED // 2 * SLOTS * H])

        with ExitStack() as part, nc.Block() as block:
            c = column_parts("peak", 0, part)
            q_got = [sb(f"peak_q{k}", [P, D], where=part) for k in eight]
            k_got = [sb(f"peak_k{k}", [P, D], where=part) for k in eight]
            m_got = [sb(f"peak_m{k}", [P, H], where=part) for k in eight]
            m_new = [sb(f"peak_new{k}", [P, H], where=part) for k in eight]
            score = [sb(f"peak_score{k}", [P, H], where=part) for k in eight]
            top = [sb(f"peak_top{k}", [P, H], where=part) for k in eight]
            qk = [sb(f"peak_qk{k}", [P, D], where=part) for k in two]
            differ = [sb(f"peak_differ{k}", [P, P], BF16, where=part) for k in range(4)]
            score_ps = [part.enter_context(nc.psum_tensor(f"score_ps{k}", [P, H * P], F32)) for k in two]
            qk_gathered = [pool_dma_sem(f"peak_qk_gathered{k}") for k in eight]
            m_gathered = [pool_dma_sem(f"peak_m_gathered{k}") for k in eight]
            qk_ready = sem("peak_qk_ready")
            score_ready = sem("peak_score_ready")
            spread_ready = sem("peak_spread_ready")
            top_ready = sem("peak_top_ready")
            new_ready = sem("peak_new_ready")

            @block.gpsimd
            def _(pool):
                turns = load_turns(pool)

                def step(at):
                    if (col := at(0)) is not None:
                        i, k = col
                        hold(pool, c["staged"], number(col))
                        gather(q_got[k][:, :], q_table, c["ends"][k][:, 0:1]).then_inc(qk_gathered[k], 16)
                        gather(k_got[k][:, :], k_table, c["ends"][k][:, 1:2]).then_inc(qk_gathered[k], 16)
                    if (col := at(4)) is not None:
                        i, k = col
                        hold(pool, new_ready, number(col))
                        scatter(m_table, c["goal"][k][:, 0:1], m_new[k][:, :]).then_inc(c["scattered"][k], 16)
                    if (col := at(3)) is not None:
                        i, k = col
                        if (two_back := at(5)) is not None:
                            hold(pool, c["scattered"][two_back[1]], two_back[0] * 16 + 16)
                        gather(m_got[k][:, :], m_table, c["ends"][k][:, 0:1]).then_inc(m_gathered[k], 16)

                over_columns(pool, turns, 4, step)
                for k in eight:
                    hold(pool, c["scattered"][k], turns * 16)

            @block.vector
            def _(dve):
                turns = load_turns(dve)
                v = nc.vector

                def write_differ(across, key, k):
                    v.tensor_scalar(differ[k % 4][:, :], across, key, LOW, ALU.not_equal, ALU.mult)

                def step(at):
                    if (col := at(0)) is not None:
                        stage_column(dve, c, col)
                    if (col := at(1)) is not None:
                        wait_past(dve, spread_ready, number(col) - 4)
                        find_goals(dve, c, col, write_differ)
                    if (col := at(2)) is not None:
                        i, k = col
                        n = number(col)
                        dve.wait_ge(qk_gathered[k], i * 32 + 32)
                        v.scalar_tensor_tensor(qk[k % 2][:, :], q_got[k][:, :], SCALE, k_got[k][:, :], ALU.mult,
                                               ALU.mult).then_inc(qk_ready, 1)
                        dve.wait_ge(qk_ready, n)
                        v.reduce_sum(score[k][:, :], qk[k % 2][:, :].rearrange("p (d h) -> p h d", h=H), axis=AX.X).then_inc(score_ready, 1)
                        hold(dve, score_ready, n)
                        v.tensor_copy(scores[:, bass.ds((i * SLOTS + k) * H, H)], score[k][:, :])
                    if (col := at(3)) is not None:
                        i, k = col
                        dve.wait_ge(spread_ready, number(col))
                        v.reduce_max(top[k][:, :], score_ps[k % 2][:, :].rearrange("p (h e) -> p h e", h=H), axis=AX.X).then_inc(top_ready, 1)
                    if (col := at(4)) is not None:
                        i, k = col
                        dve.wait_ge(m_gathered[k], i * 16 + 16)
                        v.tensor_tensor(m_new[k][:, :], m_got[k][:, :], top[k][:, :], ALU.max).then_inc(new_ready, 1)

                over_columns(dve, turns, 4, step)

            @block.tensor
            def _(pe):
                turns = load_turns(pe)

                def step(at):
                    if (col := at(0)) is not None:
                        keys_across(pe, c, col)
                    if (col := at(2)) is not None:
                        i, k = col
                        n = number(col)
                        pe.wait_ge(score_ready, n)
                        wait_past(pe, top_ready, n - 2)
                        half = H // 2
                        for b in range(2):
                            nc.tensor.matmul(score_ps[k % 2][:, b * 512:(b + 1) * 512], ident_b[:, :],
                                             differ[k % 4][:, :].unsqueeze(1).to_broadcast([P, half, P]), start=True, stop=False)
                            for h in range(half):
                                at_h = b * half + h
                                last = nc.tensor.matmul(score_ps[k % 2][:, at_h * P:(at_h + 1) * P],
                                                        score[k][:, at_h:at_h + 1].to_broadcast([P, P]), ident[:, :],
                                                        start=False, stop=h == half - 1)
                        last.then_inc(spread_ready, 1)

                over_columns(pe, turns, 2, step)

        end_part()

        with ExitStack() as part, nc.Block() as block:
            c = column_parts("acc", 0, part)
            v_got = [sb(f"acc_v{k}", [P, D], where=part) for k in eight]
            m_got = [sb(f"acc_m{k}", [P, H], where=part) for k in eight]
            above = [sb(f"acc_above{k}", [P, H], where=part) for k in eight]
            part_of = [sb(f"acc_part{k}", [P, D + H], where=part) for k in eight]
            summed = [sb(f"acc_summed{k}", [P, D + H], where=part) for k in eight]
            sum_ps = [part.enter_context(nc.psum_tensor(f"acc_sum_ps{k}", [P, 512], F32)) for k in two]
            gathered = [pool_dma_sem(f"acc_gathered{k}") for k in eight]
            above_ready = sem("acc_above_ready")
            weight_ready = sem("acc_weight_ready")
            part_ready = sem("acc_part_ready")
            sum_ready = sem("acc_sum_ready")
            summed_ready = sem("acc_summed_ready")

            @block.gpsimd
            def _(pool):
                turns = load_turns(pool)

                def step(at):
                    if (col := at(0)) is not None:
                        i, k = col
                        hold(pool, c["staged"], number(col))
                        gather(v_got[k][:, :], v_table, c["ends"][k][:, 1:2]).then_inc(gathered[k], 16)
                        gather(m_got[k][:, :], m_table, c["ends"][k][:, 0:1]).then_inc(gathered[k], 16)
                    if (col := at(5)) is not None:
                        i, k = col
                        hold(pool, summed_ready, number(col))
                        if (two_back := at(7)) is not None:
                            hold(pool, c["scattered"][two_back[1]], two_back[0] * 16 + 16)
                        hold(pool, c["goal_ready"], number(col))
                        scatter(acc_table, c["goal"][k][:, 0:1], summed[k][:, :], compute_op=ALU.add).then_inc(c["scattered"][k], 16)

                over_columns(pool, turns, 5, step)
                for k in eight:
                    hold(pool, c["scattered"][k], turns * 16)

            @block.vector
            def _(dve):
                turns = load_turns(dve)
                v = nc.vector

                def write_same(across, key, k):
                    v.tensor_scalar(c["same"][k % 4][:, :], across, key, None, ALU.is_equal)

                def step(at):
                    if (col := at(0)) is not None:
                        stage_column(dve, c, col)
                    if (col := at(1)) is not None:
                        wait_past(dve, sum_ready, number(col) - 4)
                        find_goals(dve, c, col, write_same)
                    if (col := at(2)) is not None:
                        i, k = col
                        dve.wait_ge(gathered[k], i * 32 + 32)
                        v.tensor_tensor(above[k][:, :], scores[:, bass.ds((i * SLOTS + k) * H, H)], m_got[k][:, :],
                                        ALU.subtract).then_inc(above_ready, 1)
                    if (col := at(3)) is not None:
                        i, k = col
                        dve.wait_ge(weight_ready, number(col))
                        v.tensor_tensor(part_of[k][:, 0:D].rearrange("p (d h) -> p d h", h=H),
                                        v_got[k][:, :].rearrange("p (d h) -> p d h", h=H),
                                        part_of[k][:, D:D + H].unsqueeze(1).to_broadcast([P, DH, H]), ALU.mult).then_inc(part_ready, 1)

                over_columns(dve, turns, 3, step)

            @block.tensor
            def _(pe):
                turns = load_turns(pe)

                def step(at):
                    if (col := at(0)) is not None:
                        keys_across(pe, c, col)
                    if (col := at(3)) is not None:
                        i, k = col
                        n = number(col)
                        pe.wait_ge(part_ready, n)
                        wait_past(pe, summed_ready, n - 2)
                        nc.tensor.matmul(sum_ps[k % 2][:, 0:D + H], c["same"][k % 4][:, :], part_of[k][:, :],
                                         start=True, stop=True).then_inc(sum_ready, 1)

                over_columns(pe, turns, 3, step)

            @block.scalar
            def _(act):
                turns = load_turns(act)

                def step(at):
                    if (col := at(0)) is not None:
                        i, k = col
                        act.wait_ge(above_ready, number(col))
                        nc.scalar.activation(part_of[k][:, D:D + H], above[k][:, :], ACT.Exp).then_inc(weight_ready, 1)
                    if (col := at(1)) is not None:
                        i, k = col
                        act.wait_ge(sum_ready, number(col))
                        nc.scalar.activation(summed[k][:, :], sum_ps[k % 2][:, 0:D + H], ACT.Copy).then_inc(summed_ready, 1)

                over_columns(act, turns, 1, step)

        end_part()

        with ExitStack() as part, nc.Block() as block:
            acc = [sb(f"e_acc{u}", [P, ROWS, D + H], where=part) for u in two]
            vb = [sb(f"e_v{u}", [P, ROWS, D], where=part) for u in two]
            x1 = [sb(f"e_x1_{u}", [P, ROWS, D], where=part) for u in two]
            peak = [sb(f"e_peak{u}", [P, ROWS * H], where=part) for u in two]
            above = [sb(f"e_above{u}", [P, ROWS * H], where=part) for u in two]
            weight = [sb(f"e_weight{u}", [P, ROWS, H], where=part) for u in two]
            total = [sb(f"e_total{u}", [P, ROWS, H], where=part) for u in two]
            own = [sb(f"e_own{u}", [P, ROWS, D], where=part) for u in two]
            ht = [sb(f"e_ht{u}", [P, KC, TILE], where=part) for u in two]
            result = [sb(f"e_result{u}", [P, ROWS, D], where=part) for u in two]
            loaded = [sem(f"e_loaded{u}") for u in two]
            x1_loaded = [sem(f"e_x1_loaded{u}") for u in two]
            e_chain = sem("e_above_raw")
            total_ready = sem("e_total_ready")
            full_ready = sem("e_full_ready")
            above_ready = sem("e_above_ready")
            exp_ready = sem("e_exp_ready")
            weight_ready = sem("e_weight_ready")
            own_ready = sem("e_own_ready")
            mean_ready = sem("e_mean_ready")
            turned = sem("e_turned")
            ht_ready = sem("e_ht_ready")
            product_ready = sem("e_product_ready")
            x1_biased = sem("e_x1_biased")
            result_ready = sem("e_result_ready")
            result_stored = [sem(f"e_result_stored{u}") for u in two]
            turn_ps = [part.enter_context(nc.psum_tensor(f"e_turn_ps{u}", [P, KC * TILE], F32)) for u in two]
            out_ps = [part.enter_context(nc.psum_tensor(f"e_out_ps{u}", [P, ROWS * D], F32)) for u in two]

            @block.sync
            def _(sp):
                def step(at):
                    if at(0) is not None:
                        i, u = at(0)
                        tile = tile_of(at(0))
                        wait_past(sp, mean_ready, tile - 1)
                        sp.dma_start(acc[u][:, :, :].rearrange("p r d -> p (r d)"), row_block(acc_table, tile)).then_inc(loaded[u], 16)
                        sp.dma_start(vb[u][:, :, :].rearrange("p r d -> p (r d)"), row_block(v_table, tile)).then_inc(loaded[u], 16)
                        sp.dma_start(peak[u][:, :], row_block(m_table, tile)).then_inc(loaded[u], 16)
                    if at(2) is not None:
                        i, u = at(2)
                        tile = tile_of(at(2))
                        wait_past(sp, result_ready, tile - 1)
                        sp.dma_start(x1[u][:, :, :].rearrange("p r d -> p (r d)"), row_block(x1_table, tile)).then_inc(x1_loaded[u], 16)
                    if at(4) is not None:
                        i, u = at(4)
                        tile = tile_of(at(4))
                        sp.wait_ge(result_ready, tile + 1)
                        if isinstance(tile, int) and tile == NT - 1:
                            sp.dma_start(out[tile * TILE:plan.n, :].rearrange("(p r) d -> p (r d)", r=ROWS),
                                         result[u][0:plan.last_p, :, :].rearrange("p r d -> p (r d)")).then_inc(result_stored[u], 16)
                        else:
                            sp.dma_start(row_block(out, tile), result[u][:, :, :].rearrange("p r d -> p (r d)")).then_inc(result_stored[u], 16)

                over_tiles(sp, plan, 4, step)
                for u in two:
                    sp.wait_ge(result_stored[u], 16 * (NT // 2))

            @block.gpsimd
            def _(pool):
                def step(at):
                    if at(0) is not None:
                        i, u = at(0)
                        tile = tile_of(at(0))
                        if at(2) is not None:
                            hold(pool, turned, tile - 1)
                        hold(pool, weight_ready, tile + 1)
                        nc.gpsimd.tensor_tensor(own[u][:, :, :].rearrange("p r (d h) -> p r d h", h=H),
                                                vb[u][:, :, :].rearrange("p r (d h) -> p r d h", h=H),
                                                weight[u][:, :, :].unsqueeze(2).to_broadcast([P, ROWS, DH, H]),
                                                ALU.mult).then_inc(own_ready, 1)
                    if at(2) is not None:
                        i, u = at(2)
                        hold(pool, x1_loaded[u], i * 16 + 16)
                        nc.gpsimd.tensor_tensor(x1[u][:, :, :], x1[u][:, :, :], b_out[:, :].unsqueeze(1).to_broadcast([P, ROWS, D]),
                                                ALU.add).then_inc(x1_biased, 1)

                over_tiles(pool, plan, 2, step)

            @block.vector
            def _(dve):
                v = nc.vector

                def step(at):
                    if at(0) is not None:
                        i, u = at(0)
                        tile = tile_of(at(0))
                        dve.wait_ge(loaded[u], i * 48 + 48)
                        v.tensor_tensor(above[u][:, :], self_score[:, bass.ds(tile * (ROWS * H), ROWS * H)], peak[u][:, :],
                                        ALU.subtract).then_inc(e_chain, 1)
                    if at(3) is not None:
                        i, u = at(3)
                        t3 = tile_of(at(3))
                        dve.wait_ge(product_ready, t3 + 1)
                        dve.wait_ge(x1_biased, t3 + 1)
                        dve.wait_ge(result_stored[u], i * 16)
                        v.tensor_tensor(result[u][:, :, :], out_ps[u][:, :].rearrange("p (r d) -> p r d", r=ROWS), x1[u][:, :, :],
                                        ALU.add).then_inc(result_ready, 1)
                    if at(0) is not None:
                        i, u = at(0)
                        dve.wait_ge(e_chain, tile + 1)
                        v.tensor_scalar(above[u][:, :], above[u][:, :], 0.0, None, ALU.min).then_inc(above_ready, 1)
                        dve.wait_ge(exp_ready, tile + 1)
                        hold(dve, own_ready, tile)
                        v.tensor_tensor(weight[u][:, :, :], weight[u][:, :, :],
                                        n_self[:, bass.ds(tile * ROWS, ROWS)].unsqueeze(2).to_broadcast([P, ROWS, H]),
                                        ALU.mult).then_inc(weight_ready, 1)
                    if at(1) is not None:
                        i, u = at(1)
                        t1 = tile_of(at(1))
                        v.tensor_tensor(total[u][:, :, :], acc[u][:, :, D:D + H], weight[u][:, :, :], ALU.add).then_inc(total_ready, 1)
                        dve.wait_ge(total_ready, t1 * 3 + 1)
                        v.tensor_scalar(total[u][:, :, :], total[u][:, :, :], 0.5, None, ALU.max).then_inc(total_ready, 1)
                        dve.wait_ge(total_ready, t1 * 3 + 2)
                        v.reciprocal(total[u][:, :, :], total[u][:, :, :]).then_inc(total_ready, 1)
                        dve.wait_ge(own_ready, t1 + 1)
                        v.tensor_tensor(acc[u][:, :, 0:D], acc[u][:, :, 0:D], own[u][:, :, :], ALU.add).then_inc(full_ready, 1)
                        dve.wait_ge(total_ready, t1 * 3 + 3)
                        dve.wait_ge(full_ready, t1 + 1)
                        wait_past(dve, turned, t1 - 1)
                        v.tensor_tensor(own[u][:, :, :].rearrange("p r (d h) -> p r d h", h=H),
                                        acc[u][:, :, 0:D].rearrange("p r (d h) -> p r d h", h=H),
                                        total[u][:, :, :].unsqueeze(2).to_broadcast([P, ROWS, DH, H]),
                                        ALU.mult).then_inc(mean_ready, 1)

                over_tiles(dve, plan, 3, step)

            @block.scalar
            def _(act):
                def step(at):
                    if at(0) is not None:
                        i, u = at(0)
                        tile = tile_of(at(0))
                        act.wait_ge(above_ready, tile + 1)
                        nc.scalar.activation(weight[u][:, :, :].rearrange("p r h -> p (r h)"), above[u][:, :], ACT.Exp).then_inc(exp_ready, 1)
                    if at(2) is not None:
                        i, u = at(2)
                        tile = tile_of(at(2))
                        act.wait_ge(turned, tile + 1)
                        wait_past(act, product_ready, tile - 1)
                        for kc in range(KC):
                            last = nc.scalar.activation(ht[u][:, kc, :], turn_ps[u][:, kc * TILE:(kc + 1) * TILE], ACT.Copy)
                        last.then_inc(ht_ready, 1)

                over_tiles(act, plan, 2, step)

            @block.tensor
            def _(pe):
                def step(at):
                    if at(1) is not None:
                        i, u = at(1)
                        tile = tile_of(at(1))
                        pe.wait_ge(mean_ready, tile + 1)
                        wait_past(pe, ht_ready, tile - 1)
                        for kc in range(KC):
                            for j in range(ROWS):
                                last = nc.tensor.transpose(turn_ps[u][:, kc * TILE + j * P:kc * TILE + (j + 1) * P],
                                                           own[u][:, j, kc * P:(kc + 1) * P], ident[:, :])
                        last.then_inc(turned, 1)
                    if at(2) is not None:
                        i, u = at(2)
                        tile = tile_of(at(2))
                        pe.wait_ge(ht_ready, tile + 1)
                        wait_past(pe, result_ready, tile - 1)
                        for j in range(ROWS):
                            for kc in range(KC):
                                last = nc.tensor.matmul(out_ps[u][:, j * D:(j + 1) * D], ht[u][:, kc, j * P:(j + 1) * P],
                                                        w_out[:, kc, :], start=kc == 0, stop=kc == KC - 1)
                        last.then_inc(product_ready, 1)

                over_tiles(pe, plan, 2, step)


INPUTS = ["x", "src", "dst"] + ["L0_gnn_" + k for k in ("w1", "b1", "gamma", "beta", "w2", "b2", "w_gcn", "b_gcn")] + \
    ["L1_gnn_" + k for k in ("Wq", "bq", "Wk", "bk", "Wv", "bv", "Wo", "bo")]


def kernel(**inputs):
    import numpy as np
    from concourse import bacc
    from concourse.bass_utils import run_bass_kernel_spmd

    nc = bacc.Bacc("TRN2", target_bir_lowering=False, num_devices=1)
    arrays, args = {}, []
    for name in INPUTS:
        a = np.ascontiguousarray(inputs[name])
        arrays[f"in_{name}"] = a
        args.append(nc.dram_tensor(f"in_{name}", a.shape, mybir.dt.from_np(a.dtype), kind="ExternalInput").ap())
    out = nc.dram_tensor("out", list(arrays["in_x"].shape), F32, kind="ExternalOutput").ap()
    build(nc, *args, out)
    return run_bass_kernel_spmd(nc, [arrays], core_ids=[0]).results[0]["out"]
```

```python
from contextlib import ExitStack

import concourse.bass as bass
from concourse import mybir

F32 = mybir.dt.float32
BF16 = mybir.dt.bfloat16
F16 = mybir.dt.float16
I32 = mybir.dt.int32
ALU = mybir.AluOpType
ACT = mybir.ActivationFunctionType
AX = mybir.AxisListType

P = 128
D = 256
KC = D // P
H = 8
DH = D // H
ROWS = 4
TILE = P * ROWS
SLOTS = 8
GROUPS = 4
SCALE = float(DH) ** -0.5
LOW = -1.0e30
EPS = 1e-5
HIST = 6
W = ROWS * D
PEAKS, SUMS, WEIGHTS = 0, H, H + D
WIDE = D + 2 * H


class Plan:

    def __init__(self, n, e):
        self.n, self.e = n, e
        self.tiles = -(-n // TILE)
        self.tiles += self.tiles % 2
        self.last = n - (self.tiles - 1) * TILE
        assert 0 < self.last < TILE and self.last % ROWS == 0 and self.last + P <= TILE
        self.last_p = self.last // ROWS
        self.table = self.tiles * TILE
        self.per_part = -(-e // P)
        self.cols = self.tiles * HIST
        assert self.per_part <= self.cols
        self.full_parts = e // self.per_part
        self.rest = e - self.full_parts * self.per_part
        self.packed = self.cols + 8


def row_block(table, tile):
    return table[bass.ds(tile * TILE, TILE), :].rearrange("(p r) d -> p (r d)", p=P)


def over_tiles(eng, plan, lag, step):
    pairs = plan.tiles // 2

    def pair(i, fixed):
        for u in range(2):
            def at(l):
                back, slot = divmod(u - l, 2)
                if fixed and not 0 <= 2 * (i + back) + slot < plan.tiles:
                    return None
                return i + back, slot

            step(at)

    head = (lag + 2) // 2
    for i in range(head):
        pair(i, True)
    with eng.Fori(head, pairs - 1) as i:
        pair(i, False)
    for i in range(pairs - 1, (plan.tiles - 1 + lag) // 2 + 1):
        pair(i, True)


def over_columns(eng, turns, lag, step):
    assert lag < SLOTS

    def turn(i, first, after):
        for k in range(SLOTS if not after else lag):
            def at(l):
                back, slot = divmod(k - l, SLOTS)
                if (first and back < 0) or (after and back == 0):
                    return None
                return i + back, slot

            step(at)

    turn(0, True, False)
    with eng.Fori(1, turns) as i:
        turn(i, False, False)
    turn(turns, False, True)


def row_moments(v, dve, hold, x, stats, moments, stats_ready, moments_ready, i):
    for j in range(ROWS):
        last = v.bn_stats(stats[:, j, :], x[:, j, :])
    last.then_inc(stats_ready, 1)
    hold(dve, stats_ready, i + 1)
    for j in range(ROWS):
        last = v.bn_aggr(moments[:, j, :], stats[:, j, :])
    last.then_inc(moments_ready, 1)


def row_scales(v, dve, moments, std, rstd, shift, std_ready, rstd_ready, shift_ready, i):
    dve.wait_ge(std_ready, i + 1)
    v.reciprocal(rstd[:, :], std[:, :]).then_inc(rstd_ready, 1)
    dve.wait_ge(rstd_ready, i + 1)
    v.scalar_tensor_tensor(shift[:, :], moments[:, :, 0], -1.0, rstd[:, :], ALU.mult, ALU.mult).then_inc(shift_ready, 1)


def build(nc, x, src, dst, w1, b1, gamma, beta, w2, b2, w_gcn, b_gcn,
          wq, bq, wk, bk, wv, bv, wo, bo, out):
    plan = Plan(x.shape[0], src.shape[0])
    NT, TAB, COLS, PACKED = plan.tiles, plan.table, plan.cols, plan.packed

    def dram(name, shape, dt=F32):
        return nc.dram_tensor(name, shape, dt, kind="Internal").ap()

    h1_table = dram("h1_table", [NT * P, KC * TILE])
    y_table = dram("y_table", [TAB, D])
    agg_table = dram("agg_table", [TAB + 2 * P, D])
    x1_table = dram("x1_table", [TAB, D])
    q_table = dram("q_table", [TAB, D])
    kv_table = dram("kv_table", [TAB, 2 * D])
    acc_table = dram("acc_table", [TAB + 2 * P, WIDE])

    with ExitStack() as ctx:
        def sb(name, shape, dt=F32, where=ctx):
            return where.enter_context(nc.sbuf_tensor(name, shape, dt))

        in_use = []

        def sem(name):
            in_use.append(nc.alloc_semaphore(name))
            return in_use[-1]

        def pool_dma_sem(name):
            return nc.alloc_semaphore(name)

        def end_part():
            with nc.Block() as block:
                @block.sync
                def _(sp):
                    for s in in_use:
                        sp.sem_clear(s)
            for s in in_use:
                nc.release_semaphore(s)
            in_use.clear()

        ident = sb("ident", [P, P])
        ident_b = sb("ident_b", [P, P], BF16)
        earlier = sb("earlier", [P, P])
        spare = sb("spare", [P, 3])
        lane = sb("lane", [P, max(P, NT * ROWS)], F16)
        w1_t = sb("w1_t", [P, KC, D])
        w_mix = sb("w_mix", [P, KC, D])
        b_mix = sb("b_mix", [P, D])
        w_qkv = sb("w_qkv", [P, KC, 3 * D])
        b_qkv = sb("b_qkv", [P, 3 * D])
        w_out = sb("w_out", [P, KC, D])
        b_out = sb("b_out", [P, D])
        b_agg = sb("b_agg", [P, D])
        eps_col = sb("eps_col", [P, 1])
        bn_in = sb("bn_in", [P, 3, KC])
        dst_lo = sb("dst_lo", [P, COLS])
        dst_hi = sb("dst_hi", [P, COLS])
        is_self = sb("is_self", [P, COLS])
        packed_i = sb("packed_i", [P, 2, GROUPS, PACKED], I32)
        packed_f = sb("packed_f", [P, 2, GROUPS, PACKED])
        more_turns = sb("more_turns", [P, 1], I32)
        dinv = sb("dinv", [P, NT * ROWS])
        n_self = sb("n_self", [P, NT * ROWS])
        held = nc.alloc_semaphore("held")

        def hold(eng, s, value):
            eng.wait_ge(s, value)
            if not isinstance(value, int):
                eng.sem_inc(held, 1)

        with ExitStack() as part:
            w1_n = sb("w1_n", [P, KC, D], where=part)
            w2_n = sb("w2_n", [P, KC, D], where=part)
            wg_n = sb("wg_n", [P, KC, D], where=part)
            wg_t = sb("wg_t", [P, KC, D], where=part)
            b2_c = sb("b2_c", [P, KC], where=part)
            edges = sb("edges", [P, 2, COLS], I32, where=part)
            work_i = sb("work_i", [P, 2, COLS], I32, where=part)
            place = sb("place", [P, COLS], I32, where=part)
            edges_f = sb("edges_f", [P, 2, COLS], where=part)
            odd = sb("odd", [P, 2, 2, COLS], where=part)
            apart = sb("apart", [P, COLS], where=part)
            member = sb("member", [P, COLS], where=part)
            stock = sb("stock", [P, 2, COLS], where=part)
            best = sb("best", [P, 2, 8], where=part)
            counts = sb("counts", [P, GROUPS], where=part)
            most = sb("most", [P, GROUPS], where=part)
            most_i = sb("most_i", [P, GROUPS], I32, where=part)
            longest = sb("longest", [P, 1], where=part)
            empty = sb("empty", [P, 2 * GROUPS * PACKED], where=part)
            ps = [part.enter_context(nc.psum_tensor(f"prep_ps{i}", [P, 512], F32)) for i in range(4)]
            loaded = sem("prep_loaded")
            pads_ready = sem("pads_ready")
            edges_loaded = sem("edges_loaded")
            const_ready = sem("const_ready")
            turned = sem("weights_turned")
            copied = sem("weights_copied")
            mixed = sem("weights_mixed")
            chain = sem("prep_chain")
            counted = sem("edges_counted")
            most_ready = sem("most_ready")
            best_ready = [sem(f"best_ready{g}") for g in range(GROUPS)]
            replaced = [sem(f"best_replaced{g}") for g in range(GROUPS)]
            vchain = sem("prep_vector_chain")
            n_loads = 16

            with nc.Block() as block:
                @block.sync
                def _(sp):
                    def halves(w):
                        return w.rearrange("(c p) n -> p c n", p=P)

                    def column(v):
                        return v.rearrange("(c p) -> p c", p=P)

                    n = 0
                    pairs = [(w1_n[:, :, :], halves(w1)), (w2_n[:, :, :], halves(w2)), (wg_n[:, :, :], halves(w_gcn)),
                             (w_out[:, :, :], halves(wo)), (b_out[:, :], bo.partition_broadcast(P)),
                             (b_agg[:, :], b_gcn.partition_broadcast(P))]
                    for i, (w, b) in enumerate(((wq, bq), (wk, bk), (wv, bv))):
                        pairs.append((w_qkv[:, :, i * D:(i + 1) * D], halves(w)))
                        pairs.append((b_qkv[:, i * D:(i + 1) * D], b.partition_broadcast(P)))
                    with nc.allow_non_contiguous_dma(reason="a few hundred words, once"):
                        for i, v in enumerate((b1, gamma, beta)):
                            pairs.append((bn_in[:, i, :], column(v)))
                        pairs.append((b2_c[:, :], column(b2)))
                        assert len(pairs) == n_loads
                        sp.wait_ge(pads_ready, 1)
                        full, per, rest = plan.full_parts, plan.per_part, plan.rest
                        for i, e in enumerate((src, dst)):
                            lo = full // 16 * 16
                            for a, b in ((0, lo), (lo, full)):
                                if a < b:
                                    sp.dma_start(edges[a:b, i, 0:per], e[a * per:b * per].rearrange("(p c) -> p c", c=per)).then_inc(edges_loaded, 16)
                                    n += 1
                            if rest:
                                sp.dma_start(edges[full:full + 1, i, 0:rest], e[full * per:plan.e].rearrange("(p c) -> p c", p=1)).then_inc(edges_loaded, 16)
                                n += 1
                        plan.edge_loads = n
                        for o, i in pairs:
                            sp.dma_start(o, i).then_inc(loaded, 16)
                        sp.wait_ge(loaded, 16 * n_loads)
                        sp.wait_ge(edges_loaded, 16 * n)

                @block.gpsimd
                def _(pool):
                    pool.iota(edges[:, :, :], [[0, 2 * COLS]], base=plan.n, channel_multiplier=1).then_inc(pads_ready, 1)
                    pool.iota(place[:, :], [[1, COLS]], base=0, channel_multiplier=0).then_inc(const_ready, 1)
                    for i, base in enumerate((plan.n, TAB, TAB + P)):
                        pool.iota(spare[:, i:i + 1], [[0, 1]], base=base, channel_multiplier=1,
                                  allow_small_or_imprecise_dtypes=True).then_inc(const_ready, 1)
                    pool.iota(lane[:, :], [[1, max(P, NT * ROWS)]], base=0, channel_multiplier=0,
                              allow_small_or_imprecise_dtypes=True).then_inc(const_ready, 1)
                    pool.memset(eps_col[:, :], EPS).then_inc(const_ready, 1)
                    pool.memset(ident[:, :], 0.0).then_inc(chain, 1)
                    pool.memset(ident_b[:, :], 0.0).then_inc(chain, 1)
                    pool.memset(earlier[:, :], 0.0).then_inc(chain, 1)
                    pool.memset(packed_i[:, :, :, :], 0).then_inc(const_ready, 1)
                    pool.wait_ge(chain, 3)
                    for m in (ident, ident_b):
                        pool.affine_select(out=m[:, :], in_=m[:, :], compare_op=ALU.not_equal, fill=1.0, base=0,
                                           pattern=[[-1, P]], channel_multiplier=1).then_inc(const_ready, 1)
                    pool.affine_select(out=earlier[:, :], in_=earlier[:, :], compare_op=ALU.is_ge, fill=1.0, base=0,
                                       pattern=[[1, P]], channel_multiplier=-1).then_inc(const_ready, 1)
                    pool.wait_ge(counted, GROUPS)
                    pool.partition_all_reduce(most[:, :], counts[:, :], P, bass.bass_isa.ReduceOp.max).then_inc(most_ready, 1)

                @block.tensor
                def _(pe):
                    pe.wait_ge(loaded, 16 * n_loads)
                    pe.wait_ge(const_ready, 10)
                    for b, w in enumerate((w1_n, wg_n)):
                        for kc in range(KC):
                            for oc in range(KC):
                                last = nc.tensor.transpose(ps[b][:, kc * D + oc * P:kc * D + oc * P + P],
                                                           w[:, oc, kc * P:(kc + 1) * P], ident[:, :])
                        last.then_inc(turned, 1)
                    pe.wait_ge(copied, 2)
                    for kc in range(KC):
                        for jc in range(KC):
                            nc.tensor.matmul(ps[2][:, kc * D:(kc + 1) * D], w2_n[:, jc, kc * P:(kc + 1) * P],
                                             wg_t[:, jc, :], start=jc == 0, stop=jc == KC - 1)
                    for jc in range(KC):
                        last = nc.tensor.matmul(ps[3][:, 0:D], b2_c[:, jc:jc + 1].to_broadcast([P, P]), wg_t[:, jc, :],
                                                start=jc == 0, stop=jc == KC - 1)
                    last.then_inc(mixed, 1)

                @block.scalar
                def _(act):
                    for b, w in enumerate((w1_t, wg_t)):
                        act.wait_ge(turned, b + 1)
                        nc.scalar.activation(w[:, :, :].rearrange("p a b -> p (a b)"), ps[b][:, :], ACT.Copy).then_inc(copied, 1)
                    act.wait_ge(mixed, 1)
                    nc.scalar.activation(w_mix[:, :, :].rearrange("p a b -> p (a b)"), ps[2][:, :], ACT.Copy)
                    nc.scalar.activation(b_mix[:, :], ps[3][:, 0:D], ACT.Copy)

                @block.vector
                def _(dve):
                    done = [0]

                    def link(ins):
                        done[0] += 1
                        ins.then_inc(vchain, 1)
                        dve.wait_ge(vchain, done[0])

                    v = nc.vector
                    dve.wait_ge(edges_loaded, 16 * plan.edge_loads)
                    dve.wait_ge(const_ready, 10)
                    v.tensor_scalar(work_i[:, 0, :], edges[:, 1, :], 2, P - 1, ALU.logical_shift_right, ALU.bitwise_and)
                    link(v.tensor_scalar(work_i[:, 1, :], edges[:, 1, :], 9, 2, ALU.logical_shift_right, ALU.logical_shift_left))
                    link(v.tensor_copy(dst_lo[:, :], work_i[:, 0, :]))
                    v.tensor_copy(dst_hi[:, :], work_i[:, 1, :])
                    link(v.tensor_copy(edges_f[:, :, :], edges[:, :, :]))
                    link(v.tensor_scalar(work_i[:, 0, :], edges[:, 1, :], ROWS - 1, None, ALU.bitwise_and))
                    link(v.tensor_copy(member[:, :], work_i[:, 0, :]))
                    v.tensor_tensor(dst_hi[:, :], dst_hi[:, :], member[:, :], ALU.add)
                    v.tensor_tensor(is_self[:, :], edges_f[:, 0, :], edges_f[:, 1, :], ALU.is_equal)
                    link(v.tensor_tensor(apart[:, :], edges_f[:, 0, :], edges_f[:, 1, :], ALU.not_equal))
                    link(v.tensor_scalar(work_i[:, :, :], edges[:, :, :], 1, None, ALU.bitwise_and))
                    link(v.tensor_copy(odd[:, :, 1, :], work_i[:, :, :]))
                    link(v.tensor_scalar(odd[:, :, 0, :], odd[:, :, 1, :], -1.0, 1.0, ALU.mult, ALU.add))
                    link(v.tensor_scalar(place[:, :], place[:, :], 16, 0x40000000, ALU.logical_shift_left, ALU.bitwise_or))
                    for i in range(2):
                        link(v.tensor_tensor(edges[:, i, :], edges[:, i, :], place[:, :], ALU.bitwise_or))
                    for g in range(GROUPS):
                        link(v.tensor_tensor(member[:, :], apart[:, :], odd[:, 0, g & 1, :], ALU.mult))
                        link(v.tensor_tensor(member[:, :], member[:, :], odd[:, 1, g >> 1, :], ALU.mult))
                        v.reduce_sum(counts[:, g:g + 1], member[:, :], axis=AX.X).then_inc(counted, 1)
                        dve.wait_ge(counted, g + 1)
                    dve.wait_ge(most_ready, 1)
                    link(v.tensor_scalar(most[:, :], most[:, :], 1.0, None, ALU.max))
                    link(v.tensor_copy(most_i[:, :], most[:, :]))
                    link(v.reduce_max(longest[:, :], most[:, :], axis=AX.X))
                    link(v.tensor_scalar(longest[:, :], longest[:, :], 4.0, -3.0, ALU.max, ALU.add))
                    link(v.tensor_copy(more_turns[:, :], longest[:, :]))
                    link(v.tensor_scalar(more_turns[:, :], more_turns[:, :], 1, None, ALU.logical_shift_right))
                    for g in range(GROUPS):
                        link(v.tensor_tensor(member[:, :], apart[:, :], odd[:, 0, g & 1, :], ALU.mult))
                        link(v.tensor_tensor(member[:, :], member[:, :], odd[:, 1, g >> 1, :], ALU.mult))
                        for i in range(2):
                            link(v.tensor_tensor(stock[:, i, :], edges[:, i, :].bitcast(F32), member[:, :], ALU.mult))
                        length = dve.value_load(most_i[0:1, g:g + 1], min_val=1, max_val=COLS)
                        with dve.Fori(0, length, 8) as c:
                            for i in range(2):
                                v.max(out=best[:, i, :], in_=stock[:, i, :]).then_inc(best_ready[g], 1)
                            hold(dve, best_ready[g], c // 8 * 2 + 2)
                            for i in range(2):
                                v.tensor_copy(packed_i[:, i, g, bass.ds(c, 8)], best[:, i, :].bitcast(I32))
                                v.match_replace(out=stock[:, i, :], in_to_replace=best[:, i, :], in_values=stock[:, i, :],
                                                imm_value=0.0).then_inc(replaced[g], 1)
                            hold(dve, replaced[g], c // 8 * 2 + 2)
                    pi = packed_i[:, :, :, :].rearrange("p a g c -> p (a g c)")
                    pf = packed_f[:, :, :, :].rearrange("p a g c -> p (a g c)")
                    link(v.tensor_copy(pf, pi))
                    link(v.tensor_scalar(empty[:, :], pf, 0.0, None, ALU.is_equal))
                    link(v.tensor_scalar(pi, pi, 0xFFFF, None, ALU.bitwise_and))
                    link(v.tensor_copy(pf, pi))
                    link(v.scalar_tensor_tensor(pi, empty[:, :], spare[:, 0:1], pf, ALU.mult, ALU.add))
                    for i in range(2):
                        for g in range(GROUPS):
                            at = (i * GROUPS + g) * PACKED
                            parity = g >> i & 1
                            v.scalar_tensor_tensor(packed_f[:, i, g, :], empty[:, at:at + PACKED], spare[:, 1 + parity:2 + parity],
                                                   packed_f[:, i, g, :], ALU.mult, ALU.add)

        end_part()

        with ExitStack() as part:
            two = range(2)
            xb = [sb(f"a_x{u}", [P, ROWS, D], where=part) for u in two]
            stats = [sb(f"a_stats{u}", [P, ROWS, 6], where=part) for u in two]
            moments = [sb(f"a_moments{u}", [P, ROWS, 2], where=part) for u in two]
            std = [sb(f"a_std{u}", [P, ROWS], where=part) for u in two]
            rstd = [sb(f"a_rstd{u}", [P, ROWS], where=part) for u in two]
            shift = [sb(f"a_shift{u}", [P, ROWS], where=part) for u in two]
            hn = [sb(f"a_hn{u}", [P, ROWS, D], where=part) for u in two]
            ht = [sb(f"a_ht{u}", [P, KC, TILE], where=part) for u in two]
            h1 = [sb(f"h1_{u}", [P, KC, TILE], where=part) for u in two]
            zero = sb("zero", [P, 2 * WIDE], where=part)
            third = HIST // 2
            hot_hi = [sb(f"hot_hi{w}", [P, third, NT * ROWS], F16, where=part) for w in two]
            hot_lo = [sb(f"hot_lo{w}", [P, third, 2, P], F16, where=part) for w in two]
            bn_stats = sb("bn_stats", [P, KC, NT * 6], where=part)
            bn_moments = sb("bn_moments", [P, KC, 2], where=part)
            bn_scale = sb("bn_scale", [P, KC], where=part)
            bn_shift = sb("bn_shift", [P, KC], where=part)
            x_loaded = [sem(f"a_x_loaded{u}") for u in two]
            stats_ready = [sem(f"a_stats_ready{u}") for u in two]
            moments_ready = [sem(f"a_moments_ready{u}") for u in two]
            std_ready = [sem(f"a_std_ready{u}") for u in two]
            rstd_ready = [sem(f"a_rstd_ready{u}") for u in two]
            shift_ready = [sem(f"a_shift_ready{u}") for u in two]
            hn_ready = [sem(f"a_hn_ready{u}") for u in two]
            turned = [sem(f"a_turned{u}") for u in two]
            ht_by_dve = [sem(f"a_ht_by_dve{u}") for u in two]
            ht_by_act = [sem(f"a_ht_by_act{u}") for u in two]
            product_ready = [sem(f"a_product_ready{u}") for u in two]
            h1_ready = [sem(f"a_h1_ready{u}") for u in two]
            h1_counted = [sem(f"a_h1_counted{u}") for u in two]
            h1_stored = [pool_dma_sem(f"a_h1_stored{u}") for u in two]
            hot_ready = [sem(f"hot_ready{w}") for w in two]
            hot_used = [sem(f"hot_used{w}") for w in two]
            zeroed = pool_dma_sem("acc_zeroed")
            zero_ready = sem("zero_ready")
            hist_ps = [part.enter_context(nc.psum_tensor(f"hist_ps{i}", [P, NT * ROWS], F32)) for i in two]

            with ExitStack() as inner, nc.Block() as block:
                turn_ps = [inner.enter_context(nc.psum_tensor(f"a_turn_ps{u}", [P, KC * TILE], F32)) for u in two]
                h1_ps = inner.enter_context(nc.psum_tensor("a_h1_ps", [P, KC * TILE], F32))

                @block.sync
                def _(sp):
                    def step(at):
                        if (here := at(0)) is None:
                            return
                        i, u = here
                        tile = i * 2 + u
                        sp.wait_ge(hn_ready[u], i)
                        if isinstance(tile, int) and tile == NT - 1:
                            rows = x[tile * TILE:plan.n, :].rearrange("(p r) d -> p (r d)", r=ROWS)
                            sp.dma_start(xb[u][0:plan.last_p, :, :].rearrange("p r d -> p (r d)"), rows).then_inc(x_loaded[u], 16)
                        else:
                            sp.dma_start(xb[u][:, :, :].rearrange("p r d -> p (r d)"), row_block(x, tile)).then_inc(x_loaded[u], 16)

                    over_tiles(sp, plan, 0, step)

                @block.gpsimd
                def _(pool):
                    pool.memset(zero[:, :], 0.0).then_inc(zero_ready, 1)
                    pool.wait_ge(zero_ready, 1)

                    def step(at):
                        if at(1) is None:
                            return
                        i, u = at(1)
                        tile = i * 2 + u
                        hold(pool, h1_ready[u], i + 1)
                        pool.dma_start(h1_table[bass.ds(tile * P, P), :], h1[u][:, :, :].rearrange("p k c -> p (k c)")).then_inc(h1_stored[u], 16)

                    over_tiles(pool, plan, 1, step)
                    for u in two:
                        pool.wait_ge(h1_stored[u], 16 * (NT // 2))
                    for table, width in ((acc_table, WIDE), (agg_table, D)):
                        pool.dma_start(table[TAB:TAB + 2 * P, :].rearrange("(p r) d -> p (r d)", p=P), zero[:, 0:2 * width]).then_inc(zeroed, 16)
                    pool.wait_ge(zeroed, 32)

                @block.scalar
                def _(act):
                    def step(at):
                        if at(0) is not None:
                            i, u = at(0)
                            act.wait_ge(moments_ready[u], i + 1)
                            act.wait_ge(shift_ready[u], i)
                            nc.scalar.activation(std[u][:, :], moments[u][:, :, 1], ACT.Sqrt, bias=eps_col[:, 0:1]).then_inc(std_ready[u], 1)
                            act.wait_ge(shift_ready[u], i + 1)
                            act.wait_ge(turned[u], i)
                            for j in range(ROWS):
                                last = nc.scalar.activation(hn[u][:, j, :], xb[u][:, j, :], ACT.Relu,
                                                            bias=shift[u][:, j:j + 1], scale=rstd[u][:, j:j + 1])
                            last.then_inc(hn_ready[u], 1)
                        if at(2) is not None:
                            i, u = at(2)
                            act.wait_ge(product_ready[u], i + 1)
                            act.wait_ge(h1_stored[u], 16 * i)
                            act.wait_ge(h1_counted[u], i)
                            for oc in range(KC):
                                last = nc.scalar.activation(h1[u][:, oc, :], h1_ps[:, oc * TILE:(oc + 1) * TILE],
                                                            ACT.Identity, bias=bn_in[:, 0, oc:oc + 1])
                            last.then_inc(h1_ready[u], 1)
                        if at(1) is not None:
                            i, u = at(1)
                            act.wait_ge(turned[u], i + 1)
                            act.wait_ge(product_ready[u], i)
                            nc.scalar.activation(ht[u][:, 1, :], turn_ps[u][:, TILE:2 * TILE], ACT.Copy).then_inc(ht_by_act[u], 1)

                    over_tiles(act, plan, 2, step)

                @block.tensor
                def _(pe):
                    def step(at):
                        if at(0) is not None:
                            i, u = at(0)
                            tile = i * 2 + u
                            fixed = isinstance(tile, int)
                            pe.wait_ge(hn_ready[u], i + 1)
                            pe.wait_ge(ht_by_dve[u], i)
                            pe.wait_ge(ht_by_act[u], i)
                            for kc in range(KC):
                                for j in range(ROWS):
                                    last = nc.tensor.transpose(turn_ps[u][:, kc * TILE + j * P:kc * TILE + (j + 1) * P],
                                                               hn[u][:, j, kc * P:(kc + 1) * P], ident[:, :])
                            last.then_inc(turned[u], 1)
                            for w in two:
                                pe.wait_ge(hot_ready[w], tile + 1)
                                for c in range(third):
                                    first = fixed and tile == 0 and w == 0 and c == 0
                                    end = fixed and tile == NT - 1 and w == 1 and c == third - 1
                                    for b in two:
                                        last = nc.tensor.matmul(hist_ps[b][:, :], hot_lo[w][:, c, b, :], hot_hi[w][:, c, :],
                                                                start=first, stop=end)
                                last.then_inc(hot_used[w], 1)
                        if at(1) is not None:
                            i, u = at(1)
                            pe.wait_ge(ht_by_dve[u], i + 1)
                            pe.wait_ge(ht_by_act[u], i + 1)
                            pe.wait_ge(h1_ready[1 - u], i + u)
                            for oc in range(KC):
                                for kc in range(KC):
                                    last = nc.tensor.matmul(h1_ps[:, oc * TILE:(oc + 1) * TILE], w1_t[:, kc, oc * P:(oc + 1) * P],
                                                            ht[u][:, kc, :], start=kc == 0, stop=kc == KC - 1)
                            last.then_inc(product_ready[u], 1)

                    over_tiles(pe, plan, 1, step)

                @block.vector
                def _(dve):
                    v = nc.vector

                    def one_hots(tile, w):
                        hold(dve, hot_used[w], tile)
                        for c in range(third):
                            col = bass.ds(tile * HIST + (w * third + c), 1)
                            v.tensor_scalar(hot_hi[w][:, c, :], lane[:, 0:NT * ROWS], dst_hi[:, col], None, ALU.is_equal)
                            v.tensor_scalar(hot_lo[w][:, c, 0, :], lane[:, 0:P], dst_lo[:, col], None, ALU.is_equal)
                            last = v.tensor_scalar(hot_lo[w][:, c, 1, :], lane[:, 0:P], dst_lo[:, col], is_self[:, col],
                                                   ALU.is_equal, ALU.mult)
                        last.then_inc(hot_ready[w], 1)

                    def step(at):
                        if at(0) is not None:
                            i, u = at(0)
                            tile = i * 2 + u
                            dve.wait_ge(x_loaded[u], 16 * i + 16)
                            dve.wait_ge(hn_ready[u], i)
                            row_moments(v, dve, hold, xb[u], stats[u], moments[u], stats_ready[u], moments_ready[u], i)
                            one_hots(tile, 0)
                            row_scales(v, dve, moments[u], std[u], rstd[u], shift[u],
                                       std_ready[u], rstd_ready[u], shift_ready[u], i)
                        if at(1) is not None:
                            i, u = at(1)
                            dve.wait_ge(turned[u], i + 1)
                            dve.wait_ge(product_ready[u], i)
                            v.tensor_copy(ht[u][:, 0, :], turn_ps[u][:, 0:TILE]).then_inc(ht_by_dve[u], 1)
                        if at(0) is not None:
                            one_hots(tile, 1)
                        if at(2) is not None:
                            i, u = at(2)
                            t2 = i * 2 + u
                            hold(dve, h1_ready[u], i + 1)
                            for oc in range(KC):
                                seen = h1[u][:, oc, :]
                                if isinstance(t2, int) and t2 == NT - 1:
                                    seen = seen.rearrange("p (j q) -> p j q", j=ROWS)[:, :, 0:plan.last_p]
                                last = v.bn_stats(bn_stats[:, oc, bass.ds(t2 * 6, 6)], seen)
                            last.then_inc(h1_counted[u], 1)

                    over_tiles(dve, plan, 2, step)

            hb = [sb(f"hb{u}", [P, KC, TILE], where=part) for u in two]
            mix = [sb(f"mix{u}", [P, ROWS, D], where=part) for u in two]
            y_out = [sb(f"y_out{u}", [P, ROWS, D], where=part) for u in two]
            agg_out = [sb(f"agg_out{u}", [P, ROWS, D], where=part) for u in two]
            self_weight = sb("self_weight", [P, NT * ROWS], where=part)
            h1_loaded = [sem(f"b_h1_loaded{u}") for u in two]
            hb_ready = [sem(f"hb_ready{u}") for u in two]
            mix_product = [sem(f"mix_product{u}") for u in two]
            mix_ready = [sem(f"mix_ready{u}") for u in two]
            y_ready = [sem(f"y_ready{u}") for u in two]
            agg_ready = [sem(f"agg_ready{u}") for u in two]
            y_stored = [pool_dma_sem(f"y_stored{u}") for u in two]
            agg_stored = [pool_dma_sem(f"agg_stored{u}") for u in two]
            bn_ready = sem("bn_ready")
            b_chain = sem("b_chain")
            roots_ready = sem("roots_ready")

            with ExitStack() as inner, nc.Block() as block:
                mix_ps = [inner.enter_context(nc.psum_tensor(f"mix_ps{u}", [P, ROWS * D], F32)) for u in two]

                @block.sync
                def _(sp):
                    def step(at):
                        i, u = at(0)
                        sp.wait_ge(hb_ready[u], i)
                        sp.dma_start(h1[u][:, :, :].rearrange("p k c -> p (k c)"),
                                     h1_table[bass.ds((i * 2 + u) * P, P), :]).then_inc(h1_loaded[u], 16)

                    over_tiles(sp, plan, 0, step)

                @block.scalar
                def _(act):
                    act.wait_ge(b_chain, 4)
                    nc.scalar.activation(dinv[:, :], dinv[:, :], ACT.Sqrt).then_inc(roots_ready, 1)
                    nc.scalar.activation(bn_scale[:, :], bn_moments[:, :, 1], ACT.Sqrt, bias=eps_col[:, 0:1]).then_inc(roots_ready, 1)
                    act.wait_ge(bn_ready, 1)

                    def step(at):
                        if at(0) is not None:
                            i, u = at(0)
                            act.wait_ge(h1_loaded[u], 16 * i + 16)
                            act.wait_ge(mix_product[u], i)
                            for kc in range(KC):
                                last = nc.scalar.activation(hb[u][:, kc, :], h1[u][:, kc, :], ACT.Relu,
                                                            bias=bn_shift[:, kc:kc + 1], scale=bn_scale[:, kc:kc + 1])
                            last.then_inc(hb_ready[u], 1)
                        if at(2) is not None:
                            i, u = at(2)
                            tile = i * 2 + u
                            hold(act, mix_ready[u], i + 1)
                            hold(act, agg_stored[u], 16 * i)
                            for j in range(ROWS):
                                last = nc.scalar.activation(agg_out[u][:, j, :], mix[u][:, j, :], ACT.Copy,
                                                            scale=self_weight[:, bass.ds(tile * ROWS + j, 1)])
                            last.then_inc(agg_ready[u], 1)

                    over_tiles(act, plan, 2, step)

                @block.tensor
                def _(pe):
                    def step(at):
                        i, u = at(0)
                        pe.wait_ge(hb_ready[u], i + 1)
                        pe.wait_ge(mix_ready[u], i)
                        for j in range(ROWS):
                            for kc in range(KC):
                                last = nc.tensor.matmul(mix_ps[u][:, j * D:(j + 1) * D], hb[u][:, kc, j * P:(j + 1) * P],
                                                        w_mix[:, kc, :], start=kc == 0, stop=kc == KC - 1)
                        last.then_inc(mix_product[u], 1)

                    over_tiles(pe, plan, 0, step)

                @block.vector
                def _(dve):
                    v = nc.vector
                    v.tensor_scalar(dinv[:, :], hist_ps[0][:, :], 1.0, None, ALU.add).then_inc(b_chain, 1)
                    v.tensor_copy(n_self[:, :], hist_ps[1][:, :]).then_inc(b_chain, 1)
                    for oc in range(KC):
                        v.bn_aggr(bn_moments[:, oc, :], bn_stats[:, oc, :]).then_inc(b_chain, 1)
                    dve.wait_ge(roots_ready, 2)
                    v.reciprocal(dinv[:, :], dinv[:, :]).then_inc(b_chain, 1)
                    v.reciprocal(bn_scale[:, :], bn_scale[:, :]).then_inc(b_chain, 1)
                    dve.wait_ge(b_chain, 6)
                    v.scalar_tensor_tensor(self_weight[:, :], n_self[:, :], 1.0, dinv[:, :], ALU.add, ALU.mult)
                    v.tensor_tensor(bn_scale[:, :], bn_scale[:, :], bn_in[:, 1, :], ALU.mult).then_inc(b_chain, 1)
                    dve.wait_ge(b_chain, 7)
                    v.scalar_tensor_tensor(bn_shift[:, :], bn_moments[:, :, 0], -1.0, bn_scale[:, :], ALU.mult, ALU.mult).then_inc(b_chain, 1)
                    dve.wait_ge(b_chain, 8)
                    v.tensor_tensor(bn_shift[:, :], bn_shift[:, :], bn_in[:, 2, :], ALU.add).then_inc(bn_ready, 1)

                    def step(at):
                        i, u = at(0)
                        tile = i * 2 + u
                        dve.wait_ge(mix_product[u], i + 1)
                        dve.wait_ge(agg_ready[u], i)
                        v.tensor_tensor(mix[u][:, :, :], mix_ps[u][:, :].rearrange("p (j d) -> p j d", j=ROWS),
                                        b_mix[:, :].unsqueeze(1).to_broadcast([P, ROWS, D]), ALU.add).then_inc(mix_ready[u], 1)
                        dve.wait_ge(mix_ready[u], i + 1)
                        dve.wait_ge(y_stored[u], 16 * i)
                        for j in range(ROWS):
                            last = v.tensor_scalar(y_out[u][:, j, :], mix[u][:, j, :],
                                                   dinv[:, bass.ds(tile * ROWS + j, 1)], None, ALU.mult)
                        last.then_inc(y_ready[u], 1)

                    over_tiles(dve, plan, 0, step)

                @block.gpsimd
                def _(pool):
                    def step(at):
                        i, u = at(0)
                        tile = i * 2 + u
                        for ready, rows, table, stored in ((y_ready, y_out, y_table, y_stored),
                                                           (agg_ready, agg_out, agg_table, agg_stored)):
                            hold(pool, ready[u], i + 1)
                            pool.dma_start(row_block(table, tile), rows[u][:, :, :].rearrange("p r d -> p (r d)")).then_inc(stored[u], 16)

                    over_tiles(pool, plan, 0, step)
                    for u in two:
                        pool.wait_ge(y_stored[u], 16 * (NT // 2))
                        pool.wait_ge(agg_stored[u], 16 * (NT // 2))

        end_part()

        eight = range(SLOTS)

        def column_parts(name, key, where):
            return {
                "key": key,
                "group": (lambda k: k & 3) if key == 0 else (lambda k: (k & 1) << 1 | k >> 1 & 1),
                "ends": [sb(f"{name}_ends{k}", [P, 2], I32, where) for k in eight],
                "keys": [sb(f"{name}_keys{k}", [P, 2], F32, where) for k in eight],
                "same": [sb(f"{name}_same{k}", [P, P], F32, where) for k in range(4)],
                "rank_of": sb(f"{name}_rank_of", [P, P], F32, where),
                "rank": [sb(f"{name}_rank{k}", [P, 1], F32, where) for k in eight],
                "offset": [sb(f"{name}_offset{k}", [P, 1], F32, where) for k in eight],
                "goal": [sb(f"{name}_goal{k}", [P, 1], I32, where) for k in eight],
                "across": [where.enter_context(nc.psum_tensor(f"{name}_across{k}", [P, 512], F32)) for k in range(2)],
                "staged": sem(f"{name}_staged"),
                "across_ready": sem(f"{name}_across_ready"),
                "ranked": sem(f"{name}_ranked"),
                "offset_ready": sem(f"{name}_offset_ready"),
                "goal_ready": sem(f"{name}_goal_ready"),
                "scattered": [pool_dma_sem(f"{name}_scattered{k}") for k in eight],
            }

        def number(column):
            i, k = column
            return i * SLOTS + (k + 1)

        def wait_past(eng, s, value):
            if not isinstance(value, int) or value > 0:
                eng.wait_ge(s, value)

        def load_turns(eng):
            return eng.value_load(more_turns[0:1, 0:1], min_val=0, max_val=PACKED // 2 - 2) + 2

        def stage_column(dve, c, column):
            i, k = column
            g = c["group"](k % GROUPS)
            at = bass.ds(i * 2 + k // GROUPS, 1)
            hold(dve, c["scattered"][k], i * 16)
            nc.vector.tensor_copy(c["ends"][k][:, :], packed_i[:, :, g, at].rearrange("p a o -> p (a o)"))
            nc.vector.tensor_copy(c["keys"][k][:, 0:1], packed_f[:, c["key"], g, at])
            nc.vector.tensor_scalar(c["keys"][k][:, 1:2], packed_f[:, c["key"], g, at], spare[:, 1 + k % 2:2 + k % 2], None,
                                    ALU.subtract).then_inc(c["staged"], 1)

        def keys_across(pe, c, column):
            i, k = column
            pe.wait_ge(c["staged"], number(column))
            wait_past(pe, c["ranked"], number(column) - 2)
            nc.tensor.matmul(c["across"][k % 2][:, 0:P], c["keys"][k][:, 0:1].to_broadcast([P, P]), ident[:, :],
                             start=True, stop=True).then_inc(c["across_ready"], 1)

        def find_goals(dve, c, column, write_same):
            i, k = column
            v = nc.vector
            n = number(column)
            across, keys = c["across"][k % 2][:, 0:P], c["keys"][k]
            dve.wait_ge(c["across_ready"], n)
            write_same(across, keys[:, 0:1], k)
            v.scalar_tensor_tensor(c["rank_of"][:, :], across, keys[:, 0:1], earlier[:, :], ALU.is_equal, ALU.mult,
                                   accum_out=c["rank"][k][:, 0:1]).then_inc(c["ranked"], 1)
            dve.wait_ge(c["ranked"], n)
            v.tensor_scalar(c["offset"][k][:, :], c["rank"][k][:, :], 0.0, keys[:, 1:2], ALU.is_equal,
                            ALU.mult).then_inc(c["offset_ready"], 1)
            dve.wait_ge(c["offset_ready"], n)
            v.tensor_scalar(c["goal"][k][:, :], c["offset"][k][:, :], spare[:, 1 + k % 2:2 + k % 2], None, ALU.add).then_inc(c["goal_ready"], 1)

        def gather(rows, table, index):
            return nc.gpsimd.indirect_dma_start(out=rows, out_offset=None, in_=table,
                                                in_offset=bass.IndirectOffsetOnAxis(ap=index, axis=0))

        def scatter(table, index, rows, **how):
            return nc.gpsimd.indirect_dma_start(out=table, out_offset=bass.IndirectOffsetOnAxis(ap=index, axis=0),
                                                in_=rows, in_offset=None, **how)

        with ExitStack() as part, nc.Block() as block:
            c = column_parts("gcn", 1, part)
            got = [sb(f"gcn_got{k}", [P, D], where=part) for k in eight]
            summed = [sb(f"gcn_summed{k}", [P, D], where=part) for k in eight]
            sum_ps = [part.enter_context(nc.psum_tensor(f"gcn_sum_ps{k}", [P, 512], F32)) for k in range(2)]
            gathered = [pool_dma_sem(f"gcn_gathered{k}") for k in eight]
            sum_ready = sem("gcn_sum_ready")
            summed_ready = sem("gcn_summed_ready")

            @block.gpsimd
            def _(pool):
                turns = load_turns(pool)

                def step(at):
                    if (col := at(0)) is not None:
                        i, k = col
                        hold(pool, c["staged"], number(col))
                        gather(got[k][:, :], y_table, c["ends"][k][:, 0:1]).then_inc(gathered[k], 16)
                    if (col := at(3)) is not None:
                        i, k = col
                        hold(pool, summed_ready, number(col))
                        if (two_back := at(5)) is not None:
                            hold(pool, c["scattered"][two_back[1]], two_back[0] * 16 + 16)
                        hold(pool, c["goal_ready"], number(col))
                        scatter(agg_table, c["goal"][k][:, 0:1], summed[k][:, :], compute_op=ALU.add).then_inc(c["scattered"][k], 16)

                over_columns(pool, turns, 3, step)
                for k in eight:
                    hold(pool, c["scattered"][k], turns * 16)

            @block.vector
            def _(dve):
                turns = load_turns(dve)

                def write_same(across, key, k):
                    nc.vector.tensor_scalar(c["same"][k % 4][:, :], across, key, None, ALU.is_equal)

                def step(at):
                    if (col := at(0)) is not None:
                        stage_column(dve, c, col)
                    if (col := at(1)) is not None:
                        wait_past(dve, sum_ready, number(col) - 4)
                        find_goals(dve, c, col, write_same)

                over_columns(dve, turns, 1, step)

            @block.tensor
            def _(pe):
                turns = load_turns(pe)

                def step(at):
                    if (col := at(0)) is not None:
                        keys_across(pe, c, col)
                    if (col := at(2)) is not None:
                        i, k = col
                        pe.wait_ge(c["ranked"], number(col))
                        pe.wait_ge(gathered[k], i * 16 + 16)
                        wait_past(pe, summed_ready, number(col) - 2)
                        nc.tensor.matmul(sum_ps[k % 2][:, 0:D], c["same"][k % 4][:, :], got[k][:, :],
                                         start=True, stop=True).then_inc(sum_ready, 1)

                over_columns(pe, turns, 2, step)

            @block.scalar
            def _(act):
                turns = load_turns(act)

                def step(at):
                    i, k = col = at(0)
                    act.wait_ge(sum_ready, number(col))
                    nc.scalar.activation(summed[k][:, :], sum_ps[k % 2][:, 0:D], ACT.Copy).then_inc(summed_ready, 1)

                over_columns(act, turns, 0, step)

        end_part()

        with ExitStack() as part, nc.Block() as block:
            agg = [sb(f"c_agg{u}", [P, ROWS, D], where=part) for u in two]
            xb = [sb(f"c_x{u}", [P, ROWS, D], where=part) for u in two]
            x1 = [sb(f"c_x1_{u}", [P, ROWS, D], where=part) for u in two]
            stats = [sb(f"c_stats{u}", [P, ROWS, 6], where=part) for u in two]
            moments = [sb(f"c_moments{u}", [P, ROWS, 2], where=part) for u in two]
            std = [sb(f"c_std{u}", [P, ROWS], where=part) for u in two]
            rstd = [sb(f"c_rstd{u}", [P, ROWS], where=part) for u in two]
            shift = [sb(f"c_shift{u}", [P, ROWS], where=part) for u in two]
            hn = [sb(f"c_hn{u}", [P, ROWS, D], where=part) for u in two]
            ht = [sb(f"c_ht{u}", [P, KC, TILE], where=part) for u in two]
            qb = [sb(f"c_q{u}", [P, ROWS, 1, D], where=part) for u in two]
            kv = [sb(f"c_kv{u}", [P, ROWS, 2, D], where=part) for u in two]
            qk = [sb(f"c_qk{u}", [P, ROWS, D], where=part) for u in two]
            raw = [sb(f"c_raw{u}", [P, ROWS, H], where=part) for u in two]
            masked = [sb(f"c_masked{u}", [P, ROWS, H], where=part) for u in two]
            acc = [sb(f"c_acc{u}", [P, ROWS, WIDE], where=part) for u in two]
            has_self = sb("has_self", [P, NT * ROWS], where=part)
            no_self = sb("no_self", [P, NT * ROWS], where=part)
            loaded = [sem(f"c_loaded{u}") for u in two]
            biased = [sem(f"c_biased{u}") for u in two]
            x1_ready = [sem(f"c_x1_ready{u}") for u in two]
            x1_stored = [sem(f"c_x1_stored{u}") for u in two]
            stats_ready = [sem(f"c_stats_ready{u}") for u in two]
            moments_ready = [sem(f"c_moments_ready{u}") for u in two]
            std_ready = [sem(f"c_std_ready{u}") for u in two]
            rstd_ready = [sem(f"c_rstd_ready{u}") for u in two]
            shift_ready = [sem(f"c_shift_ready{u}") for u in two]
            hn_ready = [sem(f"c_hn_ready{u}") for u in two]
            turned = sem("c_turned")
            ht_ready = sem("c_ht_ready")
            product_ready = sem("c_product_ready")
            qkv_ready = sem("c_qkv_ready")
            qkv_stored = [sem(f"c_qkv_stored{u}") for u in two]
            qk_ready = sem("c_qk_ready")
            raw_ready = sem("c_raw_ready")
            masked_ready = sem("c_masked_ready")
            peak_ready = sem("c_peak_ready")
            own_ready = sem("c_own_ready")
            acc_stored = [sem(f"c_acc_stored{u}") for u in two]
            c_chain = sem("c_chain")
            turn_ps = part.enter_context(nc.psum_tensor("c_turn_ps", [P, KC * TILE], F32))
            qkv_ps = [part.enter_context(nc.psum_tensor(f"c_qkv_ps{i}", [P, ROWS * D], F32)) for i in range(3)]

            def tile_of(t):
                return t[0] * 2 + t[1]

            @block.sync
            def _(sp):
                def step(at):
                    if at(0) is not None:
                        i, u = at(0)
                        tile = tile_of(at(0))
                        sp.wait_ge(x1_ready[u], i)
                        sp.dma_start(agg[u][:, :, :].rearrange("p r d -> p (r d)"), row_block(agg_table, tile)).then_inc(loaded[u], 16)
                        if isinstance(tile, int) and tile == NT - 1:
                            rows = x[tile * TILE:plan.n, :].rearrange("(p r) d -> p (r d)", r=ROWS)
                            sp.dma_start(xb[u][0:plan.last_p, :, :].rearrange("p r d -> p (r d)"), rows).then_inc(loaded[u], 16)
                        else:
                            sp.dma_start(xb[u][:, :, :].rearrange("p r d -> p (r d)"), row_block(x, tile)).then_inc(loaded[u], 16)
                    if at(1) is not None:
                        i, u = at(1)
                        sp.wait_ge(x1_ready[u], i + 1)
                        sp.dma_start(row_block(x1_table, tile_of(at(1))), x1[u][:, :, :].rearrange("p r d -> p (r d)")).then_inc(x1_stored[u], 16)
                    if at(3) is not None:
                        i, u = at(3)
                        tile = tile_of(at(3))
                        sp.wait_ge(qkv_ready, tile * 3 + 3)
                        for table, rows in ((q_table, qb), (kv_table, kv)):
                            sp.dma_start(row_block(table, tile), rows[u][:, :, :, :].rearrange("p r n d -> p (r n d)")).then_inc(qkv_stored[u], 16)
                    if at(4) is not None:
                        i, u = at(4)
                        tile = tile_of(at(4))
                        sp.wait_ge(peak_ready, tile + 1)
                        sp.wait_ge(own_ready, tile + 1)
                        sp.dma_start(row_block(acc_table, tile), acc[u][:, :, :].rearrange("p r w -> p (r w)")).then_inc(acc_stored[u], 16)

                over_tiles(sp, plan, 4, step)
                for u in two:
                    sp.wait_ge(x1_stored[u], 16 * (NT // 2))
                    sp.wait_ge(qkv_stored[u], 32 * (NT // 2))
                    sp.wait_ge(acc_stored[u], 16 * (NT // 2))

            @block.gpsimd
            def _(pool):
                def step(at):
                    if at(0) is not None:
                        i, u = at(0)
                        hold(pool, loaded[u], i * 32 + 32)
                        nc.gpsimd.tensor_tensor(xb[u][:, :, :], xb[u][:, :, :], b_agg[:, :].unsqueeze(1).to_broadcast([P, ROWS, D]),
                                                ALU.add).then_inc(biased[u], 1)
                    if at(2) is not None:
                        i, u = at(2)
                        tile = tile_of(at(2))
                        hold(pool, qkv_ready, tile * 3 + 2)
                        wait_past(pool, raw_ready, tile - 1)
                        nc.gpsimd.tensor_tensor(qk[u][:, :, :], qb[u][:, :, 0, :], kv[u][:, :, 0, :], ALU.mult).then_inc(qk_ready, 1)

                over_tiles(pool, plan, 2, step)

            @block.scalar
            def _(act):
                def step(at):
                    if at(0) is not None:
                        i, u = at(0)
                        act.wait_ge(moments_ready[u], i + 1)
                        act.wait_ge(shift_ready[u], i)
                        nc.scalar.activation(std[u][:, :], moments[u][:, :, 1], ACT.Sqrt, bias=eps_col[:, 0:1]).then_inc(std_ready[u], 1)
                        act.wait_ge(shift_ready[u], i + 1)
                        wait_past(act, turned, tile_of(at(0)) - 1)
                        for j in range(ROWS):
                            last = nc.scalar.activation(hn[u][:, j, :], x1[u][:, j, :], ACT.Relu,
                                                        bias=shift[u][:, j:j + 1], scale=rstd[u][:, j:j + 1])
                        last.then_inc(hn_ready[u], 1)
                        tile = tile_of(at(0))
                        act.wait_ge(turned, tile + 1)
                        wait_past(act, product_ready, tile * 3 - 3)
                        for kc in range(KC):
                            last = nc.scalar.activation(ht[u][:, kc, :], turn_ps[:, kc * TILE:(kc + 1) * TILE], ACT.Copy)
                        last.then_inc(ht_ready, 1)
                    if at(3) is not None:
                        i, u = at(3)
                        tile = tile_of(at(3))
                        hold(act, qkv_ready, tile * 3 + 3)
                        hold(act, acc_stored[u], i * 16)
                        for j in range(ROWS):
                            last = nc.scalar.activation(acc[u][:, j, SUMS:WEIGHTS], kv[u][:, j, 1, :], ACT.Copy,
                                                        scale=n_self[:, bass.ds(tile * ROWS + j, 1)])
                        last.then_inc(own_ready, 1)

                over_tiles(act, plan, 3, step)

            @block.tensor
            def _(pe):
                def step(at):
                    if at(0) is not None:
                        i, u = at(0)
                        pe.wait_ge(hn_ready[u], i + 1)
                        wait_past(pe, ht_ready, tile_of(at(0)))
                        for kc in range(KC):
                            for j in range(ROWS):
                                last = nc.tensor.transpose(turn_ps[:, kc * TILE + j * P:kc * TILE + (j + 1) * P],
                                                           hn[u][:, j, kc * P:(kc + 1) * P], ident[:, :])
                        last.then_inc(turned, 1)
                    if at(1) is not None:
                        i, u = at(1)
                        tile = tile_of(at(1))
                        pe.wait_ge(ht_ready, tile + 1)
                        for n in range(3):
                            wait_past(pe, qkv_ready, tile * 3 - 2 + n)
                            for j in range(ROWS):
                                for kc in range(KC):
                                    last = nc.tensor.matmul(qkv_ps[n][:, j * D:(j + 1) * D], ht[u][:, kc, j * P:(j + 1) * P],
                                                            w_qkv[:, kc, n * D:(n + 1) * D], start=kc == 0, stop=kc == KC - 1)
                            last.then_inc(product_ready, 1)

                over_tiles(pe, plan, 1, step)

            @block.vector
            def _(dve):
                v = nc.vector
                v.tensor_scalar(has_self[:, :], n_self[:, :], 1.0, None, ALU.min).then_inc(c_chain, 1)
                dve.wait_ge(c_chain, 1)
                v.tensor_scalar(no_self[:, :], has_self[:, :], -1.0, -LOW, ALU.add, ALU.mult).then_inc(c_chain, 1)
                dve.wait_ge(c_chain, 2)
                v.tensor_scalar(has_self[:, :], has_self[:, :], SCALE, None, ALU.mult).then_inc(c_chain, 1)
                dve.wait_ge(c_chain, 3)

                def step(at):
                    if at(0) is not None:
                        i, u = at(0)
                        tile = tile_of(at(0))
                        hold(dve, biased[u], i + 1)
                        hold(dve, x1_stored[u], i * 16)
                        hold(dve, hn_ready[u], i)
                        for j in range(ROWS):
                            last = v.scalar_tensor_tensor(x1[u][:, j, :], agg[u][:, j, :], dinv[:, bass.ds(tile * ROWS + j, 1)],
                                                          xb[u][:, j, :], ALU.mult, ALU.add)
                        last.then_inc(x1_ready[u], 1)
                        dve.wait_ge(x1_ready[u], i + 1)
                        row_moments(v, dve, hold, x1[u], stats[u], moments[u], stats_ready[u], moments_ready[u], i)
                    if at(2) is not None:
                        i, u2 = at(2)
                        t2 = tile_of(at(2))
                        for n in range(3):
                            dve.wait_ge(product_ready, t2 * 3 + 1 + n)
                            if n == 0:
                                dve.wait_ge(qkv_stored[u2], i * 32)
                                wait_past(dve, qk_ready, t2 - 1)
                            if n == 2:
                                wait_past(dve, own_ready, t2 - 1)
                            goes = qb[u2][:, :, 0, :] if n == 0 else kv[u2][:, :, n - 1, :]
                            v.tensor_tensor(goes, qkv_ps[n][:, :].rearrange("p (j d) -> p j d", j=ROWS),
                                            b_qkv[:, n * D:(n + 1) * D].unsqueeze(1).to_broadcast([P, ROWS, D]),
                                            ALU.add).then_inc(qkv_ready, 1)
                            if n == 0 and at(0) is not None:
                                i0, u = at(0)
                                row_scales(v, dve, moments[u], std[u], rstd[u], shift[u],
                                           std_ready[u], rstd_ready[u], shift_ready[u], i0)
                    elif at(0) is not None:
                        row_scales(v, dve, moments[u], std[u], rstd[u], shift[u],
                                   std_ready[u], rstd_ready[u], shift_ready[u], i)
                    if at(3) is not None:
                        i, u = at(3)
                        tile = tile_of(at(3))
                        dve.wait_ge(qk_ready, tile + 1)
                        v.reduce_sum(raw[u][:, :, :], qk[u][:, :, :].rearrange("p j (d h) -> p j h d", h=H),
                                     axis=AX.X).then_inc(raw_ready, 1)
                        hold(dve, raw_ready, tile + 1)
                        here = bass.ds(tile * ROWS, ROWS)
                        v.tensor_tensor(masked[u][:, :, :], raw[u][:, :, :], has_self[:, here].unsqueeze(2).to_broadcast([P, ROWS, H]),
                                        ALU.mult).then_inc(masked_ready, 1)
                        hold(dve, masked_ready, tile + 1)
                        hold(dve, acc_stored[u], i * 16)
                        v.tensor_copy(acc[u][:, :, WEIGHTS:WIDE], n_self[:, here].unsqueeze(2).to_broadcast([P, ROWS, H]))
                        v.tensor_tensor(acc[u][:, :, PEAKS:SUMS], masked[u][:, :, :], no_self[:, here].unsqueeze(2).to_broadcast([P, ROWS, H]),
                                        ALU.add).then_inc(peak_ready, 1)

                over_tiles(dve, plan, 3, step)

        end_part()
        with ExitStack() as part, nc.Block() as block:
            c = column_parts("attend", 0, part)
            q_got = [sb(f"q_got{k}", [P, D], where=part) for k in eight]
            kv_got = [sb(f"kv_got{k}", [P, 2, D], where=part) for k in eight]
            row_got = [sb(f"row_got{k}", [P, H + WIDE], where=part) for k in eight]
            row_new = [sb(f"row_new{k}", [P, WIDE], where=part) for k in eight]
            top = [sb(f"top{k}", [P, H], where=part) for k in eight]
            below = [sb(f"below{k}", [P, 2, H], where=part) for k in eight]
            share = [sb(f"share{k}", [P, D + 2 * H], where=part) for k in eight]
            kept = [sb(f"kept{k}", [P, D + H], where=part) for k in two]
            qk = [sb(f"attend_qk{k}", [P, D], where=part) for k in two]
            differ = [sb(f"differ{k}", [P, P], BF16, where=part) for k in range(4)]
            low_col = sb("low_col", [P, 1], where=part)
            spread_ps = [part.enter_context(nc.psum_tensor(f"spread_ps{k}", [P, H * P], F32)) for k in two]
            sum_ps = [part.enter_context(nc.psum_tensor(f"attend_sum_ps{k}", [P, 512], F32)) for k in two]
            qkv_gathered = [pool_dma_sem(f"qkv_gathered{k}") for k in eight]
            row_gathered = [pool_dma_sem(f"row_gathered{k}") for k in eight]
            low_ready = sem("low_ready")
            qk_ready = sem("attend_qk_ready")
            score_ready = sem("score_ready")
            differ_ready = sem("differ_ready")
            spread_ready = sem("spread_ready")
            top_ready = sem("top_ready")
            peak_ready = sem("peak_ready")
            below_ready = sem("below_ready")
            weight_ready = sem("weight_ready")
            share_ready = sem("share_ready")
            kept_ready = sem("kept_ready")
            sum_ready = sem("attend_sum_ready")
            row_ready = sem("row_ready")

            @block.gpsimd
            def _(pool):
                turns = load_turns(pool)

                def step(at):
                    if (col := at(6)) is not None:
                        i, k = col
                        hold(pool, row_ready, number(col))
                        hold(pool, c["goal_ready"], number(col))
                        scatter(acc_table, c["goal"][k][:, 0:1], row_new[k][:, :]).then_inc(c["scattered"][k], 16)
                    if (col := at(1)) is not None:
                        i, k = col
                        hold(pool, c["staged"], number(col))
                        gather(q_got[k][:, :], q_table, c["ends"][k][:, 0:1]).then_inc(qkv_gathered[k], 16)
                        gather(kv_got[k][:, :, :].rearrange("p n d -> p (n d)"), kv_table, c["ends"][k][:, 1:2]).then_inc(qkv_gathered[k], 16)
                    if (col := at(4)) is not None:
                        i, k = col
                        if (two_back := at(6)) is not None:
                            hold(pool, c["scattered"][two_back[1]], two_back[0] * 16 + 16)
                        gather(row_got[k][:, H:H + WIDE], acc_table, c["ends"][k][:, 0:1]).then_inc(row_gathered[k], 16)

                over_columns(pool, turns, 6, step)
                for k in eight:
                    hold(pool, c["scattered"][k], turns * 16)

            @block.vector
            def _(dve):
                turns = load_turns(dve)
                v = nc.vector

                def write_same(across, key, k):
                    v.tensor_scalar(c["same"][k % 4][:, :], across, key, None, ALU.is_equal)

                def step(at):
                    if at(0) is not None:
                        stage_column(dve, c, at(0))
                    if (col := at(5)) is not None:
                        i, k = col
                        n = number(col)
                        dve.wait_ge(row_gathered[k], i * 16 + 16)
                        dve.wait_ge(top_ready, n)
                        v.tensor_tensor(row_new[k][:, PEAKS:SUMS], row_got[k][:, H:2 * H], top[k][:, :], ALU.max).then_inc(peak_ready, 1)
                        dve.wait_ge(peak_ready, n)
                        v.tensor_tensor(below[k][:, :, :], row_got[k][:, 0:2 * H].rearrange("p (n h) -> p n h", h=H),
                                        row_new[k][:, PEAKS:SUMS].unsqueeze(1).to_broadcast([P, 2, H]), ALU.subtract).then_inc(below_ready, 1)
                        dve.wait_ge(weight_ready, n)
                        v.tensor_tensor(share[k][:, 0:D].rearrange("p (d h) -> p d h", h=H),
                                        kv_got[k][:, 1, :].rearrange("p (d h) -> p d h", h=H),
                                        share[k][:, D:D + H].unsqueeze(1).to_broadcast([P, DH, H]), ALU.mult).then_inc(share_ready, 1)
                        wait_past(dve, sum_ready, n - 2)
                        v.tensor_tensor(kept[k % 2][:, :].rearrange("p (d h) -> p d h", h=H),
                                        row_got[k][:, H + SUMS:H + WIDE].rearrange("p (d h) -> p d h", h=H),
                                        share[k][:, D + H:D + 2 * H].unsqueeze(1).to_broadcast([P, DH + 1, H]), ALU.mult).then_inc(kept_ready, 1)
                    if (col := at(2)) is not None:
                        wait_past(dve, sum_ready, number(col) - 4)
                        wait_past(dve, differ_ready, number(col) - 4)
                        find_goals(dve, c, col, write_same)
                    if (col := at(3)) is not None:
                        i, k = col
                        n = number(col)
                        dve.wait_ge(qkv_gathered[k], i * 32 + 32)
                        v.scalar_tensor_tensor(qk[k % 2][:, :], q_got[k][:, :], SCALE, kv_got[k][:, 0, :], ALU.mult,
                                               ALU.mult).then_inc(qk_ready, 1)
                        dve.wait_ge(qk_ready, n)
                        v.reduce_sum(row_got[k][:, 0:H], qk[k % 2][:, :].rearrange("p (d h) -> p h d", h=H), axis=AX.X).then_inc(score_ready, 1)
                    if (col := at(4)) is not None:
                        i, k = col
                        dve.wait_ge(spread_ready, number(col))
                        v.reduce_max(top[k][:, :], spread_ps[k % 2][:, :].rearrange("p (h e) -> p h e", h=H), axis=AX.X).then_inc(top_ready, 1)

                over_columns(dve, turns, 5, step)

            @block.tensor
            def _(pe):
                turns = load_turns(pe)

                def step(at):
                    if (col := at(5)) is not None:
                        i, k = col
                        n = number(col)
                        pe.wait_ge(share_ready, n)
                        wait_past(pe, row_ready, n - 2)
                        nc.tensor.matmul(sum_ps[k % 2][:, 0:D + H], c["same"][k % 4][:, :], share[k][:, 0:D + H], start=True, stop=False)
                        pe.wait_ge(kept_ready, n)
                        nc.tensor.matmul(sum_ps[k % 2][:, 0:D + H], ident[:, :], kept[k % 2][:, :],
                                         start=False, stop=True).then_inc(sum_ready, 1)
                    if (col := at(1)) is not None:
                        keys_across(pe, c, col)
                    if (col := at(3)) is not None:
                        i, k = col
                        n = number(col)
                        pe.wait_ge(differ_ready, n)
                        pe.wait_ge(score_ready, n)
                        wait_past(pe, top_ready, n - 2)
                        half = H // 2
                        for b in range(2):
                            nc.tensor.matmul(spread_ps[k % 2][:, b * 512:(b + 1) * 512], ident_b[:, :],
                                             differ[k % 4][:, :].unsqueeze(1).to_broadcast([P, half, P]), start=True, stop=False)
                            for h in range(half):
                                at_h = b * half + h
                                last = nc.tensor.matmul(spread_ps[k % 2][:, at_h * P:(at_h + 1) * P],
                                                        row_got[k][:, at_h:at_h + 1].to_broadcast([P, P]), ident[:, :],
                                                        start=False, stop=h == half - 1)
                        last.then_inc(spread_ready, 1)

                over_columns(pe, turns, 5, step)

            @block.scalar
            def _(act):
                turns = load_turns(act)
                nc.scalar.activation(low_col[:, :], eps_col[:, :], ACT.Copy, scale=0.0, bias=LOW).then_inc(low_ready, 1)
                act.wait_ge(low_ready, 1)

                def step(at):
                    if (col := at(5)) is not None:
                        i, k = col
                        act.wait_ge(below_ready, number(col))
                        nc.scalar.activation(share[k][:, D:D + 2 * H], below[k][:, :, :].rearrange("p n h -> p (n h)"),
                                             ACT.Exp).then_inc(weight_ready, 1)
                    if (col := at(5)) is not None:
                        i, k = col
                        act.wait_ge(sum_ready, number(col))
                        nc.scalar.activation(row_new[k][:, SUMS:WIDE], sum_ps[k % 2][:, 0:D + H], ACT.Copy).then_inc(row_ready, 1)
                    if (col := at(2)) is not None:
                        i, k = col
                        act.wait_ge(c["ranked"], number(col))
                        wait_past(act, spread_ready, number(col) - 4)
                        nc.scalar.activation(differ[k % 4][:, :], c["same"][k % 4][:, :], ACT.Identity,
                                             bias=low_col[:, 0:1], scale=-LOW).then_inc(differ_ready, 1)

                over_columns(act, turns, 5, step)

        end_part()

        with ExitStack() as part, nc.Block() as block:
            three = range(3)
            acc = [sb(f"e_acc{u}", [P, ROWS, WIDE], where=part) for u in two]
            x1 = [sb(f"e_x1_{u}", [P, ROWS, D], where=part) for u in two]
            total = [sb(f"e_total{u}", [P, ROWS, H], where=part) for u in two]
            mean = [sb(f"e_mean{u}", [P, ROWS, D], where=part) for u in two]
            ht = [sb(f"e_ht{u}", [P, KC, TILE], where=part) for u in two]
            result = [sb(f"e_result{u}", [P, ROWS, D], where=part) for u in two]
            loaded = [sem(f"e_loaded{u}") for u in two]
            x1_loaded = [sem(f"e_x1_loaded{u}") for u in two]
            total_ready = sem("e_total_ready")
            mean_ready = sem("e_mean_ready")
            turned = sem("e_turned")
            ht_ready = sem("e_ht_ready")
            product_ready = sem("e_product_ready")
            x1_biased = sem("e_x1_biased")
            result_ready = sem("e_result_ready")
            result_stored = [sem(f"e_result_stored{u}") for u in two]
            turn_ps = [part.enter_context(nc.psum_tensor(f"e_turn_ps{u}", [P, KC * TILE], F32)) for u in two]
            out_ps = [part.enter_context(nc.psum_tensor(f"e_out_ps{u}", [P, ROWS * D], F32)) for u in two]

            @block.sync
            def _(sp):
                def step(at):
                    if at(0) is not None:
                        i, u = at(0)
                        tile = tile_of(at(0))
                        wait_past(sp, mean_ready, tile - 1)
                        sp.dma_start(acc[u][:, :, :].rearrange("p r w -> p (r w)"), row_block(acc_table, tile)).then_inc(loaded[u], 16)
                    if at(1) is not None:
                        i, u = at(1)
                        tile = tile_of(at(1))
                        wait_past(sp, result_ready, tile - 1)
                        sp.dma_start(x1[u][:, :, :].rearrange("p r d -> p (r d)"), row_block(x1_table, tile)).then_inc(x1_loaded[u], 16)
                    if at(4) is not None:
                        i, u = at(4)
                        tile = tile_of(at(4))
                        sp.wait_ge(result_ready, tile + 1)
                        if isinstance(tile, int) and tile == NT - 1:
                            sp.dma_start(out[tile * TILE:plan.n, :].rearrange("(p r) d -> p (r d)", r=ROWS),
                                         result[u][0:plan.last_p, :, :].rearrange("p r d -> p (r d)")).then_inc(result_stored[u], 16)
                        else:
                            sp.dma_start(row_block(out, tile), result[u][:, :, :].rearrange("p r d -> p (r d)")).then_inc(result_stored[u], 16)
                over_tiles(sp, plan, 4, step)
                for u in two:
                    sp.wait_ge(result_stored[u], 16 * (NT // 2))

            @block.gpsimd
            def _(pool):
                def step(at):
                    i, u = at(0)
                    hold(pool, x1_loaded[u], i * 16 + 16)
                    nc.gpsimd.tensor_tensor(x1[u][:, :, :], x1[u][:, :, :], b_out[:, :].unsqueeze(1).to_broadcast([P, ROWS, D]),
                                            ALU.add).then_inc(x1_biased, 1)

                over_tiles(pool, plan, 0, step)

            @block.vector
            def _(dve):
                v = nc.vector

                def step(at):
                    if at(0) is not None:
                        i, u = at(0)
                        tile = tile_of(at(0))
                        dve.wait_ge(loaded[u], i * 16 + 16)
                        v.tensor_scalar(total[u][:, :, :], acc[u][:, :, WEIGHTS:WIDE], 0.5, None, ALU.max).then_inc(total_ready, 1)
                        dve.wait_ge(total_ready, tile * 2 + 1)
                        v.reciprocal(total[u][:, :, :], total[u][:, :, :]).then_inc(total_ready, 1)
                        dve.wait_ge(total_ready, tile * 2 + 2)
                        wait_past(dve, turned, tile - 1)
                        v.tensor_tensor(mean[u][:, :, :].rearrange("p r (d h) -> p r d h", h=H),
                                        acc[u][:, :, SUMS:WEIGHTS].rearrange("p r (d h) -> p r d h", h=H),
                                        total[u][:, :, :].unsqueeze(2).to_broadcast([P, ROWS, DH, H]),
                                        ALU.mult).then_inc(mean_ready, 1)
                    if at(2) is not None:
                        i, u = at(2)
                        tile = tile_of(at(2))
                        dve.wait_ge(product_ready, tile + 1)
                        dve.wait_ge(x1_biased, tile + 1)
                        dve.wait_ge(result_stored[u], i * 16)
                        v.tensor_tensor(result[u][:, :, :], out_ps[u][:, :].rearrange("p (r d) -> p r d", r=ROWS), x1[u][:, :, :],
                                        ALU.add).then_inc(result_ready, 1)

                over_tiles(dve, plan, 2, step)

            @block.scalar
            def _(act):
                def step(at):
                    i, u = at(0)
                    tile = tile_of(at(0))
                    act.wait_ge(turned, tile + 1)
                    wait_past(act, product_ready, tile - 1)
                    for kc in range(KC):
                        last = nc.scalar.activation(ht[u][:, kc, :], turn_ps[u][:, kc * TILE:(kc + 1) * TILE], ACT.Copy)
                    last.then_inc(ht_ready, 1)

                over_tiles(act, plan, 0, step)

            @block.tensor
            def _(pe):
                def step(at):
                    if at(0) is not None:
                        i, u = at(0)
                        tile = tile_of(at(0))
                        pe.wait_ge(mean_ready, tile + 1)
                        wait_past(pe, ht_ready, tile - 1)
                        for kc in range(KC):
                            for j in range(ROWS):
                                last = nc.tensor.transpose(turn_ps[u][:, kc * TILE + j * P:kc * TILE + (j + 1) * P],
                                                           mean[u][:, j, kc * P:(kc + 1) * P], ident[:, :])
                        last.then_inc(turned, 1)
                    if at(1) is not None:
                        i, u = at(1)
                        tile = tile_of(at(1))
                        pe.wait_ge(ht_ready, tile + 1)
                        wait_past(pe, result_ready, tile - 1)
                        for j in range(ROWS):
                            for kc in range(KC):
                                last = nc.tensor.matmul(out_ps[u][:, j * D:(j + 1) * D], ht[u][:, kc, j * P:(j + 1) * P],
                                                        w_out[:, kc, :], start=kc == 0, stop=kc == KC - 1)
                        last.then_inc(product_ready, 1)

                over_tiles(pe, plan, 1, step)


INPUTS = ["x", "src", "dst"] + ["L0_gnn_" + k for k in ("w1", "b1", "gamma", "beta", "w2", "b2", "w_gcn", "b_gcn")] + \
    ["L1_gnn_" + k for k in ("Wq", "bq", "Wk", "bk", "Wv", "bv", "Wo", "bo")]


def kernel(**inputs):
    import numpy as np
    from concourse import bacc
    from concourse.bass_utils import run_bass_kernel_spmd

    nc = bacc.Bacc("TRN2", target_bir_lowering=False, num_devices=1)
    arrays, args = {}, []
    for name in INPUTS:
        a = np.ascontiguousarray(inputs[name])
        arrays[f"in_{name}"] = a
        args.append(nc.dram_tensor(f"in_{name}", a.shape, mybir.dt.from_np(a.dtype), kind="ExternalInput").ap())
    out = nc.dram_tensor("out", list(arrays["in_x"].shape), F32, kind="ExternalOutput").ap()
    build(nc, *args, out)
    return run_bass_kernel_spmd(nc, [arrays], core_ids=[0]).results[0]["out"]
```

```python
from contextlib import ExitStack

import concourse.bass as bass
from concourse import mybir

F32 = mybir.dt.float32
BF16 = mybir.dt.bfloat16
F16 = mybir.dt.float16
I32 = mybir.dt.int32
ALU = mybir.AluOpType
ACT = mybir.ActivationFunctionType
AX = mybir.AxisListType

P = 128
D = 256
KC = D // P
H = 8
DH = D // H
ROWS = 4
TILE = P * ROWS
SLOTS = 8
GROUPS = 2
BY_SOURCE, BY_TARGET = 0, 1
SCALE = float(DH) ** -0.5
LOW = -1.0e30
EPS = 1e-5
HIST = 6
PEAKS, SUMS, WEIGHTS = 0, H, H + D
WIDE = D + 2 * H


class Plan:

    def __init__(self, n, e):
        self.n, self.e = n, e
        self.tiles = -(-n // TILE)
        self.tiles += self.tiles % 2
        self.last = n - (self.tiles - 1) * TILE
        assert 0 < self.last < TILE and self.last % ROWS == 0 and self.last + P <= TILE
        self.last_p = self.last // ROWS
        self.table = self.tiles * TILE
        self.per_part = -(-e // P)
        self.cols = self.tiles * HIST
        assert self.per_part <= self.cols
        self.full_parts = e // self.per_part
        self.rest = e - self.full_parts * self.per_part
        self.most_turns = max(2, -(-self.cols // 4))
        self.room = (8 * self.most_turns, 4 * self.most_turns + 8)


def row_block(table, tile):
    return table[bass.ds(tile * TILE, TILE), :].rearrange("(p r) d -> p (r d)", p=P)


def over_tiles(eng, plan, lag, step, slots=2):
    turns = plan.tiles // slots

    def turn(i, fixed):
        for u in range(slots):
            def at(l):
                back, slot = divmod(u - l, slots)
                turn_of = i + back
                if fixed and not 0 <= turn_of * slots + slot < plan.tiles:
                    return None
                if slots == 2:
                    return turn_of, slot
                return turn_of * 2 + slot // 2, slot % 2, turn_of, slot

            step(at)

    head = lag // slots + 1
    for i in range(head):
        turn(i, True)
    last = turns if plan.tiles % slots else turns - 1
    with eng.Fori(head, last) as i:
        turn(i, False)
    for i in range(last, (plan.tiles - 1 + lag) // slots + 1):
        turn(i, True)


def over_columns(eng, turns, lag, step):
    assert lag < SLOTS

    def turn(i, first, after):
        for k in range(SLOTS if not after else lag):
            def at(l):
                back, slot = divmod(k - l, SLOTS)
                if (first and back < 0) or (after and back == 0):
                    return None
                return i + back, slot

            step(at)

    turn(0, True, False)
    with eng.Fori(1, turns) as i:
        turn(i, False, False)
    turn(turns, False, True)


def row_moments(v, dve, hold, x, stats, moments, stats_ready, moments_ready, i):
    for j in range(ROWS):
        last = v.bn_stats(stats[:, j, :], x[:, j, :])
    last.then_inc(stats_ready, 1)
    hold(dve, stats_ready, i + 1)
    for j in range(ROWS):
        last = v.bn_aggr(moments[:, j, :], stats[:, j, :])
    last.then_inc(moments_ready, 1)


def row_scales(v, dve, moments, std, rstd, shift, std_ready, rstd_ready, shift_ready, i):
    dve.wait_ge(std_ready, i + 1)
    v.reciprocal(rstd[:, :], std[:, :]).then_inc(rstd_ready, 1)
    dve.wait_ge(rstd_ready, i + 1)
    v.scalar_tensor_tensor(shift[:, :], moments[:, :, 0], -1.0, rstd[:, :], ALU.mult, ALU.mult).then_inc(shift_ready, 1)


def build(nc, x, src, dst, w1, b1, gamma, beta, w2, b2, w_gcn, b_gcn,
          wq, bq, wk, bk, wv, bv, wo, bo, out):
    plan = Plan(x.shape[0], src.shape[0])
    NT, TAB, COLS, ROOM = plan.tiles, plan.table, plan.cols, plan.room
    USED = 4 * plan.most_turns
    BESIDE = NT // 2 - 1

    def dram(name, shape, dt=F32):
        return nc.dram_tensor(name, shape, dt, kind="Internal").ap()

    h1_table = dram("h1_table", [NT * P, KC * TILE])
    y_table = dram("y_table", [TAB, D])
    agg_table = dram("agg_table", [TAB + 2 * P, D])
    x1_table = dram("x1_table", [TAB, D])
    q_table = dram("q_table", [TAB, D])
    kv_table = dram("kv_table", [TAB, 2 * D])
    acc_table = dram("acc_table", [TAB + 2 * P, WIDE])

    with ExitStack() as ctx:
        def sb(name, shape, dt=F32, where=ctx):
            return where.enter_context(nc.sbuf_tensor(name, shape, dt))

        in_use = []

        def sem(name):
            in_use.append(nc.alloc_semaphore(name))
            return in_use[-1]

        def pool_dma_sem(name):
            return nc.alloc_semaphore(name)

        def end_part():
            with nc.Block() as block:
                @block.sync
                def _(sp):
                    for s in in_use:
                        sp.sem_clear(s)
            for s in in_use:
                nc.release_semaphore(s)
            in_use.clear()

        ident = sb("ident", [P, P])
        ident_b = sb("ident_b", [P, P], BF16)
        earlier = sb("earlier", [P, P])
        spare = sb("spare", [P, 3])
        lane = sb("lane", [P, max(P, NT * ROWS)], F16)
        w1_t = sb("w1_t", [P, KC, D])
        w_mix = sb("w_mix", [P, KC, D])
        b_mix = sb("b_mix", [P, D])
        w_qkv_hi = sb("w_qkv_hi", [P, KC, 3 * D], F16)
        w_qkv_lo = sb("w_qkv_lo", [P, KC, 3 * D], F16)
        unscale = sb("unscale", [P, 1])
        b_qkv = sb("b_qkv", [P, 3 * D])
        w_out = sb("w_out", [P, KC, D])
        b_out = sb("b_out", [P, D])
        b_agg = sb("b_agg", [P, D])
        eps_col = sb("eps_col", [P, 1])
        one_col = sb("one_col", [P, 1])
        bn_in = sb("bn_in", [P, 3, KC])
        lo_pair = sb("lo_pair", [P, COLS, 2], F16)
        dst_hi = sb("dst_hi", [P, COLS])
        packed_i = [sb(f"packed_i{m}", [P, 2, GROUPS, ROOM[m]], I32) for m in (BY_SOURCE, BY_TARGET)]
        packed_f = [sb(f"packed_f{m}", [P, GROUPS, USED]) for m in (BY_SOURCE, BY_TARGET)]
        stock = sb("stock", [P, 2, GROUPS, 2, COLS])
        more_turns = sb("more_turns", [P, 2], I32)
        rounds = sb("rounds", [P, 2], I32)
        dinv = sb("dinv", [P, NT * ROWS])
        n_self = sb("n_self", [P, NT * ROWS])
        held = nc.alloc_semaphore("held")

        def hold(eng, s, value):
            eng.wait_ge(s, value)
            if not isinstance(value, int):
                eng.sem_inc(held, 1)

        def finish_packing(v, link, m, empty, nodes_f):
            pi = packed_i[m][:, :, :, 0:USED].rearrange("p a g c -> p (a g) c")
            link(v.tensor_scalar(empty[:, :, :], pi.bitcast(F32), 0.0, None, ALU.is_equal))
            link(v.tensor_scalar(pi, pi, 0xFFFF, None, ALU.bitwise_and))
            link(v.tensor_copy(nodes_f[:, :, :], pi))
            v.scalar_tensor_tensor(pi, empty[:, :, :], spare[:, 0:1], nodes_f[:, :, :], ALU.mult, ALU.add)
            for g in range(GROUPS):
                at = m * GROUPS + g
                v.scalar_tensor_tensor(packed_f[m][:, g, :], empty[:, at, :], spare[:, 1 + g:2 + g], nodes_f[:, at, :], ALU.mult, ALU.add)

        with ExitStack() as part:
            w1_n = sb("w1_n", [P, KC, D], where=part)
            w2_n = sb("w2_n", [P, KC, D], where=part)
            wg_n = sb("wg_n", [P, KC, D], where=part)
            wg_t = sb("wg_t", [P, KC, D], where=part)
            w_qkv = sb("w_qkv", [P, KC, 3 * D], where=part)
            w_power = sb("w_power", [P, KC * 3 * D], I32, where=part)
            w_peak = sb("w_peak", [P, 1], where=part)
            w_peaks = sb("w_peaks", [P, 1], where=part)
            w_scale = sb("w_scale", [P, 1], where=part)
            b2_c = sb("b2_c", [P, KC], where=part)
            edges = sb("edges", [P, 2, COLS], I32, where=part)
            work_i = sb("work_i", [P, 2, COLS], I32, where=part)
            place = sb("place", [P, COLS], I32, where=part)
            edges_f = sb("edges_f", [P, 2, COLS], where=part)
            odd = sb("odd", [P, 2, 2, COLS], where=part)
            apart = sb("apart", [P, COLS], where=part)
            member = sb("member", [P, COLS], where=part)
            dst_lo = sb("dst_lo", [P, COLS], where=part)
            self_lo = sb("self_lo", [P, COLS], where=part)
            counts = sb("counts", [P, 2 * GROUPS], where=part)
            most = sb("most", [P, 2 * GROUPS], where=part)
            rounds_f = sb("rounds_f", [P, 2], where=part)
            longest = sb("longest", [P, 2], where=part)
            turns_f = sb("turns_f", [P, 2], where=part)
            ps = [part.enter_context(nc.psum_tensor(f"prep_ps{i}", [P, 512], F32)) for i in range(4)]
            loaded = sem("prep_loaded")
            pads_ready = sem("pads_ready")
            edges_loaded = sem("edges_loaded")
            const_ready = sem("const_ready")
            turned = sem("weights_turned")
            copied = sem("weights_copied")
            mixed = sem("weights_mixed")
            chain = sem("prep_chain")
            counted = sem("edges_counted")
            stocked = sem("edges_stocked")
            w_peak_ready = sem("w_peak_ready")
            w_peaks_ready = sem("w_peaks_ready")
            most_ready = sem("most_ready")
            vchain = sem("prep_vector_chain")
            n_loads = 16

            with nc.Block() as block:
                @block.sync
                def _(sp):
                    def halves(w):
                        return w.rearrange("(c p) n -> p c n", p=P)

                    def column(v):
                        return v.rearrange("(c p) -> p c", p=P)

                    n = 0
                    pairs = [(w1_n[:, :, :], halves(w1)), (w2_n[:, :, :], halves(w2)), (wg_n[:, :, :], halves(w_gcn)),
                             (w_out[:, :, :], halves(wo)), (b_out[:, :], bo.partition_broadcast(P)),
                             (b_agg[:, :], b_gcn.partition_broadcast(P))]
                    for i, (w, b) in enumerate(((wq, bq), (wk, bk), (wv, bv))):
                        pairs.append((w_qkv[:, :, i * D:(i + 1) * D], halves(w)))
                        pairs.append((b_qkv[:, i * D:(i + 1) * D], b.partition_broadcast(P)))
                    with nc.allow_non_contiguous_dma(reason="a few hundred words, once"):
                        for i, v in enumerate((b1, gamma, beta)):
                            pairs.append((bn_in[:, i, :], column(v)))
                        pairs.append((b2_c[:, :], column(b2)))
                        assert len(pairs) == n_loads
                        sp.wait_ge(pads_ready, 1)
                        full, per, rest = plan.full_parts, plan.per_part, plan.rest
                        for i, e in enumerate((src, dst)):
                            lo = full // 16 * 16
                            for a, b in ((0, lo), (lo, full)):
                                if a < b:
                                    sp.dma_start(edges[a:b, i, 0:per], e[a * per:b * per].rearrange("(p c) -> p c", c=per)).then_inc(edges_loaded, 16)
                                    n += 1
                            if rest:
                                sp.dma_start(edges[full:full + 1, i, 0:rest], e[full * per:plan.e].rearrange("(p c) -> p c", p=1)).then_inc(edges_loaded, 16)
                                n += 1
                        plan.edge_loads = n
                        for o, i in pairs:
                            sp.dma_start(o, i).then_inc(loaded, 16)
                        sp.wait_ge(loaded, 16 * n_loads)
                        sp.wait_ge(edges_loaded, 16 * n)

                @block.gpsimd
                def _(pool):
                    pool.iota(edges[:, :, :], [[0, 2 * COLS]], base=plan.n, channel_multiplier=1).then_inc(pads_ready, 1)
                    pool.iota(place[:, :], [[1, COLS]], base=0, channel_multiplier=0).then_inc(const_ready, 1)
                    for i, base in enumerate((plan.n, TAB, TAB + P)):
                        pool.iota(spare[:, i:i + 1], [[0, 1]], base=base, channel_multiplier=1,
                                  allow_small_or_imprecise_dtypes=True).then_inc(const_ready, 1)
                    pool.iota(lane[:, :], [[1, max(P, NT * ROWS)]], base=0, channel_multiplier=0,
                              allow_small_or_imprecise_dtypes=True).then_inc(const_ready, 1)
                    pool.memset(eps_col[:, :], EPS).then_inc(const_ready, 1)
                    pool.memset(one_col[:, :], 1.0).then_inc(const_ready, 1)
                    pool.memset(ident[:, :], 0.0).then_inc(chain, 1)
                    pool.memset(ident_b[:, :], 0.0).then_inc(chain, 1)
                    pool.memset(earlier[:, :], 0.0).then_inc(chain, 1)
                    for m in (BY_SOURCE, BY_TARGET):
                        pool.memset(packed_i[m][:, :, :, :], 0).then_inc(const_ready, 1)
                    pool.wait_ge(chain, 3)
                    for m in (ident, ident_b):
                        pool.affine_select(out=m[:, :], in_=m[:, :], compare_op=ALU.not_equal, fill=1.0, base=0,
                                           pattern=[[-1, P]], channel_multiplier=1).then_inc(const_ready, 1)
                    pool.affine_select(out=earlier[:, :], in_=earlier[:, :], compare_op=ALU.is_ge, fill=1.0, base=0,
                                       pattern=[[1, P]], channel_multiplier=-1).then_inc(const_ready, 1)
                    pool.wait_ge(w_peak_ready, 1)
                    pool.partition_all_reduce(w_peaks[:, :], w_peak[:, :], P, bass.bass_isa.ReduceOp.max).then_inc(w_peaks_ready, 1)
                    pool.wait_ge(counted, 2 * GROUPS)
                    pool.partition_all_reduce(most[:, :], counts[:, :], P, bass.bass_isa.ReduceOp.max).then_inc(most_ready, 1)

                @block.tensor
                def _(pe):
                    pe.wait_ge(loaded, 16 * n_loads)
                    pe.wait_ge(const_ready, 12)
                    for b, w in enumerate((w1_n, wg_n)):
                        for kc in range(KC):
                            for oc in range(KC):
                                last = nc.tensor.transpose(ps[b][:, kc * D + oc * P:kc * D + oc * P + P],
                                                           w[:, oc, kc * P:(kc + 1) * P], ident[:, :])
                        last.then_inc(turned, 1)
                    pe.wait_ge(copied, 2)
                    for kc in range(KC):
                        for jc in range(KC):
                            nc.tensor.matmul(ps[2][:, kc * D:(kc + 1) * D], w2_n[:, jc, kc * P:(kc + 1) * P],
                                             wg_t[:, jc, :], start=jc == 0, stop=jc == KC - 1)
                    for jc in range(KC):
                        last = nc.tensor.matmul(ps[3][:, 0:D], b2_c[:, jc:jc + 1].to_broadcast([P, P]), wg_t[:, jc, :],
                                                start=jc == 0, stop=jc == KC - 1)
                    last.then_inc(mixed, 1)

                @block.scalar
                def _(act):
                    for b, w in enumerate((w1_t, wg_t)):
                        act.wait_ge(turned, b + 1)
                        nc.scalar.activation(w[:, :, :].rearrange("p a b -> p (a b)"), ps[b][:, :], ACT.Copy).then_inc(copied, 1)
                    act.wait_ge(mixed, 1)
                    nc.scalar.activation(w_mix[:, :, :].rearrange("p a b -> p (a b)"), ps[2][:, :], ACT.Copy)
                    nc.scalar.activation(b_mix[:, :], ps[3][:, 0:D], ACT.Copy)

                @block.vector
                def _(dve):
                    done = [0]

                    def link(ins):
                        done[0] += 1
                        ins.then_inc(vchain, 1)
                        dve.wait_ge(vchain, done[0])

                    v = nc.vector
                    dve.wait_ge(edges_loaded, 16 * plan.edge_loads)
                    dve.wait_ge(const_ready, 12)
                    dve.wait_ge(loaded, 16 * n_loads)
                    w_flat = w_qkv[:, :, :].rearrange("p k n -> p (k n)")
                    link(v.tensor_scalar(w_power[:, :], w_flat.bitcast(I32), 0x7F800000, None, ALU.bitwise_and))
                    v.reduce_max(w_peak[:, :], w_power[:, :].bitcast(F32), axis=AX.X).then_inc(w_peak_ready, 1)
                    v.tensor_scalar(work_i[:, 0, :], edges[:, 1, :], 2, P - 1, ALU.logical_shift_right, ALU.bitwise_and)
                    link(v.tensor_scalar(work_i[:, 1, :], edges[:, 1, :], 9, 2, ALU.logical_shift_right, ALU.logical_shift_left))
                    link(v.tensor_copy(dst_lo[:, :], work_i[:, 0, :]))
                    v.tensor_copy(dst_hi[:, :], work_i[:, 1, :])
                    link(v.tensor_copy(edges_f[:, :, :], edges[:, :, :]))
                    link(v.tensor_scalar(work_i[:, 0, :], edges[:, 1, :], ROWS - 1, None, ALU.bitwise_and))
                    link(v.tensor_copy(member[:, :], work_i[:, 0, :]))
                    v.tensor_tensor(dst_hi[:, :], dst_hi[:, :], member[:, :], ALU.add)
                    link(v.tensor_tensor(self_lo[:, :], edges_f[:, 0, :], edges_f[:, 1, :], ALU.is_equal))
                    link(v.scalar_tensor_tensor(self_lo[:, :], dst_lo[:, :], 1.0, self_lo[:, :], ALU.add, ALU.mult))
                    v.tensor_copy(lo_pair[:, :, 0], dst_lo[:, :])
                    v.tensor_scalar(lo_pair[:, :, 1], self_lo[:, :], -1.0, None, ALU.add)
                    link(v.tensor_tensor(apart[:, :], edges_f[:, 0, :], edges_f[:, 1, :], ALU.not_equal))
                    link(v.tensor_scalar(work_i[:, :, :], edges[:, :, :], 1, None, ALU.bitwise_and))
                    link(v.tensor_copy(odd[:, :, 1, :], work_i[:, :, :]))
                    link(v.tensor_scalar(odd[:, :, 0, :], odd[:, :, 1, :], -1.0, 1.0, ALU.mult, ALU.add))
                    link(v.tensor_scalar(place[:, :], place[:, :], 16, 0x40000000, ALU.logical_shift_left, ALU.bitwise_or))
                    for i in range(2):
                        link(v.tensor_tensor(edges[:, i, :], edges[:, i, :], place[:, :], ALU.bitwise_or))
                    for m in (BY_SOURCE, BY_TARGET):
                        for g in range(GROUPS):
                            at = m * GROUPS + g
                            link(v.tensor_tensor(member[:, :], apart[:, :], odd[:, m, g, :], ALU.mult))
                            v.reduce_sum(counts[:, at:at + 1], member[:, :], axis=AX.X).then_inc(counted, 1)
                            dve.wait_ge(counted, at + 1)
                            for i in range(2):
                                v.tensor_tensor(stock[:, m, g, i, :], edges[:, i, :].bitcast(F32), member[:, :], ALU.mult).then_inc(stocked, 1)
                            dve.wait_ge(stocked, 2 * at + 2)
                    dve.wait_ge(w_peaks_ready, 1)
                    link(v.tensor_scalar(unscale[:, :], w_peaks[:, :], 2.0 ** -100, 2.0 ** -13, ALU.max, ALU.mult))
                    link(v.reciprocal(w_scale[:, :], unscale[:, :]))
                    link(v.tensor_scalar(w_flat, w_flat, w_scale[:, 0:1], None, ALU.mult))
                    link(v.tensor_copy(w_qkv_hi[:, :, :], w_qkv[:, :, :]))
                    link(v.tensor_tensor(w_qkv_lo[:, :, :], w_qkv[:, :, :], w_qkv_hi[:, :, :], ALU.subtract))
                    dve.wait_ge(most_ready, 1)
                    link(v.tensor_scalar(most[:, :], most[:, :], 1.0, None, ALU.max))
                    link(v.reduce_max(longest[:, :], most[:, :].rearrange("p (m g) -> p m g", g=GROUPS), axis=AX.X))
                    link(v.tensor_scalar(turns_f[:, :], longest[:, :], 8.0, -5.0, ALU.max, ALU.add))
                    link(v.tensor_copy(more_turns[:, :], turns_f[:, :]))
                    link(v.tensor_scalar(more_turns[:, :], more_turns[:, :], 2, None, ALU.logical_shift_right))
                    v.tensor_scalar(rounds_f[:, 0:1], longest[:, BY_TARGET:BY_TARGET + 1], 7.0, None, ALU.add)
                    link(v.tensor_scalar(rounds_f[:, 1:2], longest[:, BY_TARGET:BY_TARGET + 1], 7.0, None, ALU.add))
                    link(v.tensor_copy(rounds[:, :], rounds_f[:, :]))
                    link(v.tensor_scalar(rounds[:, :], rounds[:, :], 3, None, ALU.logical_shift_right))
                    link(v.tensor_copy(rounds_f[:, :], rounds[:, :]))
                    v.tensor_scalar(rounds_f[:, 0:1], rounds_f[:, 0:1], float(BESIDE), 2.0, ALU.min, ALU.max)
                    link(v.tensor_scalar(rounds_f[:, 1:2], rounds_f[:, 1:2], float(-BESIDE), 1.0, ALU.add, ALU.max))
                    link(v.tensor_copy(rounds[:, :], rounds_f[:, :]))

        end_part()

        with ExitStack() as part:
            two = range(2)
            xb = [sb(f"a_x{u}", [P, ROWS, D], where=part) for u in two]
            stats = [sb(f"a_stats{u}", [P, ROWS, 6], where=part) for u in two]
            moments = [sb(f"a_moments{u}", [P, ROWS, 2], where=part) for u in two]
            std = [sb(f"a_std{u}", [P, ROWS], where=part) for u in two]
            rstd = [sb(f"a_rstd{u}", [P, ROWS], where=part) for u in two]
            shift = [sb(f"a_shift{u}", [P, ROWS], where=part) for u in two]
            hn = [sb(f"a_hn{u}", [P, ROWS, D], where=part) for u in two]
            ht = [sb(f"a_ht{u}", [P, KC, TILE], where=part) for u in two]
            h1 = [sb(f"h1_{u}", [P, KC, TILE], where=part) for u in two]
            zero = sb("zero", [P, 2 * WIDE], where=part)
            third = HIST // 2
            hot_hi = [sb(f"hot_hi{w}", [P, third, NT * ROWS], F16, where=part) for w in two]
            hot_lo = [sb(f"hot_lo{w}", [P, third, 2, P], F16, where=part) for w in two]
            bn_stats = sb("bn_stats", [P, KC, NT * 6], where=part)
            bn_moments = sb("bn_moments", [P, KC, 2], where=part)
            bn_scale = sb("bn_scale", [P, KC], where=part)
            bn_shift = sb("bn_shift", [P, KC], where=part)
            x_loaded = [sem(f"a_x_loaded{u}") for u in two]
            stats_ready = [sem(f"a_stats_ready{u}") for u in two]
            moments_ready = [sem(f"a_moments_ready{u}") for u in two]
            std_ready = [sem(f"a_std_ready{u}") for u in two]
            rstd_ready = [sem(f"a_rstd_ready{u}") for u in two]
            shift_ready = [sem(f"a_shift_ready{u}") for u in two]
            hn_ready = [sem(f"a_hn_ready{u}") for u in two]
            turned = [sem(f"a_turned{u}") for u in two]
            ht_ready = [sem(f"a_ht_ready{u}") for u in two]
            product_ready = [sem(f"a_product_ready{u}") for u in two]
            h1_ready = [sem(f"a_h1_ready{u}") for u in two]
            h1_counted = [sem(f"a_h1_counted{u}") for u in two]
            h1_stored = [pool_dma_sem(f"a_h1_stored{u}") for u in two]
            hot_ready = [sem(f"hot_ready{w}") for w in two]
            hot_used = [sem(f"hot_used{w}") for w in two]
            zeroed = pool_dma_sem("acc_zeroed")
            zero_ready = sem("zero_ready")
            hist_ps = [part.enter_context(nc.psum_tensor(f"hist_ps{i}", [P, NT * ROWS], F32)) for i in two]

            with ExitStack() as inner, nc.Block() as block:
                turn_ps = [inner.enter_context(nc.psum_tensor(f"a_turn_ps{u}", [P, KC * TILE], F32)) for u in two]
                h1_ps = inner.enter_context(nc.psum_tensor("a_h1_ps", [P, KC * TILE], F32))

                @block.sync
                def _(sp):
                    def step(at):
                        if (here := at(0)) is None:
                            return
                        i, u = here
                        tile = i * 2 + u
                        sp.wait_ge(hn_ready[u], i)
                        if isinstance(tile, int) and tile == NT - 1:
                            rows = x[tile * TILE:plan.n, :].rearrange("(p r) d -> p (r d)", r=ROWS)
                            sp.dma_start(xb[u][0:plan.last_p, :, :].rearrange("p r d -> p (r d)"), rows).then_inc(x_loaded[u], 16)
                        else:
                            sp.dma_start(xb[u][:, :, :].rearrange("p r d -> p (r d)"), row_block(x, tile)).then_inc(x_loaded[u], 16)

                    over_tiles(sp, plan, 0, step)

                @block.gpsimd
                def _(pool):
                    pool.memset(zero[:, :], 0.0).then_inc(zero_ready, 1)
                    pool.wait_ge(zero_ready, 1)

                    def step(at):
                        if at(3) is None:
                            return
                        i, u = at(3)
                        tile = i * 2 + u
                        hold(pool, h1_ready[u], i + 1)
                        pool.dma_start(h1_table[bass.ds(tile * P, P), :], h1[u][:, :, :].rearrange("p k c -> p (k c)")).then_inc(h1_stored[u], 16)

                    over_tiles(pool, plan, 3, step)
                    for u in two:
                        pool.wait_ge(h1_stored[u], 16 * (NT // 2))
                    for table, width in ((acc_table, WIDE), (agg_table, D)):
                        pool.dma_start(table[TAB:TAB + 2 * P, :].rearrange("(p r) d -> p (r d)", p=P), zero[:, 0:2 * width]).then_inc(zeroed, 16)
                    pool.wait_ge(zeroed, 32)

                @block.scalar
                def _(act):
                    def step(at):
                        if at(3) is not None:
                            i, u = at(3)
                            act.wait_ge(product_ready[u], i + 1)
                            act.wait_ge(h1_stored[u], 16 * i)
                            act.wait_ge(h1_counted[u], i)
                            for oc in range(KC):
                                last = nc.scalar.activation(h1[u][:, oc, :], h1_ps[:, oc * TILE:(oc + 1) * TILE],
                                                            ACT.Identity, bias=bn_in[:, 0, oc:oc + 1])
                            last.then_inc(h1_ready[u], 1)
                        if at(1) is not None:
                            i, u = at(1)
                            act.wait_ge(turned[u], i + 1)
                            act.wait_ge(product_ready[u], i)
                            for kc in range(KC):
                                last = nc.scalar.activation(ht[u][:, kc, :], turn_ps[u][:, kc * TILE:(kc + 1) * TILE], ACT.Copy)
                            last.then_inc(ht_ready[u], 1)
                        if at(0) is not None:
                            i, u = at(0)
                            act.wait_ge(moments_ready[u], i + 1)
                            act.wait_ge(shift_ready[u], i)
                            nc.scalar.activation(std[u][:, :], moments[u][:, :, 1], ACT.Sqrt, bias=eps_col[:, 0:1]).then_inc(std_ready[u], 1)
                            act.wait_ge(shift_ready[u], i + 1)
                            act.wait_ge(turned[u], i)
                            for j in range(ROWS):
                                last = nc.scalar.activation(hn[u][:, j, :], xb[u][:, j, :], ACT.Relu,
                                                            bias=shift[u][:, j:j + 1], scale=rstd[u][:, j:j + 1])
                            last.then_inc(hn_ready[u], 1)

                    over_tiles(act, plan, 3, step)

                @block.tensor
                def _(pe):
                    def step(at):
                        if at(1) is not None:
                            i, u = at(1)
                            tile = i * 2 + u
                            fixed = isinstance(tile, int)
                            for w in two:
                                pe.wait_ge(hot_ready[w], tile + 1)
                                for c in range(third):
                                    first = fixed and tile == 0 and w == 0 and c == 0
                                    end = fixed and tile == NT - 1 and w == 1 and c == third - 1
                                    for b in two:
                                        last = nc.tensor.matmul(hist_ps[b][:, :], hot_lo[w][:, c, b, :], hot_hi[w][:, c, :],
                                                                start=first, stop=end)
                                last.then_inc(hot_used[w], 1)
                            pe.wait_ge(hn_ready[u], i + 1)
                            pe.wait_ge(ht_ready[u], i)
                            for kc in range(KC):
                                for j in range(ROWS):
                                    last = nc.tensor.transpose(turn_ps[u][:, kc * TILE + j * P:kc * TILE + (j + 1) * P],
                                                               hn[u][:, j, kc * P:(kc + 1) * P], ident[:, :])
                            last.then_inc(turned[u], 1)
                        if at(2) is not None:
                            i, u = at(2)
                            pe.wait_ge(ht_ready[u], i + 1)
                            pe.wait_ge(h1_ready[1 - u], i + u)
                            for oc in range(KC):
                                for kc in range(KC):
                                    last = nc.tensor.matmul(h1_ps[:, oc * TILE:(oc + 1) * TILE], w1_t[:, kc, oc * P:(oc + 1) * P],
                                                            ht[u][:, kc, :], start=kc == 0, stop=kc == KC - 1)
                            last.then_inc(product_ready[u], 1)

                    over_tiles(pe, plan, 2, step)

                @block.vector
                def _(dve):
                    v = nc.vector

                    def one_hots(tile, w):
                        hold(dve, hot_used[w], tile)
                        for c in range(third):
                            col = bass.ds(tile * HIST + (w * third + c), 1)
                            v.tensor_scalar(hot_hi[w][:, c, :], lane[:, 0:NT * ROWS], dst_hi[:, col], None, ALU.is_equal)
                        last = v.tensor_tensor(hot_lo[w][:, :, :, :].rearrange("p c b q -> p (c b) q"),
                                               lane[:, 0:P].unsqueeze(1).to_broadcast([P, 2 * third, P]),
                                               lo_pair[:, bass.ds(tile * HIST + w * third, third), :].rearrange("p c b -> p (c b)")
                                               .unsqueeze(2).to_broadcast([P, 2 * third, P]), ALU.is_equal)
                        last.then_inc(hot_ready[w], 1)

                    def step(at):
                        if at(0) is not None:
                            i, u = at(0)
                            tile = i * 2 + u
                            dve.wait_ge(x_loaded[u], 16 * i + 16)
                            dve.wait_ge(hn_ready[u], i)
                            row_moments(v, dve, hold, xb[u], stats[u], moments[u], stats_ready[u], moments_ready[u], i)
                            one_hots(tile, 0)
                            row_scales(v, dve, moments[u], std[u], rstd[u], shift[u],
                                       std_ready[u], rstd_ready[u], shift_ready[u], i)
                        if at(0) is not None:
                            one_hots(tile, 1)
                        if at(4) is not None:
                            i, u = at(4)
                            t2 = i * 2 + u
                            hold(dve, h1_ready[u], i + 1)
                            for oc in range(KC):
                                seen = h1[u][:, oc, :]
                                if isinstance(t2, int) and t2 == NT - 1:
                                    seen = seen.rearrange("p (j q) -> p j q", j=ROWS)[:, :, 0:plan.last_p]
                                last = v.bn_stats(bn_stats[:, oc, bass.ds(t2 * 6, 6)], seen)
                            last.then_inc(h1_counted[u], 1)

                    over_tiles(dve, plan, 4, step)

            hb = [sb(f"hb{u}", [P, KC, TILE], where=part) for u in two]
            mix = [sb(f"mix{u}", [P, ROWS, D], where=part) for u in two]
            y_out = [sb(f"y_out{u}", [P, ROWS, D], where=part) for u in two]
            agg_out = [sb(f"agg_out{u}", [P, ROWS, D], where=part) for u in two]
            self_weight = sb("self_weight", [P, NT * ROWS], where=part)
            h1_loaded = [sem(f"b_h1_loaded{u}") for u in two]
            hb_ready = [sem(f"hb_ready{u}") for u in two]
            mix_product = [sem(f"mix_product{u}") for u in two]
            mix_ready = [sem(f"mix_ready{u}") for u in two]
            y_ready = [sem(f"y_ready{u}") for u in two]
            agg_ready = [sem(f"agg_ready{u}") for u in two]
            y_stored = [sem(f"y_stored{u}") for u in two]
            agg_stored = [pool_dma_sem(f"agg_stored{u}") for u in two]
            best = sb("mix_best", [P, GROUPS, 2, 8], where=part)
            empty = sb("mix_empty", [P, 2 * GROUPS, USED], where=part)
            nodes_f = sb("mix_nodes_f", [P, 2 * GROUPS, USED], where=part)
            best_ready = sem("mix_best_ready")
            replaced = sem("mix_best_replaced")
            packing = sem("mix_packing_chain")
            bn_ready = sem("bn_ready")
            b_chain = sem("b_chain")
            roots_ready = sem("roots_ready")

            with ExitStack() as inner, nc.Block() as block:
                mix_ps = [inner.enter_context(nc.psum_tensor(f"mix_ps{u}", [P, ROWS * D], F32)) for u in two]

                @block.sync
                def _(sp):
                    def step(at):
                        i, u = at(0)
                        sp.wait_ge(hb_ready[u], i)
                        sp.dma_start(h1[u][:, :, :].rearrange("p k c -> p (k c)"),
                                     h1_table[bass.ds((i * 2 + u) * P, P), :]).then_inc(h1_loaded[u], 16)

                    over_tiles(sp, plan, 0, step)

                @block.scalar
                def _(act):
                    act.wait_ge(b_chain, 4)
                    nc.scalar.activation(dinv[:, :], dinv[:, :], ACT.Sqrt).then_inc(roots_ready, 1)
                    nc.scalar.activation(bn_scale[:, :], bn_moments[:, :, 1], ACT.Sqrt, bias=eps_col[:, 0:1]).then_inc(roots_ready, 1)
                    act.wait_ge(bn_ready, 1)

                    def step(at):
                        if at(3) is not None:
                            i, u = at(3)
                            act.wait_ge(y_ready[u], i + 1)
                            act.dma_start(row_block(y_table, i * 2 + u), y_out[u][:, :, :].rearrange("p r d -> p (r d)")).then_inc(y_stored[u], 16)
                        if at(0) is not None:
                            i, u = at(0)
                            act.wait_ge(h1_loaded[u], 16 * i + 16)
                            act.wait_ge(mix_product[u], i)
                            for kc in range(KC):
                                last = nc.scalar.activation(hb[u][:, kc, :], h1[u][:, kc, :], ACT.Relu,
                                                            bias=bn_shift[:, kc:kc + 1], scale=bn_scale[:, kc:kc + 1])
                            last.then_inc(hb_ready[u], 1)
                        if at(2) is not None:
                            i, u = at(2)
                            tile = i * 2 + u
                            hold(act, mix_ready[u], i + 1)
                            hold(act, agg_ready[u], i)
                            hold(act, y_stored[u], 16 * i)
                            for j in range(ROWS):
                                last = nc.scalar.activation(y_out[u][:, j, :], mix[u][:, j, :], ACT.Copy,
                                                            scale=dinv[:, bass.ds(tile * ROWS + j, 1)])
                            last.then_inc(y_ready[u], 1)

                    over_tiles(act, plan, 3, step)
                    for u in two:
                        act.wait_ge(y_stored[u], 16 * (NT // 2))

                @block.tensor
                def _(pe):
                    def step(at):
                        i, u = at(0)
                        pe.wait_ge(hb_ready[u], i + 1)
                        pe.wait_ge(mix_ready[u], i)
                        for j in range(ROWS):
                            for kc in range(KC):
                                last = nc.tensor.matmul(mix_ps[u][:, j * D:(j + 1) * D], hb[u][:, kc, j * P:(j + 1) * P],
                                                        w_mix[:, kc, :], start=kc == 0, stop=kc == KC - 1)
                        last.then_inc(mix_product[u], 1)

                    over_tiles(pe, plan, 0, step)

                @block.vector
                def _(dve):
                    v = nc.vector
                    v.tensor_scalar(dinv[:, :], hist_ps[0][:, :], 1.0, None, ALU.add).then_inc(b_chain, 1)
                    v.tensor_copy(n_self[:, :], hist_ps[1][:, :]).then_inc(b_chain, 1)
                    for oc in range(KC):
                        v.bn_aggr(bn_moments[:, oc, :], bn_stats[:, oc, :]).then_inc(b_chain, 1)
                    dve.wait_ge(roots_ready, 2)
                    v.reciprocal(dinv[:, :], dinv[:, :]).then_inc(b_chain, 1)
                    v.reciprocal(bn_scale[:, :], bn_scale[:, :]).then_inc(b_chain, 1)
                    dve.wait_ge(b_chain, 6)
                    v.tensor_scalar(self_weight[:, :], n_self[:, :], 1.0, None, ALU.add)
                    v.tensor_tensor(bn_scale[:, :], bn_scale[:, :], bn_in[:, 1, :], ALU.mult).then_inc(b_chain, 1)
                    dve.wait_ge(b_chain, 7)
                    v.scalar_tensor_tensor(bn_shift[:, :], bn_moments[:, :, 0], -1.0, bn_scale[:, :], ALU.mult, ALU.mult).then_inc(b_chain, 1)
                    dve.wait_ge(b_chain, 8)
                    v.tensor_tensor(bn_shift[:, :], bn_shift[:, :], bn_in[:, 2, :], ALU.add).then_inc(bn_ready, 1)

                    def step(at):
                        i, u = at(0)
                        tile = i * 2 + u
                        dve.wait_ge(mix_product[u], i + 1)
                        dve.wait_ge(y_ready[u], i)
                        v.tensor_tensor(mix[u][:, :, :], mix_ps[u][:, :].rearrange("p (j d) -> p j d", j=ROWS),
                                        b_mix[:, :].unsqueeze(1).to_broadcast([P, ROWS, D]), ALU.add).then_inc(mix_ready[u], 1)

                    def pack_by_target(at, i):
                        for n in range(4):
                            g, end = divmod(n, 2)
                            left = stock[:, BY_TARGET, g, end, :]
                            if not isinstance(i, int) or i * 4 + n > 0:
                                hold(dve, replaced, i * 4 + n)
                            v.max(out=best[:, g, end, :], in_=left).then_inc(best_ready, 1)
                            hold(dve, best_ready, i * 4 + (n + 1))
                            v.tensor_copy(packed_i[BY_TARGET][:, end, g, bass.ds(at * 8, 8)], best[:, g, end, :].bitcast(I32))
                            v.match_replace(out=left, in_to_replace=best[:, g, end, :], in_values=left,
                                            imm_value=0.0).then_inc(replaced, 1)
                            if n == 1:
                                yield

                    def pair(i, rounds_too):
                        packing_steps = pack_by_target(i, i) if rounds_too else None
                        for u in two:
                            step(lambda l: (i, u))
                            if rounds_too:
                                next(packing_steps, None)

                    beside = dve.value_load(rounds[0:1, 0:1], min_val=2, max_val=BESIDE)
                    after = dve.value_load(rounds[0:1, 1:2], min_val=1, max_val=max(2, -(-COLS // 8) - BESIDE))
                    pair(0, True)
                    with dve.Fori(1, beside) as i:
                        pair(i, True)
                    with dve.Fori(beside, NT // 2) as i:
                        pair(i, False)
                    with dve.Fori(0, after) as i:
                        for _ in pack_by_target(i + BESIDE, i + beside):
                            pass
                    hold(dve, replaced, (beside + after) * 4)
                    done = [0]

                    def link(ins):
                        done[0] += 1
                        ins.then_inc(packing, 1)
                        dve.wait_ge(packing, done[0])

                    finish_packing(v, link, BY_TARGET, empty, nodes_f)

                @block.gpsimd
                def _(pool):
                    def step(at):
                        i, u = at(0)
                        tile = i * 2 + u
                        hold(pool, y_ready[u], i + 1)
                        hold(pool, agg_stored[u], 16 * i)
                        nc.gpsimd.tensor_tensor(agg_out[u][:, :, :], y_out[u][:, :, :],
                                                self_weight[:, bass.ds(tile * ROWS, ROWS)].unsqueeze(2).to_broadcast([P, ROWS, D]),
                                                ALU.mult).then_inc(agg_ready[u], 1)
                        hold(pool, agg_ready[u], i + 1)
                        pool.dma_start(row_block(agg_table, tile), agg_out[u][:, :, :].rearrange("p r d -> p (r d)")).then_inc(agg_stored[u], 16)

                    over_tiles(pool, plan, 0, step)
                    for u in two:
                        pool.wait_ge(agg_stored[u], 16 * (NT // 2))

        end_part()

        eight = range(SLOTS)

        def column_parts(name, key, where):
            return {
                "key": key,
                "ends": [sb(f"{name}_ends{k}", [P, 2], I32, where) for k in eight],
                "keys": [sb(f"{name}_keys{k}", [P, 2], F32, where) for k in eight],
                "same": [sb(f"{name}_same{k}", [P, P], F32, where) for k in range(4)],
                "rank_of": [sb(f"{name}_rank_of{k}", [P, P], F32, where) for k in range(2)],
                "rank": [sb(f"{name}_rank{k}", [P, 1], F32, where) for k in eight],
                "leads": [sb(f"{name}_leads{k}", [P, 1], F32, where) for k in eight],
                "goal": [sb(f"{name}_goal{k}", [P, 1], I32, where) for k in eight],
                "across": [where.enter_context(nc.psum_tensor(f"{name}_across{k}", [P, 512], F32)) for k in range(2)],
                "staged": sem(f"{name}_staged"),
                "across_ready": sem(f"{name}_across_ready"),
                "ranked": sem(f"{name}_ranked"),
                "leads_ready": sem(f"{name}_leads_ready"),
                "goal_ready": sem(f"{name}_goal_ready"),
                "scattered": [pool_dma_sem(f"{name}_scattered{k}") for k in eight],
            }

        def number(column):
            i, k = column
            return i * SLOTS + (k + 1)

        def wait_past(eng, s, value):
            if not isinstance(value, int) or value > 0:
                eng.wait_ge(s, value)

        def load_turns(eng, key):
            return eng.value_load(more_turns[0:1, key:key + 1], min_val=0, max_val=plan.most_turns - 2) + 2

        def stage_column(dve, c, column):
            i, k = column
            g, key = k % GROUPS, c["key"]
            at = bass.ds(i * (SLOTS // GROUPS) + k // GROUPS, 1)
            hold(dve, c["scattered"][k], i * 16)
            nc.vector.tensor_copy(c["ends"][k][:, :], packed_i[key][:, :, g, at].rearrange("p a o -> p (a o)"))
            nc.vector.tensor_copy(c["keys"][k][:, 0:1], packed_f[key][:, g, at])
            nc.vector.tensor_scalar(c["keys"][k][:, 1:2], packed_f[key][:, g, at], spare[:, 1 + k % 2:2 + k % 2], None,
                                    ALU.subtract).then_inc(c["staged"], 1)

        def keys_across(pe, c, column):
            i, k = column
            pe.wait_ge(c["staged"], number(column))
            wait_past(pe, c["ranked"], number(column) - 2)
            nc.tensor.matmul(c["across"][k % 2][:, 0:P], c["keys"][k][:, 0:1].to_broadcast([P, P]), ident[:, :],
                             start=True, stop=True).then_inc(c["across_ready"], 1)

        def compare_keys(dve, c, column, write_same):
            i, k = column
            across, keys = c["across"][k % 2][:, 0:P], c["keys"][k]
            wait_past(dve, c["ranked"], number(column) - 2)
            dve.wait_ge(c["across_ready"], number(column))
            write_same(across, keys[:, 0:1], k)
            nc.vector.scalar_tensor_tensor(c["rank_of"][k % 2][:, :], across, keys[:, 0:1], earlier[:, :], ALU.is_equal, ALU.mult,
                                           accum_out=c["rank"][k][:, 0:1]).then_inc(c["ranked"], 1)

        def find_goals(act, c, column):
            i, k = column
            n = number(column)
            act.wait_ge(c["ranked"], n)
            nc.scalar.activation(c["leads"][k][:, :], c["rank"][k][:, :], ACT.Relu, bias=one_col[:, 0:1], scale=-1.0).then_inc(c["leads_ready"], 1)
            act.wait_ge(c["leads_ready"], n)
            nc.scalar.activation(c["goal"][k][:, :], c["leads"][k][:, :], ACT.Identity, bias=spare[:, 1 + k % 2:2 + k % 2],
                                 scale=c["keys"][k][:, 1:2]).then_inc(c["goal_ready"], 1)

        def gather(rows, table, index):
            return nc.gpsimd.indirect_dma_start(out=rows, out_offset=None, in_=table,
                                                in_offset=bass.IndirectOffsetOnAxis(ap=index, axis=0))

        def scatter(table, index, rows, **how):
            return nc.gpsimd.indirect_dma_start(out=table, out_offset=bass.IndirectOffsetOnAxis(ap=index, axis=0),
                                                in_=rows, in_offset=None, **how)

        with ExitStack() as part, nc.Block() as block:
            c = column_parts("gcn", BY_TARGET, part)
            got = [sb(f"gcn_got{k}", [P, D], where=part) for k in eight]
            summed = [sb(f"gcn_summed{k}", [P, D], where=part) for k in eight]
            sum_ps = [part.enter_context(nc.psum_tensor(f"gcn_sum_ps{k}", [P, 512], F32)) for k in range(2)]
            gathered = [pool_dma_sem(f"gcn_gathered{k}") for k in eight]
            sum_ready = sem("gcn_sum_ready")
            best = sb("gcn_best", [P, GROUPS, 2, 8], where=part)
            empty = sb("gcn_empty", [P, 2 * GROUPS, USED], where=part)
            nodes_f = sb("gcn_nodes_f", [P, 2 * GROUPS, USED], where=part)
            best_ready = sem("gcn_best_ready")
            replaced = sem("gcn_best_replaced")
            packing = sem("gcn_packing_chain")
            summed_ready = sem("gcn_summed_ready")

            @block.gpsimd
            def _(pool):
                turns = load_turns(pool, BY_TARGET)

                def step(at):
                    if (col := at(1)) is not None:
                        i, k = col
                        hold(pool, c["staged"], number(col))
                        gather(got[k][:, :], y_table, c["ends"][k][:, 0:1]).then_inc(gathered[k], 16)
                    if (col := at(4)) is not None:
                        i, k = col
                        hold(pool, summed_ready, number(col))
                        if (two_back := at(6)) is not None:
                            hold(pool, c["scattered"][two_back[1]], two_back[0] * 16 + 16)
                        hold(pool, c["goal_ready"], number(col))
                        scatter(agg_table, c["goal"][k][:, 0:1], summed[k][:, :], compute_op=ALU.add).then_inc(c["scattered"][k], 16)

                over_columns(pool, turns, 4, step)
                for k in eight:
                    hold(pool, c["scattered"][k], turns * 16)

            @block.vector
            def _(dve):
                turns = load_turns(dve, BY_TARGET)

                def write_same(across, key, k):
                    nc.vector.tensor_scalar(c["same"][k % 4][:, :], across, key, None, ALU.is_equal)

                def step(at):
                    if (col := at(0)) is not None:
                        stage_column(dve, c, col)
                    if (col := at(1)) is not None:
                        wait_past(dve, sum_ready, number(col) - 4)
                        compare_keys(dve, c, col, write_same)
                    if (col := at(0)) is not None and col[1] % 2 == 0:
                        pack_by_source(col[0], col[1] // 2)

                def pack_by_source(i, n):
                    g, end = divmod(n, 2)
                    left = stock[:, BY_SOURCE, g, end, :]
                    if not isinstance(i, int) or i > 0:
                        hold(dve, replaced, i * 4 + (n - 3))
                    nc.vector.max(out=best[:, g, end, :], in_=left).then_inc(best_ready, 1)
                    hold(dve, best_ready, i * 4 + (n + 1))
                    nc.vector.tensor_copy(packed_i[BY_SOURCE][:, end, g, bass.ds(i * 8, 8)], best[:, g, end, :].bitcast(I32))
                    nc.vector.match_replace(out=left, in_to_replace=best[:, g, end, :], in_values=left,
                                            imm_value=0.0).then_inc(replaced, 1)

                over_columns(dve, turns, 1, step)
                hold(dve, replaced, turns * 4)
                done = [0]

                def link(ins):
                    done[0] += 1
                    ins.then_inc(packing, 1)
                    dve.wait_ge(packing, done[0])

                finish_packing(nc.vector, link, BY_SOURCE, empty, nodes_f)

            @block.tensor
            def _(pe):
                turns = load_turns(pe, BY_TARGET)

                def step(at):
                    if (col := at(0)) is not None:
                        keys_across(pe, c, col)
                    if (col := at(3)) is not None:
                        i, k = col
                        pe.wait_ge(c["ranked"], number(col))
                        pe.wait_ge(gathered[k], i * 16 + 16)
                        wait_past(pe, summed_ready, number(col) - 2)
                        nc.tensor.matmul(sum_ps[k % 2][:, 0:D], c["same"][k % 4][:, :], got[k][:, :],
                                         start=True, stop=True).then_inc(sum_ready, 1)

                over_columns(pe, turns, 3, step)

            @block.scalar
            def _(act):
                turns = load_turns(act, BY_TARGET)

                def step(at):
                    if (col := at(2)) is not None:
                        i, k = col
                        act.wait_ge(sum_ready, number(col))
                        nc.scalar.activation(summed[k][:, :], sum_ps[k % 2][:, 0:D], ACT.Copy).then_inc(summed_ready, 1)
                    if (col := at(0)) is not None:
                        find_goals(act, c, col)

                over_columns(act, turns, 2, step)

        end_part()

        with ExitStack() as part, nc.Block() as block:
            agg = [sb(f"c_agg{w}", [P, ROWS, D], where=part) for w in range(4)]
            xb = [sb(f"c_x{w}", [P, ROWS, D], where=part) for w in range(4)]
            x1 = [sb(f"c_x1_{u}", [P, ROWS, D], where=part) for u in two]
            stats = [sb(f"c_stats{u}", [P, ROWS, 6], where=part) for u in two]
            moments = [sb(f"c_moments{u}", [P, ROWS, 2], where=part) for u in two]
            std = [sb(f"c_std{u}", [P, ROWS], where=part) for u in two]
            rstd = [sb(f"c_rstd{u}", [P, ROWS], where=part) for u in two]
            shift = [sb(f"c_shift{u}", [P, ROWS], where=part) for u in two]
            hn = [sb(f"c_hn{u}", [P, ROWS, D], where=part) for u in two]
            ht_hi = [sb(f"c_ht_hi{u}", [P, KC, TILE], F16, where=part) for u in two]
            ht_lo = [sb(f"c_ht_lo{u}", [P, KC, TILE], F16, where=part) for u in two]
            qb = [sb(f"c_q{u}", [P, ROWS, 1, D], where=part) for u in two]
            kv = [sb(f"c_kv{u}", [P, ROWS, 2, D], where=part) for u in two]
            qk = [sb(f"c_qk{u}", [P, ROWS, D], where=part) for u in two]
            raw = [sb(f"c_raw{u}", [P, ROWS, H], where=part) for u in two]
            masked = [sb(f"c_masked{u}", [P, ROWS, H], where=part) for u in two]
            acc = [sb(f"c_acc{u}", [P, ROWS, WIDE], where=part) for u in two]
            has_self = sb("has_self", [P, NT * ROWS], where=part)
            no_self = sb("no_self", [P, NT * ROWS], where=part)
            loaded = [sem(f"c_loaded{w}") for w in range(4)]
            biased = sem("c_biased")
            scaled = sem("c_scaled")
            x1_ready = [sem(f"c_x1_ready{u}") for u in two]
            x1_stored = [sem(f"c_x1_stored{u}") for u in two]
            stats_ready = [sem(f"c_stats_ready{u}") for u in two]
            moments_ready = [sem(f"c_moments_ready{u}") for u in two]
            std_ready = [sem(f"c_std_ready{u}") for u in two]
            rstd_ready = [sem(f"c_rstd_ready{u}") for u in two]
            shift_ready = [sem(f"c_shift_ready{u}") for u in two]
            hn_ready = [sem(f"c_hn_ready{u}") for u in two]
            turned = sem("c_turned")
            hi_ready = sem("c_hi_ready")
            lo_ready = sem("c_lo_ready")
            product_ready = sem("c_product_ready")
            qkv_ready = sem("c_qkv_ready")
            qkv_stored = [sem(f"c_qkv_stored{u}") for u in two]
            qk_ready = sem("c_qk_ready")
            raw_ready = sem("c_raw_ready")
            masked_ready = sem("c_masked_ready")
            peak_ready = sem("c_peak_ready")
            own_ready = sem("c_own_ready")
            acc_stored = [sem(f"c_acc_stored{u}") for u in two]
            c_chain = sem("c_chain")
            turn_ps = part.enter_context(nc.psum_tensor("c_turn_ps", [P, KC * TILE], F32))
            qkv_ps = [part.enter_context(nc.psum_tensor(f"c_qkv_ps{i}", [P, ROWS * D], F32)) for i in range(3)]

            def tile_of(t):
                return t[0] * 2 + t[1]

            @block.sync
            def _(sp):
                def step(at):
                    if at(0) is not None:
                        i, w = at(0)[2:]
                        tile = tile_of(at(0))
                        pair, u = at(0)[:2]
                        wait_past(sp, x1_ready[u], pair - 1)
                        sp.dma_start(agg[w][:, :, :].rearrange("p r d -> p (r d)"), row_block(agg_table, tile)).then_inc(loaded[w], 16)
                        if isinstance(tile, int) and tile == NT - 1:
                            rows = x[tile * TILE:plan.n, :].rearrange("(p r) d -> p (r d)", r=ROWS)
                            sp.dma_start(xb[w][0:plan.last_p, :, :].rearrange("p r d -> p (r d)"), rows).then_inc(loaded[w], 16)
                        else:
                            sp.dma_start(xb[w][:, :, :].rearrange("p r d -> p (r d)"), row_block(x, tile)).then_inc(loaded[w], 16)
                    if at(3) is not None:
                        i, u = at(3)[:2]
                        sp.wait_ge(x1_ready[u], i + 1)
                        sp.dma_start(row_block(x1_table, tile_of(at(3))), x1[u][:, :, :].rearrange("p r d -> p (r d)")).then_inc(x1_stored[u], 16)
                    if at(6) is not None:
                        i, u = at(6)[:2]
                        tile = tile_of(at(6))
                        sp.wait_ge(qkv_ready, tile * 3 + 3)
                        for table, rows in ((q_table, qb), (kv_table, kv)):
                            sp.dma_start(row_block(table, tile), rows[u][:, :, :, :].rearrange("p r n d -> p (r n d)")).then_inc(qkv_stored[u], 16)
                    if at(7) is not None:
                        i, u = at(7)[:2]
                        tile = tile_of(at(7))
                        sp.wait_ge(peak_ready, tile + 1)
                        sp.wait_ge(own_ready, tile + 1)
                        sp.dma_start(row_block(acc_table, tile), acc[u][:, :, :].rearrange("p r w -> p (r w)")).then_inc(acc_stored[u], 16)

                over_tiles(sp, plan, 7, step, slots=4)
                for u in two:
                    sp.wait_ge(x1_stored[u], 16 * (NT // 2))
                    sp.wait_ge(qkv_stored[u], 32 * (NT // 2))
                    sp.wait_ge(acc_stored[u], 16 * (NT // 2))

            @block.gpsimd
            def _(pool):
                def step(at):
                    if at(2) is not None:
                        i, u, _, w = at(2)
                        hold(pool, scaled, tile_of(at(2)) + 1)
                        hold(pool, biased, tile_of(at(2)) + 1)
                        hold(pool, x1_stored[u], i * 16)
                        hold(pool, hn_ready[u], i)
                        nc.gpsimd.tensor_tensor(x1[u][:, :, :], agg[w][:, :, :], xb[w][:, :, :], ALU.add).then_inc(x1_ready[u], 1)
                    if at(5) is not None:
                        i, u = at(5)[:2]
                        tile = tile_of(at(5))
                        hold(pool, qkv_ready, tile * 3 + 2)
                        wait_past(pool, raw_ready, tile - 1)
                        nc.gpsimd.tensor_tensor(qk[u][:, :, :], qb[u][:, :, 0, :], kv[u][:, :, 0, :], ALU.mult).then_inc(qk_ready, 1)
                    if at(1) is not None:
                        i, w = at(1)[2:]
                        hold(pool, loaded[w], i * 32 + 32)
                        nc.gpsimd.tensor_tensor(xb[w][:, :, :], xb[w][:, :, :], b_agg[:, :].unsqueeze(1).to_broadcast([P, ROWS, D]),
                                                ALU.add).then_inc(biased, 1)

                over_tiles(pool, plan, 5, step, slots=4)

            @block.scalar
            def _(act):
                def step(at):
                    if at(6) is not None:
                        i, u = at(6)[:2]
                        tile = tile_of(at(6))
                        hold(act, qkv_ready, tile * 3 + 3)
                        hold(act, acc_stored[u], i * 16)
                        for j in range(ROWS):
                            last = nc.scalar.activation(acc[u][:, j, SUMS:WEIGHTS], kv[u][:, j, 1, :], ACT.Copy,
                                                        scale=n_self[:, bass.ds(tile * ROWS + j, 1)])
                        last.then_inc(own_ready, 1)
                    if at(3) is not None:
                        i, u = at(3)[:2]
                        tile = tile_of(at(3))
                        act.wait_ge(turned, tile + 1)
                        wait_past(act, product_ready, tile * 3 - 3)
                        for kc in range(KC):
                            last = nc.scalar.activation(ht_hi[u][:, kc, :], turn_ps[:, kc * TILE:(kc + 1) * TILE], ACT.Copy)
                        last.then_inc(hi_ready, 1)
                    if at(1) is not None:
                        i, w = at(1)[2:]
                        tile = tile_of(at(1))
                        hold(act, loaded[w], i * 32 + 32)
                        for j in range(ROWS):
                            last = nc.scalar.activation(agg[w][:, j, :], agg[w][:, j, :], ACT.Copy,
                                                        scale=dinv[:, bass.ds(tile * ROWS + j, 1)])
                        last.then_inc(scaled, 1)
                    if at(2) is not None:
                        i, u = at(2)[:2]
                        act.wait_ge(moments_ready[u], i + 1)
                        act.wait_ge(shift_ready[u], i)
                        nc.scalar.activation(std[u][:, :], moments[u][:, :, 1], ACT.Sqrt, bias=eps_col[:, 0:1]).then_inc(std_ready[u], 1)
                        act.wait_ge(shift_ready[u], i + 1)
                        wait_past(act, turned, tile_of(at(2)) - 1)
                        for j in range(ROWS):
                            last = nc.scalar.activation(hn[u][:, j, :], x1[u][:, j, :], ACT.Relu,
                                                        bias=shift[u][:, j:j + 1], scale=rstd[u][:, j:j + 1])
                        last.then_inc(hn_ready[u], 1)

                over_tiles(act, plan, 6, step, slots=4)

            @block.tensor
            def _(pe):
                def step(at):
                    if at(3) is not None:
                        i, u = at(3)
                        pe.wait_ge(hn_ready[u], i + 1)
                        wait_past(pe, lo_ready, tile_of(at(3)))
                        for kc in range(KC):
                            for j in range(ROWS):
                                last = nc.tensor.transpose(turn_ps[:, kc * TILE + j * P:kc * TILE + (j + 1) * P],
                                                           hn[u][:, j, kc * P:(kc + 1) * P], ident[:, :])
                        last.then_inc(turned, 1)
                    if at(4) is not None:
                        i, u = at(4)
                        tile = tile_of(at(4))
                        pe.wait_ge(hi_ready, tile + 1)
                        pe.wait_ge(lo_ready, tile + 1)
                        for n in range(3):
                            wait_past(pe, qkv_ready, tile * 3 - 2 + n)
                            for j in range(ROWS):
                                passes = [(h, w, kc) for kc in range(KC)
                                          for h, w in ((ht_hi, w_qkv_hi), (ht_hi, w_qkv_lo), (ht_lo, w_qkv_hi))]
                                for m, (h, w, kc) in enumerate(passes):
                                    last = nc.tensor.matmul(qkv_ps[n][:, j * D:(j + 1) * D], h[u][:, kc, j * P:(j + 1) * P],
                                                            w[:, kc, n * D:(n + 1) * D], start=m == 0, stop=m == len(passes) - 1)
                            last.then_inc(product_ready, 1)

                over_tiles(pe, plan, 4, step)

            @block.vector
            def _(dve):
                v = nc.vector
                v.tensor_scalar(has_self[:, :], n_self[:, :], 1.0, None, ALU.min).then_inc(c_chain, 1)
                dve.wait_ge(c_chain, 1)
                v.tensor_scalar(no_self[:, :], has_self[:, :], -1.0, -LOW, ALU.add, ALU.mult).then_inc(c_chain, 1)
                dve.wait_ge(c_chain, 2)
                v.tensor_scalar(has_self[:, :], has_self[:, :], SCALE, None, ALU.mult).then_inc(c_chain, 1)
                dve.wait_ge(c_chain, 3)

                def step(at):
                    if at(5) is not None:
                        i, u2 = at(5)[:2]
                        t2 = tile_of(at(5))
                        for n in range(3):
                            dve.wait_ge(product_ready, t2 * 3 + 1 + n)
                            if n == 0:
                                dve.wait_ge(qkv_stored[u2], i * 32)
                                wait_past(dve, qk_ready, t2 - 1)
                            if n == 2:
                                wait_past(dve, own_ready, t2 - 1)
                            goes = qb[u2][:, :, 0, :] if n == 0 else kv[u2][:, :, n - 1, :]
                            v.scalar_tensor_tensor(goes, qkv_ps[n][:, :].rearrange("p (j d) -> p j d", j=ROWS), unscale[:, 0:1],
                                                   b_qkv[:, n * D:(n + 1) * D].unsqueeze(1).to_broadcast([P, ROWS, D]),
                                                   ALU.mult, ALU.add).then_inc(qkv_ready, 1)
                    if at(3) is not None:
                        i, u = at(3)[:2]
                        tile = tile_of(at(3))
                        dve.wait_ge(hi_ready, tile + 1)
                        wait_past(dve, product_ready, tile * 3 - 3)
                        v.tensor_tensor(ht_lo[u][:, :, :].rearrange("p k n -> p (k n)"), turn_ps[:, :],
                                        ht_hi[u][:, :, :].rearrange("p k n -> p (k n)"), ALU.subtract).then_inc(lo_ready, 1)
                    if at(2) is not None:
                        i, u = at(2)[:2]
                        tile = tile_of(at(2))
                        dve.wait_ge(x1_ready[u], i + 1)
                        row_moments(v, dve, hold, x1[u], stats[u], moments[u], stats_ready[u], moments_ready[u], i)
                    if at(6) is not None:
                        i, u = at(6)[:2]
                        tile = tile_of(at(6))
                        dve.wait_ge(qk_ready, tile + 1)
                        v.reduce_sum(raw[u][:, :, :], qk[u][:, :, :].rearrange("p j (d h) -> p j h d", h=H),
                                     axis=AX.X).then_inc(raw_ready, 1)
                        hold(dve, raw_ready, tile + 1)
                        here = bass.ds(tile * ROWS, ROWS)
                        v.tensor_tensor(masked[u][:, :, :], raw[u][:, :, :], has_self[:, here].unsqueeze(2).to_broadcast([P, ROWS, H]),
                                        ALU.mult).then_inc(masked_ready, 1)
                        hold(dve, masked_ready, tile + 1)
                        hold(dve, acc_stored[u], i * 16)
                        v.tensor_copy(acc[u][:, :, WEIGHTS:WIDE], n_self[:, here].unsqueeze(2).to_broadcast([P, ROWS, H]))
                        v.tensor_tensor(acc[u][:, :, PEAKS:SUMS], masked[u][:, :, :], no_self[:, here].unsqueeze(2).to_broadcast([P, ROWS, H]),
                                        ALU.add).then_inc(peak_ready, 1)
                    if at(2) is not None:
                        i, u = at(2)[:2]
                        row_scales(v, dve, moments[u], std[u], rstd[u], shift[u],
                                   std_ready[u], rstd_ready[u], shift_ready[u], i)

                over_tiles(dve, plan, 6, step, slots=4)

        end_part()
        with ExitStack() as part, nc.Block() as block:
            c = column_parts("attend", BY_SOURCE, part)
            q_got = [sb(f"q_got{k}", [P, D], where=part) for k in eight]
            kv_got = [sb(f"kv_got{k}", [P, 2, D], where=part) for k in eight]
            row_got = [sb(f"row_got{k}", [P, H + WIDE], where=part) for k in eight]
            row_new = [sb(f"row_new{k}", [P, WIDE], where=part) for k in eight]
            top = [sb(f"top{k}", [P, H], where=part) for k in eight]
            below = [sb(f"below{k}", [P, 2, H], where=part) for k in eight]
            share = [sb(f"share{k}", [P, D + 2 * H], where=part) for k in eight]
            kept = [sb(f"kept{k}", [P, D + H], where=part) for k in two]
            qk = [sb(f"attend_qk{k}", [P, D], where=part) for k in two]
            differ = [sb(f"differ{k}", [P, P], BF16, where=part) for k in range(4)]
            low_col = sb("low_col", [P, 1], where=part)
            spread_ps = [part.enter_context(nc.psum_tensor(f"spread_ps{k}", [P, H * P], F32)) for k in two]
            sum_ps = [part.enter_context(nc.psum_tensor(f"attend_sum_ps{k}", [P, 512], F32)) for k in two]
            qkv_gathered = [pool_dma_sem(f"qkv_gathered{k}") for k in eight]
            row_gathered = [pool_dma_sem(f"row_gathered{k}") for k in eight]
            low_ready = sem("low_ready")
            qk_ready = sem("attend_qk_ready")
            score_ready = sem("score_ready")
            differ_ready = sem("differ_ready")
            spread_ready = sem("spread_ready")
            top_ready = sem("top_ready")
            peak_ready = sem("peak_ready")
            below_ready = sem("below_ready")
            weight_ready = sem("weight_ready")
            share_ready = sem("share_ready")
            kept_ready = sem("kept_ready")
            sum_ready = sem("attend_sum_ready")
            row_ready = sem("row_ready")

            @block.gpsimd
            def _(pool):
                turns = load_turns(pool, BY_SOURCE)

                def step(at):
                    if (col := at(6)) is not None:
                        i, k = col
                        hold(pool, row_ready, number(col))
                        hold(pool, c["goal_ready"], number(col))
                        scatter(acc_table, c["goal"][k][:, 0:1], row_new[k][:, :]).then_inc(c["scattered"][k], 16)
                    if (col := at(1)) is not None:
                        i, k = col
                        hold(pool, c["staged"], number(col))
                        gather(q_got[k][:, :], q_table, c["ends"][k][:, 0:1]).then_inc(qkv_gathered[k], 16)
                        gather(kv_got[k][:, :, :].rearrange("p n d -> p (n d)"), kv_table, c["ends"][k][:, 1:2]).then_inc(qkv_gathered[k], 16)
                    if (col := at(4)) is not None:
                        i, k = col
                        if (two_back := at(6)) is not None:
                            hold(pool, c["scattered"][two_back[1]], two_back[0] * 16 + 16)
                        gather(row_got[k][:, H:H + WIDE], acc_table, c["ends"][k][:, 0:1]).then_inc(row_gathered[k], 16)

                over_columns(pool, turns, 6, step)
                for k in eight:
                    hold(pool, c["scattered"][k], turns * 16)

            @block.vector
            def _(dve):
                turns = load_turns(dve, BY_SOURCE)
                v = nc.vector

                def write_same(across, key, k):
                    v.tensor_scalar(c["same"][k % 4][:, :], across, key, None, ALU.is_equal)

                def step(at):
                    if at(0) is not None:
                        stage_column(dve, c, at(0))
                    if (col := at(5)) is not None:
                        i, k = col
                        n = number(col)
                        dve.wait_ge(row_gathered[k], i * 16 + 16)
                        dve.wait_ge(top_ready, n)
                        v.tensor_tensor(row_new[k][:, PEAKS:SUMS], row_got[k][:, H:2 * H], top[k][:, :], ALU.max).then_inc(peak_ready, 1)
                        dve.wait_ge(peak_ready, n)
                        v.tensor_tensor(below[k][:, :, :], row_got[k][:, 0:2 * H].rearrange("p (n h) -> p n h", h=H),
                                        row_new[k][:, PEAKS:SUMS].unsqueeze(1).to_broadcast([P, 2, H]), ALU.subtract).then_inc(below_ready, 1)
                        dve.wait_ge(weight_ready, n)
                        v.tensor_tensor(share[k][:, 0:D].rearrange("p (d h) -> p d h", h=H),
                                        kv_got[k][:, 1, :].rearrange("p (d h) -> p d h", h=H),
                                        share[k][:, D:D + H].unsqueeze(1).to_broadcast([P, DH, H]), ALU.mult).then_inc(share_ready, 1)
                        wait_past(dve, sum_ready, n - 2)
                        v.tensor_tensor(kept[k % 2][:, :].rearrange("p (d h) -> p d h", h=H),
                                        row_got[k][:, H + SUMS:H + WIDE].rearrange("p (d h) -> p d h", h=H),
                                        share[k][:, D + H:D + 2 * H].unsqueeze(1).to_broadcast([P, DH + 1, H]), ALU.mult).then_inc(kept_ready, 1)
                    if (col := at(2)) is not None:
                        wait_past(dve, sum_ready, number(col) - 4)
                        wait_past(dve, differ_ready, number(col) - 4)
                        compare_keys(dve, c, col, write_same)
                    if (col := at(3)) is not None:
                        i, k = col
                        n = number(col)
                        dve.wait_ge(qkv_gathered[k], i * 32 + 32)
                        v.scalar_tensor_tensor(qk[k % 2][:, :], q_got[k][:, :], SCALE, kv_got[k][:, 0, :], ALU.mult,
                                               ALU.mult).then_inc(qk_ready, 1)
                        dve.wait_ge(qk_ready, n)
                        v.reduce_sum(row_got[k][:, 0:H], qk[k % 2][:, :].rearrange("p (d h) -> p h d", h=H), axis=AX.X).then_inc(score_ready, 1)
                    if (col := at(4)) is not None:
                        i, k = col
                        dve.wait_ge(spread_ready, number(col))
                        v.reduce_max(top[k][:, :], spread_ps[k % 2][:, :].rearrange("p (h e) -> p h e", h=H), axis=AX.X).then_inc(top_ready, 1)

                over_columns(dve, turns, 5, step)

            @block.tensor
            def _(pe):
                turns = load_turns(pe, BY_SOURCE)

                def step(at):
                    if (col := at(5)) is not None:
                        i, k = col
                        n = number(col)
                        pe.wait_ge(share_ready, n)
                        wait_past(pe, row_ready, n - 2)
                        nc.tensor.matmul(sum_ps[k % 2][:, 0:D + H], c["same"][k % 4][:, :], share[k][:, 0:D + H], start=True, stop=False)
                        pe.wait_ge(kept_ready, n)
                        nc.tensor.matmul(sum_ps[k % 2][:, 0:D + H], ident[:, :], kept[k % 2][:, :],
                                         start=False, stop=True).then_inc(sum_ready, 1)
                    if (col := at(1)) is not None:
                        keys_across(pe, c, col)
                    if (col := at(3)) is not None:
                        i, k = col
                        n = number(col)
                        pe.wait_ge(differ_ready, n)
                        pe.wait_ge(score_ready, n)
                        wait_past(pe, top_ready, n - 2)
                        half = H // 2
                        for b in range(2):
                            nc.tensor.matmul(spread_ps[k % 2][:, b * 512:(b + 1) * 512], ident_b[:, :],
                                             differ[k % 4][:, :].unsqueeze(1).to_broadcast([P, half, P]), start=True, stop=False)
                            for h in range(half):
                                at_h = b * half + h
                                last = nc.tensor.matmul(spread_ps[k % 2][:, at_h * P:(at_h + 1) * P],
                                                        row_got[k][:, at_h:at_h + 1].to_broadcast([P, P]), ident[:, :],
                                                        start=False, stop=h == half - 1)
                        last.then_inc(spread_ready, 1)

                over_columns(pe, turns, 5, step)

            @block.scalar
            def _(act):
                turns = load_turns(act, BY_SOURCE)
                nc.scalar.activation(low_col[:, :], eps_col[:, :], ACT.Copy, scale=0.0, bias=LOW).then_inc(low_ready, 1)
                act.wait_ge(low_ready, 1)

                def step(at):
                    if (col := at(5)) is not None:
                        i, k = col
                        act.wait_ge(below_ready, number(col))
                        nc.scalar.activation(share[k][:, D:D + 2 * H], below[k][:, :, :].rearrange("p n h -> p (n h)"),
                                             ACT.Exp).then_inc(weight_ready, 1)
                    if (col := at(5)) is not None:
                        i, k = col
                        act.wait_ge(sum_ready, number(col))
                        nc.scalar.activation(row_new[k][:, SUMS:WIDE], sum_ps[k % 2][:, 0:D + H], ACT.Copy).then_inc(row_ready, 1)
                    if (col := at(2)) is not None:
                        i, k = col
                        act.wait_ge(c["ranked"], number(col))
                        wait_past(act, spread_ready, number(col) - 4)
                        nc.scalar.activation(differ[k % 4][:, :], c["same"][k % 4][:, :], ACT.Identity,
                                             bias=low_col[:, 0:1], scale=-LOW).then_inc(differ_ready, 1)
                        find_goals(act, c, col)

                over_columns(act, turns, 5, step)

        end_part()

        with ExitStack() as part, nc.Block() as block:
            three = range(3)
            four = range(4)
            acc = [sb(f"e_acc{w}", [P, ROWS, WIDE], where=part) for w in four]
            x1 = [sb(f"e_x1_{w}", [P, ROWS, D], where=part) for w in four]
            total = [sb(f"e_total{u}", [P, ROWS, H], where=part) for u in two]
            mean = [sb(f"e_mean{u}", [P, ROWS, D], where=part) for u in two]
            ht = [sb(f"e_ht{u}", [P, KC, TILE], where=part) for u in two]
            result = [sb(f"e_result{w}", [P, ROWS, D], where=part) for w in four]
            loaded = [sem(f"e_loaded{w}") for w in four]
            x1_loaded = [sem(f"e_x1_loaded{w}") for w in four]
            total_ready = sem("e_total_ready")
            mean_ready = sem("e_mean_ready")
            turned = sem("e_turned")
            ht_ready = sem("e_ht_ready")
            product_ready = sem("e_product_ready")
            x1_biased = sem("e_x1_biased")
            result_ready = sem("e_result_ready")
            result_stored = [sem(f"e_result_stored{w}") for w in four]
            turn_ps = [part.enter_context(nc.psum_tensor(f"e_turn_ps{u}", [P, KC * TILE], F32)) for u in two]
            out_ps = [part.enter_context(nc.psum_tensor(f"e_out_ps{u}", [P, ROWS * D], F32)) for u in two]

            @block.sync
            def _(sp):
                def step(at):
                    if at(0) is not None:
                        i, w = at(0)[2:]
                        tile = tile_of(at(0))
                        wait_past(sp, mean_ready, tile - 3)
                        sp.dma_start(acc[w][:, :, :].rearrange("p r w -> p (r w)"), row_block(acc_table, tile)).then_inc(loaded[w], 16)
                        wait_past(sp, result_ready, tile - 3)
                        sp.dma_start(x1[w][:, :, :].rearrange("p r d -> p (r d)"), row_block(x1_table, tile)).then_inc(x1_loaded[w], 16)
                    if at(4) is not None:
                        i, w = at(4)[2:]
                        tile = tile_of(at(4))
                        sp.wait_ge(result_ready, tile + 1)
                        if isinstance(tile, int) and tile == NT - 1:
                            sp.dma_start(out[tile * TILE:plan.n, :].rearrange("(p r) d -> p (r d)", r=ROWS),
                                         result[w][0:plan.last_p, :, :].rearrange("p r d -> p (r d)")).then_inc(result_stored[w], 16)
                        else:
                            sp.dma_start(row_block(out, tile), result[w][:, :, :].rearrange("p r d -> p (r d)")).then_inc(result_stored[w], 16)

                over_tiles(sp, plan, 4, step, slots=4)
                for w in four:
                    sp.wait_ge(result_stored[w], 16 * ((NT + 3 - w) // 4))

            @block.gpsimd
            def _(pool):
                def step(at):
                    if at(0) is None:
                        return
                    i, w = at(0)[2:]
                    hold(pool, x1_loaded[w], i * 16 + 16)
                    nc.gpsimd.tensor_tensor(x1[w][:, :, :], x1[w][:, :, :], b_out[:, :].unsqueeze(1).to_broadcast([P, ROWS, D]),
                                            ALU.add).then_inc(x1_biased, 1)

                over_tiles(pool, plan, 0, step, slots=4)

            @block.vector
            def _(dve):
                v = nc.vector

                def step(at):
                    if at(0) is not None:
                        _, u, i, w = at(0)
                        tile = tile_of(at(0))
                        dve.wait_ge(loaded[w], i * 16 + 16)
                        v.tensor_scalar(total[u][:, :, :], acc[w][:, :, WEIGHTS:WIDE], 0.5, None, ALU.max).then_inc(total_ready, 1)
                        dve.wait_ge(total_ready, tile * 2 + 1)
                        v.reciprocal(total[u][:, :, :], total[u][:, :, :]).then_inc(total_ready, 1)
                        dve.wait_ge(total_ready, tile * 2 + 2)
                        wait_past(dve, turned, tile - 1)
                        v.tensor_tensor(mean[u][:, :, :].rearrange("p r (d h) -> p r d h", h=H),
                                        acc[w][:, :, SUMS:WEIGHTS].rearrange("p r (d h) -> p r d h", h=H),
                                        total[u][:, :, :].unsqueeze(2).to_broadcast([P, ROWS, DH, H]),
                                        ALU.mult).then_inc(mean_ready, 1)
                    if at(2) is not None:
                        _, u, i, w = at(2)
                        tile = tile_of(at(2))
                        dve.wait_ge(product_ready, tile + 1)
                        dve.wait_ge(x1_biased, tile + 1)
                        dve.wait_ge(result_stored[w], i * 16)
                        v.tensor_tensor(result[w][:, :, :], out_ps[u][:, :].rearrange("p (r d) -> p r d", r=ROWS), x1[w][:, :, :],
                                        ALU.add).then_inc(result_ready, 1)

                over_tiles(dve, plan, 2, step, slots=4)

            @block.scalar
            def _(act):
                def step(at):
                    i, u = at(0)
                    tile = tile_of(at(0))
                    act.wait_ge(turned, tile + 1)
                    wait_past(act, product_ready, tile - 1)
                    for kc in range(KC):
                        last = nc.scalar.activation(ht[u][:, kc, :], turn_ps[u][:, kc * TILE:(kc + 1) * TILE], ACT.Copy)
                    last.then_inc(ht_ready, 1)

                over_tiles(act, plan, 0, step)

            @block.tensor
            def _(pe):
                def step(at):
                    if at(0) is not None:
                        i, u = at(0)
                        tile = tile_of(at(0))
                        pe.wait_ge(mean_ready, tile + 1)
                        wait_past(pe, ht_ready, tile - 1)
                        for kc in range(KC):
                            for j in range(ROWS):
                                last = nc.tensor.transpose(turn_ps[u][:, kc * TILE + j * P:kc * TILE + (j + 1) * P],
                                                           mean[u][:, j, kc * P:(kc + 1) * P], ident[:, :])
                        last.then_inc(turned, 1)
                    if at(1) is not None:
                        i, u = at(1)
                        tile = tile_of(at(1))
                        pe.wait_ge(ht_ready, tile + 1)
                        wait_past(pe, result_ready, tile - 1)
                        for j in range(ROWS):
                            for kc in range(KC):
                                last = nc.tensor.matmul(out_ps[u][:, j * D:(j + 1) * D], ht[u][:, kc, j * P:(j + 1) * P],
                                                        w_out[:, kc, :], start=kc == 0, stop=kc == KC - 1)
                        last.then_inc(product_ready, 1)

                over_tiles(pe, plan, 1, step)


INPUTS = ["x", "src", "dst"] + ["L0_gnn_" + k for k in ("w1", "b1", "gamma", "beta", "w2", "b2", "w_gcn", "b_gcn")] + \
    ["L1_gnn_" + k for k in ("Wq", "bq", "Wk", "bk", "Wv", "bv", "Wo", "bo")]


def kernel(**inputs):
    import numpy as np
    from concourse import bacc
    from concourse.bass_utils import run_bass_kernel_spmd

    nc = bacc.Bacc("TRN2", target_bir_lowering=False, num_devices=1)
    arrays, args = {}, []
    for name in INPUTS:
        a = np.ascontiguousarray(inputs[name])
        arrays[f"in_{name}"] = a
        args.append(nc.dram_tensor(f"in_{name}", a.shape, mybir.dt.from_np(a.dtype), kind="ExternalInput").ap())
    out = nc.dram_tensor("out", list(arrays["in_x"].shape), F32, kind="ExternalOutput").ap()
    build(nc, *args, out)
    return run_bass_kernel_spmd(nc, [arrays], core_ids=[0]).results[0]["out"]
```
